# Optimizing a Trainium2 kernel written in Bass

```python
import numpy as np
import jax
import jax.numpy as jnp

def _softmax(x, axis=-1):
    return jax.nn.softmax(x, axis=axis)
def _gelu(x):
    return jax.nn.gelu(x, approximate=True)
def _silu(x):
    return jax.nn.silu(x)
def _sigmoid(x):
    return jax.nn.sigmoid(x)
def _layernorm(x, axis=-1, eps=1e-5):
    m = jnp.mean(x, axis=axis, keepdims=True)
    v = jnp.var(x, axis=axis, keepdims=True)
    return (x - m) / jnp.sqrt(v + eps)
def _scatter_add(tgt, idx, src, axis=0):
    return tgt.at[idx].add(src)
def _segment_sum(src, seg, n):
    return jax.ops.segment_sum(src, seg, n)

kernel_name = 'mk_adj_ffn_d1_adj_256_2a23b2'

def setup_inputs(seed: int = 0):
    np.random.seed(seed)
    _w = jnp.asarray
    def _rec_inputs():
        import jax
        import jax.numpy as jnp
        _gk = jax.random.key(seed)
        x = -0.0002928 + 1 * jax.random.normal(jax.random.fold_in(_gk, 1), (16, 1024, 256), jnp.float32)
        _a = jax.random.bernoulli(jax.random.fold_in(_gk, 2), 0.015625, (16, 1024, 1024))
        _a = jnp.logical_or(_a, jnp.eye(1024, dtype=bool))
        adj = _a.astype(jnp.int32)
        return x, adj
    x, adj = _rec_inputs()
    def _L0_gnn_setup():
        import jax, jax.numpy as jnp
        import numpy as np
        B, N, DIN, DOUT, H = (8, 2048, 256, 256, 8)
        HD = DOUT // H
        SCALE = HD ** (-0.5)
        key = jax.random.key(seed)
        ks = jax.random.split(key, 10)
        x = jax.random.normal(ks[0], (B, N, DIN), dtype=jnp.float32)
        adj = jax.random.randint(ks[1], (B, N, N), 0, 2, dtype=jnp.int32)
        eye = jnp.eye(N, dtype=jnp.int32)
        adj = jnp.maximum(adj, eye[None])
        s_in = (2.0 / DIN) ** 0.5
        s_out = (2.0 / DOUT) ** 0.5
        Wq = jax.random.normal(ks[2], (DOUT, DIN), dtype=jnp.float32) * s_in
        Wk = jax.random.normal(ks[3], (DOUT, DIN), dtype=jnp.float32) * s_in
        Wv = jax.random.normal(ks[4], (DOUT, DIN), dtype=jnp.float32) * s_in
        Wo = jax.random.normal(ks[5], (DOUT, DOUT), dtype=jnp.float32) * s_out
        bq = jnp.zeros((DOUT,), jnp.float32)
        bk = jnp.zeros((DOUT,), jnp.float32)
        bv = jnp.zeros((DOUT,), jnp.float32)
        bo = jnp.zeros((DOUT,), jnp.float32)
        return {'x': x, 'adj': adj, 'Wq': Wq, 'bq': bq, 'Wk': Wk, 'bk': bk, 'Wv': Wv, 'bv': bv, 'Wo': Wo, 'bo': bo}
    _L0_gnn_all = _L0_gnn_setup()
    _L0_gnn_in = {k: v for k, v in _L0_gnn_all.items() if k in ('Wq', 'bq', 'Wk', 'bk', 'Wv', 'bv', 'Wo', 'bo', )}
    del _L0_gnn_all

    def _L0_ffn_setup():
        import jax, jax.numpy as jnp
        import numpy as np
        B, N, D = (16, 4096, 256)
        NUM_EXPERTS, TOP_K, HEADS = (4, 2, 4)
        N_EDGES = 1048576
        LN_EPS = 1e-05

        def _layernorm(x, g, b):
            mu = x.mean(-1, keepdims=True)
            var = ((x - mu) ** 2).mean(-1, keepdims=True)
            return (x - mu) * jax.lax.rsqrt(var + LN_EPS) * g + b

        def _forward(x, edge_index, W_gat, att_src, att_dst, b_gat, ln_gamma, ln_beta, W1, b1, W2, b2):
            Bc, Nc, Dc = x.shape
            M = Bc * Nc
            x_flat = x.reshape(M, Dc)
            h = (x_flat @ W_gat).reshape(M, HEADS, NUM_EXPERTS)
            loops = jnp.arange(M, dtype=edge_index.dtype)
            src = jnp.concatenate([edge_index[0], loops])
            dst = jnp.concatenate([edge_index[1], loops])
            a_src = (h * att_src).sum(-1)
            a_dst = (h * att_dst).sum(-1)
            e = jax.nn.leaky_relu(a_src[src] + a_dst[dst], negative_slope=0.2)
            e_max = jax.ops.segment_max(e, dst, num_segments=M)
            ee = jnp.exp(e - e_max[dst])
            denom = jax.ops.segment_sum(ee, dst, num_segments=M)
            alpha = ee / (denom[dst] + 1e-16)
            msg = h[src] * alpha[:, :, None]
            agg = jax.ops.segment_sum(msg, dst, num_segments=M).reshape(M, HEADS * NUM_EXPERTS) + b_gat
            scores = _layernorm(agg, ln_gamma, ln_beta).reshape(M, HEADS, NUM_EXPERTS).mean(1)
            scores = scores.reshape(Bc, Nc, NUM_EXPERTS)
            topk_s, topk_i = jax.lax.top_k(scores, TOP_K)
            w = jax.nn.softmax(topk_s, axis=-1)
            out = jnp.zeros_like(x)
            for ei in range(NUM_EXPERTS):
                g = jnp.where(topk_i == ei, w, 0.0).sum(-1)
                hh = jax.nn.gelu(x @ W1[ei] + b1[ei], approximate=False)
                out = out + g[..., None] * (hh @ W2[ei] + b2[ei])
            return out
        key = jax.random.key(seed)
        ks = jax.random.split(key, 8)
        s = 0.05
        return {'x': jax.random.normal(ks[0], (B, N, D), jnp.float32), 'W_gat': jax.random.normal(ks[1], (D, HEADS * NUM_EXPERTS), jnp.float32) * s, 'att_src': jax.random.normal(ks[2], (HEADS, NUM_EXPERTS), jnp.float32) * s, 'att_dst': jax.random.normal(ks[3], (HEADS, NUM_EXPERTS), jnp.float32) * s, 'b_gat': jnp.zeros((HEADS * NUM_EXPERTS,), jnp.float32), 'ln_gamma': jnp.ones((HEADS * NUM_EXPERTS,), jnp.float32), 'ln_beta': jnp.zeros((HEADS * NUM_EXPERTS,), jnp.float32), 'W1': jax.random.normal(ks[4], (NUM_EXPERTS, D, 2 * D), jnp.float32) * s, 'b1': jnp.zeros((NUM_EXPERTS, 2 * D), jnp.float32), 'W2': jax.random.normal(ks[5], (NUM_EXPERTS, 2 * D, D), jnp.float32) * s, 'b2': jnp.zeros((NUM_EXPERTS, D), jnp.float32), 'edge_index': jax.random.randint(ks[6], (2, N_EDGES), 0, B * N, jnp.int32)}
    _L0_ffn_all = _L0_ffn_setup()
    _L0_ffn_in = {k: v for k, v in _L0_ffn_all.items() if k in ('W_gat', 'att_src', 'att_dst', 'b_gat', 'ln_gamma', 'ln_beta', 'W1', 'b1', 'W2', 'b2', 'edge_index', )}
    del _L0_ffn_all

    return {
        "x": x,
        "adj": adj,
        "L0_gnn_Wq": _L0_gnn_in["Wq"],
        "L0_gnn_bq": _L0_gnn_in["bq"],
        "L0_gnn_Wk": _L0_gnn_in["Wk"],
        "L0_gnn_bk": _L0_gnn_in["bk"],
        "L0_gnn_Wv": _L0_gnn_in["Wv"],
        "L0_gnn_bv": _L0_gnn_in["bv"],
        "L0_gnn_Wo": _L0_gnn_in["Wo"],
        "L0_gnn_bo": _L0_gnn_in["bo"],
        "L0_ffn_W_gat": _L0_ffn_in["W_gat"],
        "L0_ffn_att_src": _L0_ffn_in["att_src"],
        "L0_ffn_att_dst": _L0_ffn_in["att_dst"],
        "L0_ffn_b_gat": _L0_ffn_in["b_gat"],
        "L0_ffn_ln_gamma": _L0_ffn_in["ln_gamma"],
        "L0_ffn_ln_beta": _L0_ffn_in["ln_beta"],
        "L0_ffn_W1": _L0_ffn_in["W1"],
        "L0_ffn_b1": _L0_ffn_in["b1"],
        "L0_ffn_W2": _L0_ffn_in["W2"],
        "L0_ffn_b2": _L0_ffn_in["b2"],
        "L0_ffn_edge_index": _L0_ffn_in["edge_index"],
    }

def reference(x, adj, L0_gnn_Wq, L0_gnn_bq, L0_gnn_Wk, L0_gnn_bk, L0_gnn_Wv, L0_gnn_bv, L0_gnn_Wo, L0_gnn_bo, L0_ffn_W_gat, L0_ffn_att_src, L0_ffn_att_dst, L0_ffn_b_gat, L0_ffn_ln_gamma, L0_ffn_ln_beta, L0_ffn_W1, L0_ffn_b1, L0_ffn_W2, L0_ffn_b2, L0_ffn_edge_index):
    import jax
    import jax.numpy as jnp
    def _L0_gnn_ref(x, adj, Wq, bq, Wk, bk, Wv, bv, Wo, bo):
        import jax, jax.numpy as jnp
        import numpy as np
        B, N, DIN, DOUT, H = (8, 2048, 256, 256, 8)
        HD = DOUT // H
        SCALE = HD ** (-0.5)
        b, n, _ = x.shape

        def proj(W, bias):
            y = jnp.einsum('bnf,of->bno', x, W) + bias
            return y.reshape(b, n, H, HD).transpose(0, 2, 1, 3)
        Q, K, V = (proj(Wq, bq), proj(Wk, bk), proj(Wv, bv))
        scores = jnp.einsum('bhnd,bhmd->bhnm', Q, K) * SCALE
        mask = adj[:, None, :, :] == 0
        scores = jnp.where(mask, -jnp.inf, scores)
        attn = jax.nn.softmax(scores, axis=-1)
        attn = jnp.nan_to_num(attn, nan=0.0)
        out = jnp.einsum('bhnm,bhmd->bhnd', attn, V)
        out = out.transpose(0, 2, 1, 3).reshape(b, n, DOUT)
        return jnp.einsum('bno,po->bnp', out, Wo) + bo

    def _L0_ffn_ref(x, W_gat, att_src, att_dst, b_gat, ln_gamma, ln_beta, W1, b1, W2, b2, edge_index):
        import jax, jax.numpy as jnp
        import numpy as np
        B, N, D = (16, 4096, 256)
        NUM_EXPERTS, TOP_K, HEADS = (4, 2, 4)
        N_EDGES = 1048576
        LN_EPS = 1e-05

        def _layernorm(x, g, b):
            mu = x.mean(-1, keepdims=True)
            var = ((x - mu) ** 2).mean(-1, keepdims=True)
            return (x - mu) * jax.lax.rsqrt(var + LN_EPS) * g + b

        def _forward(x, edge_index, W_gat, att_src, att_dst, b_gat, ln_gamma, ln_beta, W1, b1, W2, b2):
            Bc, Nc, Dc = x.shape
            M = Bc * Nc
            x_flat = x.reshape(M, Dc)
            h = (x_flat @ W_gat).reshape(M, HEADS, NUM_EXPERTS)
            loops = jnp.arange(M, dtype=edge_index.dtype)
            src = jnp.concatenate([edge_index[0], loops])
            dst = jnp.concatenate([edge_index[1], loops])
            a_src = (h * att_src).sum(-1)
            a_dst = (h * att_dst).sum(-1)
            e = jax.nn.leaky_relu(a_src[src] + a_dst[dst], negative_slope=0.2)
            e_max = jax.ops.segment_max(e, dst, num_segments=M)
            ee = jnp.exp(e - e_max[dst])
            denom = jax.ops.segment_sum(ee, dst, num_segments=M)
            alpha = ee / (denom[dst] + 1e-16)
            msg = h[src] * alpha[:, :, None]
            agg = jax.ops.segment_sum(msg, dst, num_segments=M).reshape(M, HEADS * NUM_EXPERTS) + b_gat
            scores = _layernorm(agg, ln_gamma, ln_beta).reshape(M, HEADS, NUM_EXPERTS).mean(1)
            scores = scores.reshape(Bc, Nc, NUM_EXPERTS)
            topk_s, topk_i = jax.lax.top_k(scores, TOP_K)
            w = jax.nn.softmax(topk_s, axis=-1)
            out = jnp.zeros_like(x)
            for ei in range(NUM_EXPERTS):
                g = jnp.where(topk_i == ei, w, 0.0).sum(-1)
                hh = jax.nn.gelu(x @ W1[ei] + b1[ei], approximate=False)
                out = out + g[..., None] * (hh @ W2[ei] + b2[ei])
            return out
        return _forward(x, edge_index, W_gat, att_src, att_dst, b_gat, ln_gamma, ln_beta, W1, b1, W2, b2)

    x = x + _L0_gnn_ref(_layernorm(x, axis=-1), adj, L0_gnn_Wq, L0_gnn_bq, L0_gnn_Wk, L0_gnn_bk, L0_gnn_Wv, L0_gnn_bv, L0_gnn_Wo, L0_gnn_bo)
    x = x + _L0_ffn_ref(_layernorm(x, axis=-1), L0_ffn_W_gat, L0_ffn_att_src, L0_ffn_att_dst, L0_ffn_b_gat, L0_ffn_ln_gamma, L0_ffn_ln_beta, L0_ffn_W1, L0_ffn_b1, L0_ffn_W2, L0_ffn_b2, L0_ffn_edge_index)
    return x


_drawn_inputs = setup_inputs


def setup_inputs(seed=0):
    import zlib

    import numpy as np

    out = dict(_drawn_inputs(seed))
    spreads = {'L0_gnn_bq': (0.0, 0.1),
     'L0_gnn_bk': (0.0, 0.8),
     'L0_gnn_bv': (0.0, 0.1),
     'L0_gnn_bo': (0.0, 0.1),
     'L0_ffn_b_gat': (0.0, 0.1),
     'L0_ffn_ln_gamma': (1.0, 0.2),
     'L0_ffn_ln_beta': (0.0, 0.328),
     'L0_ffn_b1': (0.0, 0.1),
     'L0_ffn_b2': (0.0, 0.1)}
    factors = {'L0_ffn_att_src': 4.508, 'L0_ffn_att_dst': 7.504}
    for name, (base, spread) in spreads.items():
        noise = np.random.default_rng([zlib.crc32(name.encode()), seed]).standard_normal(out[name].shape)
        drawn = base * np.exp(spread * noise) if base else spread * noise
        out[name] = jnp.asarray(drawn.astype(out[name].dtype))
    for name, factor in factors.items():
        out[name] = (out[name] * factor).astype(out[name].dtype)
    return out
```

```python
from contextlib import ExitStack

import concourse.bass as bass
from concourse import mybir

P = 128
H, HD = 8, 32
SCALE = HD ** -0.5
LN_EPS = 1e-5
GC = 16
ROW = 32
MASKED = -1.0e30
LEAK = 0.2
NO_KEY = -1.0e29

ALU = mybir.AluOpType
ACT = mybir.ActivationFunctionType
F32, BF16, I32 = mybir.dt.float32, mybir.dt.bfloat16, mybir.dt.int32
AX_X = mybir.AxisListType.X
N, D = 1024, 256
TN = N // P


class Arrays:
    pass


class Chain:

    def __init__(self, engine, sem):
        self.engine, self.sem, self.count = engine, sem, 0

    def __call__(self, ins):
        self.count += 1
        ins.then_inc(self.sem, 1)
        self.engine.wait_ge(self.sem, self.count)

    def restart(self):
        self.engine.sem_clear(self.sem)
        self.count = 0

    def loop(self, times, body):
        with self.engine.Fori(0, times) as i:
            self.restart()
            body(i)
        self.restart()


def attention_phase(nc, d, B):
    with ExitStack() as ctx:
        def sb(name, shape, dt=F32):
            return ctx.enter_context(nc.sbuf_tensor(name, shape, dt))

        def sem(name):
            return ctx.enter_context(nc.semaphore(name))

        wq, wk, wv, wo = (sb(n, [P, 2, D]) for n in ("wq", "wk", "wv", "wo"))
        wgat = sb("wgat", [P, 2, GC])
        bqk = sb("bqk", [P, 2, 2])
        bv, bo = sb("bv", [P, D]), sb("bo", [P, D])
        att = sb("att", [P, 2, GC])
        ident = sb("ident", [P, P])
        ident16 = sb("ident16", [P, P], BF16)
        ones32 = sb("ones32", [P, 32])
        eps = sb("eps", [P, 1])
        xb = sb("xb", [P, TN, D])
        xn = sb("xn", [P, TN, D])
        xnT = sb("xnT", [P, 2, N])
        stats = sb("stats", [P, TN, 6])
        mv = sb("mv", [P, TN, 2])
        rstd = sb("rstd", [P, TN])
        qf = sb("qf", [P, 2, N])
        kf = sb("kf", [P, 2, N])
        x1 = qf[:, :, :].rearrange("p g (t d) -> p (g t) d", d=D)
        qp = sb("qp", [P, 3, 2, N], BF16)
        kp = sb("kp", [P, 3, 2, N], BF16)
        q1s, k1s = sb("q1s", [P, H, N], BF16), sb("k1s", [P, H, N], BF16)
        q2s, k2s = sb("q2s", [96, H, N], BF16), sb("k2s", [96, H, N], BF16)
        vt = sb("vt", [P, TN, D])
        adjb = sb("adjb", [P, 2, N], I32)
        mb = sb("mb", [P, TN, N], BF16)
        mT = sb("mT", [P, TN, N], BF16)
        junk = sb("junk", [P, 4, 512], BF16)
        mx = sb("mx", [P, 2, TN, 2])
        m3 = sb("m3", [P, 2, TN, 96], BF16)
        mneg = sb("mneg", [P, TN])
        mrem = sb("mrem", [P, TN])
        pt = sb("pt", [P, 2, N])
        den = sb("den", [32, 2, 512])
        oT = xnT
        tab = sb("tab", [P, TN, ROW])
        tmp16 = kf[:, 0, 0:TN * GC].rearrange("p (t n) -> p t n", t=TN)
        ps = ctx.enter_context(nc.psum_tensor("ps", [P, 8, 512], F32))
        A0 = 6
        O0 = 4

        s_w, s_setup, s_ready = sem("s_w"), sem("s_setup"), sem("s_ready")
        s_arrived, s_clearing, s_go, s_left = sem("s_arrived"), sem("s_clearing"), sem("s_go"), sem("s_left")
        first_sem = sem("s_first")
        s_x, s_rstd, s_xn, s_tr, s_xnT, s_q, s_k, s_v = (sem("s_" + n) for n in ("x", "rstd", "xn", "tr", "xnT", "q", "k", "v"))
        s_adj = [sem("s_adj0"), sem("s_adj1")]
        s_mb, s_mtp = sem("s_mb"), sem("s_mtp")
        s_mT = [sem("s_mT0"), sem("s_mT1")]
        s_qf, s_kf, s_vt, s_qp, s_kp = sem("s_qf"), sem("s_kf"), sem("s_vt"), sem("s_qp"), sem("s_kp")
        s_qst = [sem(f"s_qst{n}") for n in range(4)]
        s_kst = [sem(f"s_kst{n}") for n in range(4)]
        s_sc, s_mx, s_m3, s_nmp, s_nm = sem("s_sc"), sem("s_mx"), sem("s_m3"), sem("s_nmp"), sem("s_nm")
        s_st, s_exp, s_pv, s_o, s_dve = sem("s_st"), sem("s_exp"), sem("s_pv"), sem("s_o"), sem("s_dve")
        s_wo, s_x1, s_mv, s_xn2, s_tr2, s_xn2T, s_h, s_tab, s_out = (
            sem("s_" + n) for n in ("wo", "x1", "mv", "xn2", "tr2", "xn2T", "h", "tab", "out"))
        s_xbo = sem("s_xbo")
        last_sem = sem("s_last")
        assert last_sem.num - first_sem.num < 60
        block = ctx.enter_context(nc.Block())

        ORDER = [0, 4, 1, 5, 2, 6, 3, 7]

        def next_batch(engine, i):
            engine.sem_inc(s_arrived, 1)
            engine.wait_ge(s_go, i + 1)
            engine.sem_inc(s_left, 1)

        @block.sync
        def _(sp):
            for dst, src in ((wq, d.wqT), (wk, d.wkT), (wv, d.wvT), (wo, d.woT)):
                sp.dma_start(dst[:, :, :], src.rearrange("(c p) n -> p c n", p=P)).then_inc(s_w, 16)
            sp.dma_start(wgat[:, :, :], d.wgat.rearrange("(c p) n -> p c n", p=P)).then_inc(s_w, 16)
            sp.dma_start(bv[:, :], d.bv.rearrange("(a n) -> a n", a=1).to_broadcast([P, D])).then_inc(s_w, 16)
            sp.dma_start(bo[:, :], d.bo.rearrange("(a n) -> a n", a=1).to_broadcast([P, D])).then_inc(s_w, 16)
            for n, b in enumerate((d.bq, d.bk)):
                for c in range(2):
                    sp.dma_start(bqk[:, n, c:c + 1], b[c * P:(c + 1) * P].rearrange("(p a) -> p a", a=1)).then_inc(s_w, 16)
            for n, a in enumerate((d.att_src, d.att_dst)):
                sp.dma_start(att[:, n, :], a.rearrange("h e -> (h e)").rearrange("(a n) -> a n", a=1)
                             .to_broadcast([P, GC])).then_inc(s_w, 16)
            with sp.Fori(0, B) as i:
                sp.dma_start(xb[:, :, :], d.x[bass.ds(i, 1), :, :].rearrange("a (t p) n -> p (a t) n", p=P)).then_inc(s_x, 16)
                for t in range(TN):
                    if t >= 2:
                        sp.wait_ge(s_mb, t - 1)
                    sp.dma_start(adjb[:, t % 2, :], d.adj[bass.ds(i, 1), t * P:(t + 1) * P, :].rearrange("a p n -> p (a n)"))\
                        .then_inc(s_adj[t % 2], 16)
                sp.wait_ge(s_qp, 3)
                for a in range(4):
                    rows = slice(32 * a, 32 * a + 32)
                    for dst, r, part in ((q1s, 0, 0), (q1s, 1, 0), (q1s, 2, 1), (q1s, 3, 1), (q2s, 0, 0), (q2s, 1, 2)):
                        sp.dma_start(dst[32 * r:32 * r + 32, :, :].rearrange("p (g a) n -> p a g n", a=4)[:, a, :, :],
                                     qp[rows, part, :, :]).then_inc(s_qst[a], 16)
                sp.wait_ge(s_x1, TN)
                sp.dma_start(d.x1[bass.ds(i, 1), :, :].rearrange("a (t p) n -> p (a t) n", p=P), x1[:, :, :]).then_inc(s_out, 16)
                sp.wait_ge(s_xn2T, 2)
                sp.dma_start(d.xnT[bass.ds(i, 1), :, :, :].rearrange("a p c n -> p (a c) n"), xnT[:, :, :]).then_inc(s_out, 16)
                sp.wait_ge(s_tab, 1)
                sp.dma_start(d.tab[bass.ds(i, 1), :, :].rearrange("a (t p) n -> p (a t) n", p=P), tab[:, :, :]).then_inc(s_out, 16)
                sp.wait_ge(s_out, 48)
                sp.wait_ge(s_arrived, i * 4 + 4)
                sp.sem_inc(s_clearing, 1)
                sp.sem_clear(range(first_sem.num, last_sem.num + 1))
                sp.sem_inc(s_go, 1)

        @block.gpsimd
        def _(pool):
            def setup(n, ins):
                ins.then_inc(s_setup, 1)
                pool.wait_ge(s_setup, n)

            setup(1, pool.memset(ident[:, :], 0.0))
            setup(2, pool.memset(m3[:, :, :, :], 0.0))
            setup(3, pool.affine_select(out=ident[:, :], in_=ident[:, :], compare_op=ALU.not_equal, fill=1.0, base=0,
                                        pattern=[[-1, P]], channel_multiplier=1))
            setup(4, pool.memset(ones32[:, :], 1.0))
            setup(5, pool.memset(k2s[64:96, :, :], 1.0))
            setup(6, pool.memset(eps[:, :], LN_EPS))
            setup(7, pool.tensor_copy(ident16[:, :], ident[:, :]))
            pool.memset(tab[:, :, :], 0.0).then_inc(s_ready, 1)
            with pool.Fori(0, B) as i:
                for t in range(TN):
                    pool.wait_ge(s_adj[t % 2], 16 * (t // 2) + 16)
                    pool.tensor_scalar(mb[:, t, :], adjb[:, t % 2, :], 0, MASKED, ALU.is_equal, ALU.mult).then_inc(s_mb, 1)
                pool.wait_ge(s_kf, 2)
                pool.tensor_copy(kp[:, 0, :, :], kf[:, :, :]).then_inc(s_kp, 1)
                pool.wait_ge(s_kp, 1)
                pool.tensor_tensor(kf[:, :, :], kf[:, :, :], kp[:, 0, :, :], ALU.subtract).then_inc(s_kp, 1)
                pool.wait_ge(s_kp, 2)
                pool.tensor_copy(kp[:, 1, :, :], kf[:, :, :]).then_inc(s_kp, 1)
                pool.wait_ge(s_kp, 3)
                pool.tensor_tensor(kp[:, 2, :, :], kf[:, :, :], kp[:, 1, :, :], ALU.subtract).then_inc(s_kp, 2)
                pool.wait_ge(s_xn, TN)
                pool.tensor_tensor(xb[:, :, :], xb[:, :, :], bo[:, None, :].to_broadcast([P, TN, D]), ALU.add).then_inc(s_xbo, 1)
                pool.wait_ge(s_xbo, 1)
                next_batch(pool, i)

        @block.scalar
        def _(act):
            act.wait_ge(s_ready, 1)
            act.wait_ge(s_w, 16 * 13)
            with act.Fori(0, B) as i:
                act.wait_ge(s_mv, 1)
                act.activation(rstd[:, :], mv[:, :, 1], ACT.Sqrt, bias=eps[:, 0:1]).then_inc(s_rstd, 1)
                act.wait_ge(s_tr, TN)
                act.activation(xnT[:, 0, :].rearrange("p (b n) -> p b n", b=2), ps[:, 0:2, :], ACT.Copy).then_inc(s_xnT, 1)
                for g in range(2):
                    act.wait_ge(s_q, g + 1)
                    act.activation(qf[:, g, :].rearrange("p (b n) -> p b n", b=2), ps[:, 4 + 2 * g:6 + 2 * g, :],
                                   ACT.Identity, bias=bqk[:, 0, g:g + 1]).then_inc(s_qf, 1)
                for g in range(2):
                    act.wait_ge(s_k, g + 1)
                    act.activation(kf[:, g, :].rearrange("p (b n) -> p b n", b=2), ps[:, 2 * g:2 * g + 2, :],
                                   ACT.Identity, bias=bqk[:, 1, g:g + 1]).then_inc(s_kf, 1)
                for c in range(0, TN, 2):
                    act.wait_ge(s_mtp, c + 1)
                    act.activation(mT[:, c, :], ps[:, c % 2, :].bitcast(BF16), ACT.Copy).then_inc(s_mT[0], 1)
                act.wait_ge(s_kp, 5)
                for a in range(4):
                    rows = slice(32 * a, 32 * a + 32)
                    for dst, r, part in ((k1s, 0, 0), (k1s, 1, 1), (k1s, 2, 0), (k1s, 3, 1), (k2s, 0, 2), (k2s, 1, 0)):
                        act.dma_start(dst[32 * r:32 * r + 32, :, :].rearrange("p (g a) n -> p a g n", a=4)[:, a, :, :],
                                      kp[rows, part, :, :]).then_inc(s_kst[a], 16)
                for j in range(H):
                    act.wait_ge(s_nmp, j + 1)
                    act.activation(q2s[64:96, ORDER[j], :], ps[64:96, A0, :].bitcast(BF16), ACT.Copy).then_inc(s_nm, 1)
                    for c in range(TN):
                        n = j * TN + c
                        act.wait_ge(s_st, n + 1)
                        if n >= 2:
                            act.wait_ge(s_pv, n - 1)
                        act.activation(pt[:, n % 2, :].rearrange("p (b n) -> p b n", b=2),
                                       ps[:, 2 * (n % 2):2 * (n % 2) + 2, :], ACT.Exp).then_inc(s_exp, 1)
                act.wait_ge(s_mv, 2)
                act.activation(rstd[:, :], mv[:, :, 1], ACT.Sqrt, bias=eps[:, 0:1]).then_inc(s_rstd, 1)
                act.wait_ge(s_tr2, TN)
                act.activation(xnT[:, 0, :].rearrange("p (b n) -> p b n", b=2), ps[:, 4:6, :], ACT.Copy).then_inc(s_xn2T, 1)
                next_batch(act, i)

        @block.vector
        def _(dve):
            dve.wait_ge(s_ready, 1)
            dve.wait_ge(s_w, 16 * 13)
            link = Chain(dve, s_dve)

            def layernorm(src, scale_at):
                for t in range(TN):
                    last = dve.bn_stats(stats[:, t, :], src[:, t, :])
                link(last)
                for t in range(TN):
                    last = dve.bn_aggr(mv[:, t, :], stats[:, t, :])
                last.then_inc(s_mv, 1)
                dve.wait_ge(s_rstd, scale_at)
                link(dve.reciprocal(rstd[:, :], rstd[:, :]))

            with dve.Fori(0, B) as i:
                link.count = 0
                dve.wait_ge(s_x, 16)
                layernorm(xb, 1)
                for t in range(TN):
                    dve.tensor_scalar(xn[:, t, :], xb[:, t, :], mv[:, t, 0:1], rstd[:, t:t + 1], ALU.subtract, ALU.mult)\
                        .then_inc(s_xn, 1)
                dve.wait_ge(s_tr, TN)
                dve.tensor_copy(xnT[:, 1, :].rearrange("p (b n) -> p b n", b=2), ps[:, 2:4, :]).then_inc(s_xnT, 1)
                dve.wait_ge(s_qf, 2)
                link(dve.tensor_scalar(qf[:, :, :], qf[:, :, :], SCALE, None, ALU.mult))
                link(dve.tensor_copy(qp[:, 0, :, :], qf[:, :, :]))
                link(dve.tensor_tensor(qf[:, :, :], qf[:, :, :], qp[:, 0, :, :], ALU.subtract))
                link(dve.tensor_copy(qp[:, 1, :, :], qf[:, :, :]))
                dve.tensor_tensor(qp[:, 2, :, :], qf[:, :, :], qp[:, 1, :, :], ALU.subtract).then_inc(s_qp, 3)
                dve.wait_ge(s_v, 1)
                dve.tensor_tensor(vt[:, :, :], ps[:, 4:8, :].rearrange("p b (c n) -> p (b c) n", c=2),
                                  bv[:, None, :].to_broadcast([P, TN, D]), ALU.add).then_inc(s_vt, 1)
                for c in range(1, TN, 2):
                    dve.wait_ge(s_mtp, c + 1)
                    dve.tensor_copy(mT[:, c, :], ps[:, c % 2, :].bitcast(BF16)).then_inc(s_mT[1], 1)

                def maxima(j):
                    for n in range(2 * TN):
                        t, mh = n // 2, n % 2
                        if n >= 4:
                            dve.wait_ge(s_mx, j * 2 * TN + n - 3)
                        dve.wait_ge(s_sc, j * 2 * TN + n + 1)
                        last = dve.tensor_tensor_reduce(out=junk[:, n % 4, :], in0=ps[:, A0 + n % 2, :], in1=mb[:, t, mh * 512:mh * 512 + 512],
                                                        scale=1.0, scalar=-3.0e38, op0=ALU.add, op1=ALU.max,
                                                        accum_out=mx[:, j % 2, t, mh:mh + 1])
                        last.then_inc(s_mx, 1)
                    dve.wait_ge(s_mx, (j + 1) * 2 * TN)
                    link(dve.tensor_tensor(mneg[:, :], mx[:, j % 2, :, 0], mx[:, j % 2, :, 1], ALU.max))
                    link(dve.tensor_scalar(mneg[:, :], mneg[:, :], NO_KEY, -1.0, ALU.max, ALU.mult))
                    part = [m3[:, j % 2, :, 64 + n] for n in range(3)]
                    link(dve.tensor_copy(part[0], mneg[:, :]))
                    link(dve.tensor_tensor(mrem[:, :], mneg[:, :], part[0], ALU.subtract))
                    link(dve.tensor_copy(part[1], mrem[:, :]))
                    dve.tensor_tensor(part[2], mrem[:, :], part[1], ALU.subtract).then_inc(s_m3, 1)

                def normalise(j):
                    g, a = ORDER[j] // 4, ORDER[j] % 4
                    dve.wait_ge(s_pv, (j + 1) * TN)
                    if j == H - 1:
                        dve.wait_ge(s_o, j)
                    for nh in range(2):
                        last = dve.reciprocal(den[:, nh, :], ps[64 * nh + 32:64 * nh + 64, O0 + j % 2, :])
                    link(last)
                    for nh in range(2):
                        last = dve.scalar_tensor_tensor(out=oT[32 * a:32 * a + 32, g, nh * 512:nh * 512 + 512],
                                                        in0=den[:, nh, :], scalar=1.0e30,
                                                        in1=ps[64 * nh:64 * nh + 32, O0 + j % 2, :], op0=ALU.min, op1=ALU.mult)
                    last.then_inc(s_o, 1)

                maxima(0)
                for j in range(H):
                    if j + 1 < H:
                        maxima(j + 1)
                    normalise(j)
                dve.wait_ge(s_xbo, 1)
                for t in range(0, TN, 2):
                    dve.wait_ge(s_wo, t + 2)
                    dve.tensor_tensor(x1[:, t:t + 2, :], ps[:, t // 2, :].rearrange("p (a n) -> p a n", a=2), xb[:, t:t + 2, :],
                                      ALU.add).then_inc(s_x1, 2)
                dve.wait_ge(s_x1, TN)
                layernorm(x1, 2)
                for t in range(TN):
                    dve.tensor_scalar(xn[:, t, :], x1[:, t, :], mv[:, t, 0:1], rstd[:, t:t + 1], ALU.subtract, ALU.mult)\
                        .then_inc(s_xn2, 1)
                dve.wait_ge(s_tr2, TN)
                dve.tensor_copy(xnT[:, 1, :].rearrange("p (b n) -> p b n", b=2), ps[:, 6:8, :]).then_inc(s_xn2T, 1)
                dve.wait_ge(s_h, 1)
                link(dve.tensor_copy(tab[:, :, 0:GC], ps[:, 0, 0:TN * GC].rearrange("p (t n) -> p t n", t=TN)))
                for n in range(2):
                    link(dve.tensor_tensor(tmp16[:, :, :], tab[:, :, 0:GC], att[:, n, None, :].to_broadcast([P, TN, GC]), ALU.mult))
                    link(dve.tensor_reduce(tab[:, :, GC + 4 * n:GC + 4 * n + 4], tmp16[:, :, :].rearrange("p t (h e) -> p t h e", h=4),
                                              AX_X, ALU.add))
                dve.sem_inc(s_tab, 1)
                next_batch(dve, i)

        @block.tensor
        def _(pe):
            pe.wait_ge(s_ready, 1)
            pe.wait_ge(s_w, 16 * 13)
            with pe.Fori(0, B) as i:
                for t in range(TN):
                    pe.wait_ge(s_xn, t + 1)
                    for c in range(2):
                        last = pe.transpose(ps[:, 2 * c + t // 4, (t % 4) * P:(t % 4 + 1) * P], xn[:, t, c * P:(c + 1) * P], ident[:, :])
                    last.then_inc(s_tr, 1)
                pe.wait_ge(s_xnT, 2)

                def project(w, g, bank):
                    for nh in range(2):
                        for c in range(2):
                            last = pe.matmul(ps[:, bank + nh, :], w[:, c, g * P:(g + 1) * P], xnT[:, c, nh * 512:nh * 512 + 512],
                                             start=c == 0, stop=c == 1)
                    return last

                for g in range(2):
                    project(wq, g, 4 + 2 * g).then_inc(s_q, 1)
                for g in range(2):
                    project(wk, g, 2 * g).then_inc(s_k, 1)
                pe.wait_ge(s_qf, 2)
                for t in range(TN):
                    for c in range(2):
                        last = pe.matmul(ps[:, 4 + t // 2, (t % 2) * D:(t % 2 + 1) * D], xnT[:, c, t * P:(t + 1) * P], wv[:, c, :],
                                         start=c == 0, stop=c == 1)
                last.then_inc(s_v, 1)
                pe.wait_ge(s_mb, TN)
                pe.wait_ge(s_kf, 2)
                for c in range(TN):
                    if c >= 2:
                        pe.wait_ge(s_mT[c % 2], c // 2)
                    for t in range(TN):
                        last = pe.transpose(ps[:, c % 2, :].bitcast(BF16)[:, t * P:(t + 1) * P], mb[:, t, c * P:(c + 1) * P], ident16[:, :])
                    last.then_inc(s_mtp, 1)
                pe.wait_ge(s_vt, 1)

                def score_half(j, n):
                    h, t, mh = ORDER[j], n // 2, n % 2
                    if n == 0:
                        pe.wait_ge(s_qst[h % 4], 96)
                        pe.wait_ge(s_kst[h % 4], 96)
                        if j >= 1:
                            pe.wait_ge(s_nm, j)
                    if n >= 2:
                        pe.wait_ge(s_mx, j * 2 * TN + n - 1)
                    elif n == 1 and j >= 1:
                        pe.wait_ge(s_mx, j * 2 * TN)
                    pe.matmul(ps[:, A0 + n % 2, :], q1s[:, h, t * P:(t + 1) * P], k1s[:, h, mh * 512:mh * 512 + 512],
                              start=True, stop=True).then_inc(s_sc, 1)

                def maxima_rows(j):
                    pe.wait_ge(s_m3, j + 1)
                    for t in range(TN):
                        last = pe.transpose(ps[0:96, A0, :].bitcast(BF16)[:, t * P:(t + 1) * P], m3[:, j % 2, t, :], ident16[:, :])
                    last.then_inc(s_nmp, 1)

                def shifted_scores(j, c):
                    h, n = ORDER[j], j * TN + c
                    if n >= 2:
                        pe.wait_ge(s_exp, n - 1)
                    else:
                        pe.wait_ge(s_mT[0], 4)
                        pe.wait_ge(s_mT[1], 4)
                    if c == 0:
                        pe.wait_ge(s_nm, j + 1)
                    for lhs, rhs in ((k1s, q1s), (k2s, q2s)):
                        for nh in range(2):
                            pe.matmul(ps[:, 2 * (n % 2) + nh, :], lhs[:, h, c * P:(c + 1) * P], rhs[:, h, nh * 512:nh * 512 + 512],
                                      start=lhs is k1s, stop=False)
                    for nh in range(2):
                        last = pe.matmul(ps[:, 2 * (n % 2) + nh, :], ident16[:, :], mT[:, c, nh * 512:nh * 512 + 512],
                                         start=False, stop=True)
                    last.then_inc(s_st, 1)

                def weighted_values(j, c):
                    h, n = ORDER[j], j * TN + c
                    if c == 0 and j >= 2:
                        pe.wait_ge(s_o, j - 1)
                    pe.wait_ge(s_exp, n + 1)
                    for nh in range(2):
                        for r, lhs in enumerate((vt[:, c, 32 * h:32 * h + 32], ones32[:, :])):
                            at = 64 * nh + 32 * r
                            last = pe.matmul(ps[at:at + 32, O0 + j % 2, :], lhs, pt[:, n % 2, nh * 512:nh * 512 + 512],
                                             start=c == 0, stop=c == TN - 1, tile_position=(0, at))
                    last.then_inc(s_pv, 1)

                for n in range(2 * TN):
                    score_half(0, n)
                maxima_rows(0)
                for j in range(H):
                    for c in range(TN):
                        shifted_scores(j, c)
                        if j + 1 < H:
                            score_half(j + 1, 2 * c)
                            score_half(j + 1, 2 * c + 1)
                        if j or c:
                            weighted_values(*divmod(j * TN + c - 1, TN))
                    if j + 1 < H:
                        maxima_rows(j + 1)
                weighted_values(H - 1, TN - 1)
                pe.wait_ge(s_exp, H * TN)
                pe.wait_ge(s_o, H)
                for t in range(TN):
                    for g in range(2):
                        last = pe.matmul(ps[:, t // 2, (t % 2) * D:(t % 2 + 1) * D], oT[:, g, t * P:(t + 1) * P], wo[:, g, :],
                                         start=g == 0, stop=g == 1)
                    last.then_inc(s_wo, 1)
                for t in range(TN):
                    pe.wait_ge(s_xn2, t + 1)
                    for c in range(2):
                        last = pe.transpose(ps[:, 4 + 2 * c + t // 4, (t % 4) * P:(t % 4 + 1) * P], xn[:, t, c * P:(c + 1) * P], ident[:, :])
                    last.then_inc(s_tr2, 1)
                pe.wait_ge(s_xn2T, 2)
                pe.wait_ge(s_x1, TN)
                for t in range(TN):
                    for c in range(2):
                        last = pe.matmul(ps[:, 0, t * GC:(t + 1) * GC], xnT[:, c, t * P:(t + 1) * P], wgat[:, c, :],
                                         start=c == 0, stop=c == 1)
                last.then_inc(s_h, 1)
                next_batch(pe, i)


M = 16 * N
E = 1048576
EC = E // P
LAST = M - 1
KEY_BIT = 0x40000000
SEG, SEG_CAP = 512, 72
NSEG = EC // SEG
ROW_CAP = 640
CELL = 20
CELLS = P * CELL
BSEG, BSEG_CAP = 512, 152
NBSEG = CELLS // BSEG
SLOTS = 768
KT = SLOTS // P
FAR = 4194304.0
HC = 32


def edge_phase(nc, d):
    with ExitStack() as ctx:
        def sb(name, shape, dt=F32):
            return ctx.enter_context(nc.sbuf_tensor(name, shape, dt))

        def sem(name):
            return ctx.enter_context(nc.semaphore(name))

        CH = 1024
        NCH = EC // CH
        src, dst = sb("e_src", [P, CH], I32), sb("e_dst", [P, CH], I32)
        t0 = sb("e_t0", [P, CH], I32)
        keys = sb("e_keys", [P, EC])
        lo, hi = sb("e_lo", [P, EC], BF16), sb("e_hi", [P, EC], BF16)
        iota = sb("e_iota", [P, P])
        iota16 = sb("e_iota16", [P, P], BF16)
        ohl, ohh = sb("e_ohl", [P, 2, HC, P], BF16), sb("e_ohh", [P, 2, HC, P], BF16)
        cnt = sb("e_cnt", [P, P])
        work = sb("e_work", [P, SEG])
        found = sb("e_found", [P, SEG_CAP])
        found2 = sb("e_found2", [P, BSEG_CAP])
        first = sb("e_first", [P, NSEG * SEG_CAP])
        row = sb("e_row", [P, ROW_CAP])
        top = sb("e_top", [P, 64])
        bucket = sb("e_bucket", [P, ROW_CAP + 1])
        same, rank, pos = sb("e_same", [P, ROW_CAP]), sb("e_rank", [P, ROW_CAP]), sb("e_pos", [P, ROW_CAP])
        bi = sb("e_bi", [P, ROW_CAP], I32)
        posi = sb("e_posi", [P, ROW_CAP], I32)
        pcol = sb("e_pcol", [P, 1])
        zero = sb("e_zero", [P, CELLS])
        cells = sb("e_cells", [P, CELLS])
        left = sb("e_left", [P, 8])
        over = sb("e_over", [P, 1])
        sidx, skey = sb("e_sidx", [P, 16], I32), sb("e_skey", [P, 16])
        merged = sb("e_merged", [P, NBSEG * BSEG_CAP + P])
        heads = sb("e_heads", [P, P], I32)
        slots = sb("e_slots", [P, SLOTS])
        psum = ctx.enter_context(nc.psum_tensor("e_ps", [P, 2, 512], F32))

        s_src, s_dst, s_key, s_c = sem("e_s_src"), sem("e_s_dst"), sem("e_s_key"), sem("e_s_c")
        s_setup, s_ohl, s_ohh, s_cnt, s_added = (sem("e_s_" + n) for n in ("setup", "ohl", "ohh", "cnt", "added"))
        s_v, s_zero, s_row, s_stage, s_scat, s_cells, s_done, s_out, s_fl, s_fill = (
            sem("e_s_" + n) for n in ("v", "zero", "row", "stage", "scat", "cells", "done", "out", "fl", "fill"))
        dummy = sb("e_dummy", [P, 3])
        block = ctx.enter_context(nc.Block())
        cells_d = d.cells.rearrange("(b c) a -> b (c a)", b=P)

        @block.sync
        def _(sp):
            sp.wait_ge(s_zero, 1)
            sp.dma_start(cells_d, zero[:, :]).then_inc(s_cells, 16)
            with sp.Fori(0, NCH) as i:
                sp.wait_ge(s_key, i * 1 + 1)
                sp.dma_start(src[:, :], d.edges[0, :].rearrange("(p c) -> p c", p=P)[:, bass.ts(i, CH)]).then_inc(s_src, 16)
                sp.dma_start(dst[:, :], d.edges[1, :].rearrange("(p c) -> p c", p=P)[:, bass.ts(i, CH)]).then_inc(s_dst, 16)
            sp.wait_ge(s_added, EC // HC + 2)
            sp.dma_start(d.cnt, cnt[:, :]).then_inc(s_out, 16)
            sp.wait_ge(s_scat, 16 * ROW_CAP)
            sp.dma_start(cells[:, :], cells_d).then_inc(s_fill, 16)
            sp.wait_ge(s_done, 1)
            sp.dma_start(d.slots, slots[:, :]).then_inc(s_out, 16)
            sp.dma_start(d.over, over[:, :]).then_inc(s_out, 16)
            sp.wait_ge(s_out, 48)

        @block.gpsimd
        def _(pool):
            def setup(n, ins):
                ins.then_inc(s_setup, 1)
                pool.wait_ge(s_setup, n)
            setup(1, pool.iota(iota16[:, :], [[1, P]], base=0, channel_multiplier=0, allow_small_or_imprecise_dtypes=True))
            setup(2, pool.iota(pcol[:, :], [[0, 1]], base=0, channel_multiplier=CELL, allow_small_or_imprecise_dtypes=True))
            setup(3, pool.iota(heads[:, :], [[1, P]], base=0, channel_multiplier=P))
            setup(4, pool.memset(zero[:, :], 0.0))
            pool.memset(dummy[:, :], 0.0).then_inc(s_zero, 1)
            pool.wait_ge(s_row, 1)
            pool.wait_ge(s_cells, 16)
            with pool.Fori(0, ROW_CAP // 16) as i:
                pool.tensor_copy(sidx[:, :], posi[:, bass.ts(i, 16)]).then_inc(s_stage, 1)
                pool.tensor_copy(skey[:, :], row[:, bass.ts(i, 16)]).then_inc(s_stage, 1)
                pool.wait_ge(s_stage, i * 4 + 2)
                pool.tensor_tensor(dummy[:, 1:2], dummy[:, 0:1], dummy[:, 0:1], ALU.add).then_inc(s_stage, 1)
                for c in range(16):
                    pool.indirect_dma_start(d.cells, bass.IndirectOffsetOnAxis(ap=sidx[:, c:c + 1], axis=0), skey[:, c:c + 1], None,
                                            bounds_check=P * CELLS - 1, oob_is_err=False).then_inc(s_scat, 16)
                pool.wait_ge(s_scat, i * 256 + 256)
                pool.tensor_tensor(dummy[:, 2:3], dummy[:, 0:1], dummy[:, 0:1], ALU.add).then_inc(s_stage, 1)

        @block.tensor
        def _(pe):
            with pe.Fori(0, EC // HC // 2) as i:
                for b in range(2):
                    pe.wait_ge(s_added, i * 2 + b + 1)
                    pe.wait_ge(s_ohl, i * 2 + b + 1)
                    pe.wait_ge(s_ohh, i * 2 + b + 1)
                    for c in range(HC):
                        last = pe.matmul(psum[:, b, 0:P], ohl[:, b, c, :], ohh[:, b, c, :], start=c == 0, stop=c == HC - 1)
                    last.then_inc(s_cnt, 1)

        @block.vector
        def _(dve):
            link = Chain(dve, s_v)
            dve.wait_ge(s_setup, 4)
            link(dve.memset(left[:, :], 0.0))
            dve.memset(cnt[:, :], 0.0).then_inc(s_cnt, 2)
            dve.memset(work[:, :], 0.0).then_inc(s_added, 2)
            dve.memset(cells[:, 0:8], 0.0).then_inc(s_key, 1)

            def largest(values, out, n):
                for r in range(n):
                    link(dve.max(out[:, 8 * r:8 * r + 8], values))
                    link(dve.match_replace(values, out[:, 8 * r:8 * r + 8], values, 0.0))

            def note_left(values):
                link(dve.tensor_reduce(left[:, 1:2], values, AX_X, ALU.max))
                link(dve.tensor_tensor(left[:, 0:1], left[:, 0:1], left[:, 1:2], ALU.max))

            def make_keys(i):
                at = bass.ts(i, CH)
                dve.wait_ge(s_src, i * 16 + 16)
                dve.wait_ge(s_dst, i * 16 + 16)
                link(dve.tensor_scalar(t0[:, :], dst[:, :], M - 1, 14, ALU.bitwise_and, ALU.logical_shift_left))
                link(dve.scalar_tensor_tensor(out=t0[:, :], in0=t0[:, :], scalar=KEY_BIT, in1=src[:, :],
                                              op0=ALU.bitwise_or, op1=ALU.bitwise_or))
                link(dve.scalar_tensor_tensor(out=keys[:, at], in0=dst[:, :], scalar=float(M), in1=t0[:, :].bitcast(F32),
                                              op0=ALU.is_lt, op1=ALU.mult))
                link(dve.scalar_tensor_tensor(out=keys[:, at], in0=src[:, :], scalar=float(LAST), in1=keys[:, at],
                                              op0=ALU.is_lt, op1=ALU.mult))
                link(dve.tensor_scalar(t0[:, :], dst[:, :], 7, None, ALU.logical_shift_right))
                dve.tensor_copy(hi[:, at], t0[:, :])
                link(dve.tensor_scalar(dst[:, :], dst[:, :], P - 1, None, ALU.bitwise_and))
                link(dve.tensor_scalar(src[:, :], src[:, :], float(LAST), float(P), ALU.is_lt, ALU.mult))
                link(dve.tensor_tensor(lo[:, at], src[:, :], dst[:, :], ALU.add))
                dve.tensor_copy(t0[:, 0:1], src[:, 0:1]).then_inc(s_c, 1)
                dve.memset(t0[:, 1:2], 0).then_inc(s_key, 1)
            link.loop(NCH, make_keys)

            with dve.Fori(0, EC // HC // 2) as i:
                for b in range(2):
                    dve.wait_ge(s_cnt, i * 2 + b + 1)
                    dve.tensor_tensor(ohl[:, b, :, :], iota16[:, None, :].to_broadcast([P, HC, P]),
                                      lo[:, bass.ds((i * 2 + b) * HC, HC)][:, :, None].to_broadcast([P, HC, P]), ALU.is_equal).then_inc(s_ohl, 1)
                    dve.tensor_tensor(ohh[:, b, :, :], iota16[:, None, :].to_broadcast([P, HC, P]),
                                      hi[:, bass.ds((i * 2 + b) * HC, HC)][:, :, None].to_broadcast([P, HC, P]), ALU.is_equal).then_inc(s_ohh, 1)
                for b in range(2):
                    dve.wait_ge(s_cnt, i * 2 + b + 3)
                    if b:
                        dve.wait_ge(s_added, i * 2 + b + 2)
                    dve.tensor_tensor(cnt[:, :], cnt[:, :], psum[:, b, 0:P], ALU.add).then_inc(s_added, 1)

            def sort_segment(i):
                link(dve.tensor_copy(work[:, :], keys[:, bass.ts(i, SEG)]))
                largest(work[:, :], found, SEG_CAP // 8)
                note_left(work[:, :])
                link(dve.tensor_copy(first[:, bass.ts(i, SEG_CAP)], found[:, :]))
            link.loop(NSEG, sort_segment)

            def sort_row(i):
                largest(first[:, :], top, 8)
                link(dve.tensor_copy(row[:, bass.ts(i, 64)], top[:, :]))
            link.loop(ROW_CAP // 64, sort_row)
            note_left(first[:, :])

            link(dve.tensor_scalar(bi[:, :], row[:, :].bitcast(I32), 21, None, ALU.logical_shift_right))
            link(dve.memset(bucket[:, 0:1], -1.0))
            link(dve.tensor_copy(bucket[:, 1:ROW_CAP + 1], bi[:, :]))
            link(dve.tensor_tensor(same[:, :], bucket[:, 1:ROW_CAP + 1], bucket[:, 0:ROW_CAP], ALU.is_equal))
            link(dve.tensor_tensor_scan(rank[:, :], same[:, :], same[:, :], 0.0, ALU.mult, ALU.add))
            link(dve.tensor_scalar(same[:, :], bucket[:, 1:ROW_CAP + 1], float(KEY_BIT >> 21), None, ALU.is_ge))
            link(dve.tensor_tensor(pos[:, :], rank[:, :], same[:, :], ALU.mult))
            link(dve.tensor_scalar(pos[:, :], pos[:, :], float(CELL), None, ALU.is_ge))
            note_left(pos[:, :])
            link(dve.tensor_tensor(pos[:, :], pos[:, :], same[:, :], ALU.subtract))
            link(dve.tensor_scalar(pos[:, :], pos[:, :], FAR, FAR, ALU.mult, ALU.add))
            link(dve.tensor_scalar(bucket[:, 1:ROW_CAP + 1], bucket[:, 1:ROW_CAP + 1], float(KEY_BIT >> 21), 0.0, ALU.subtract, ALU.max))
            link(dve.tensor_scalar(bucket[:, 1:ROW_CAP + 1], bucket[:, 1:ROW_CAP + 1], float(CELLS), pcol[:, 0:1], ALU.mult, ALU.add))
            link(dve.tensor_tensor(rank[:, :], rank[:, :], bucket[:, 1:ROW_CAP + 1], ALU.add))
            link(dve.tensor_tensor(posi[:, :], rank[:, :], pos[:, :], ALU.add))
            dve.memset(top[:, 0:1], 0.0).then_inc(s_row, 1)

            link(dve.tensor_scalar(heads[:, :], heads[:, :], 14, KEY_BIT, ALU.logical_shift_left, ALU.bitwise_or))
            link(dve.tensor_scalar(heads[:, :], heads[:, :], LAST, None, ALU.bitwise_or))
            link(dve.tensor_copy(merged[:, NBSEG * BSEG_CAP:NBSEG * BSEG_CAP + P], heads[:, :].bitcast(F32)))
            dve.wait_ge(s_fill, 16)

            def sort_bucket_segment(i):
                link(dve.tensor_copy(work[:, :], cells[:, bass.ts(i, BSEG)]))
                largest(work[:, :], found2, BSEG_CAP // 8)
                note_left(work[:, :])
                link(dve.tensor_copy(merged[:, bass.ts(i, BSEG_CAP)], found2[:, :]))
            link.loop(NBSEG, sort_bucket_segment)

            def sort_bucket(i):
                largest(merged[:, :], top, 8)
                link(dve.tensor_copy(slots[:, bass.ts(i, 64)], top[:, :]))
            link.loop(SLOTS // 64, sort_bucket)
            note_left(merged[:, :])
            dve.tensor_scalar(over[:, :], left[:, 0:1], 0.0, None, ALU.is_gt).then_inc(s_done, 1)


def message_phase(nc, d):
    with ExitStack() as ctx:
        def sb(name, shape, dt=F32):
            return ctx.enter_context(nc.sbuf_tensor(name, shape, dt))

        def sem(name):
            return ctx.enter_context(nc.semaphore(name))

        slots = sb("m_slots", [P, SLOTS])
        ki = sb("m_ki", [P, SLOTS], I32)
        dsti = sb("m_dsti", [P, SLOTS], I32)
        live = sb("m_live", [P, SLOTS])
        head = sb("m_head", [P, SLOTS])
        dst = sb("m_dst", [P, SLOTS + 2])
        low = sb("m_low", [P, SLOTS])
        idx = sb("m_idx", [P, SLOTS])
        idxT, lowT = sb("m_idxT", [P, KT, P], I32), sb("m_lowT", [P, KT, P])
        same = sb("m_same", [P, SLOTS])
        pen = sb("m_pen", [P, 2, SLOTS])
        sidx = sb("m_sidx", [P, 2, 16], I32)
        stage = sb("m_stage", [P, 2, 16, ROW])
        G = sb("m_G", [P, SLOTS, 24])
        s, dd = sb("m_s", [P, 4, SLOTS]), sb("m_d", [P, 4, SLOTS])
        f, r = sb("m_f", [P, 4, SLOTS]), sb("m_r", [P, 4, SLOTS])
        hot = sb("m_hot", [P, 2, KT, P])
        iota = sb("m_iota", [P, P])
        ident = sb("m_ident", [P, P])
        rows = sb("m_rows", [P, P, ROW])
        crow = sb("m_crow", [P, ROW])
        cnt = sb("m_cnt", [P, P])
        A = sb("m_A", [P, P, 24])
        dummy, dummy2 = sb("m_dummy", [P, 3]), sb("m_dummy2", [P, 8])
        ps = ctx.enter_context(nc.psum_tensor("m_ps", [P, 8, 512], F32))
        s_in, s_setup, s_v, s_idx, s_tr, s_stage = (sem("m_s_" + n) for n in ("in", "setup", "v", "idx", "tr", "stage"))
        s_g = [sem("m_s_g0"), sem("m_s_g1")]
        s_copied, s_sd, s_back, s_bk, s_hot, s_used, s_sum, s_pre, s_exp, s_w, s_done, s_out = (
            sem("m_s_" + n) for n in ("copied", "sd", "back", "bk", "hot", "used", "sum", "pre", "exp", "w", "done", "out"))
        block = ctx.enter_context(nc.Block())

        @block.sync
        def _(sp):
            sp.dma_start(slots[:, :], d.slots).then_inc(s_in, 16)
            sp.dma_start(cnt[:, :], d.cnt).then_inc(s_in, 16)
            sp.dma_start(rows[:, :, :], d.tab.rearrange("b n c -> (b n) c").rearrange("(t p) c -> p t c", p=P)).then_inc(s_in, 16)
            sp.dma_start(crow[:, :], d.tab.rearrange("b n c -> (b n) c")[LAST:LAST + 1, :].to_broadcast([P, ROW])).then_inc(s_in, 16)
            sp.wait_ge(s_done, 1)
            sp.dma_start(d.sums, A[:, :, 0:20]).then_inc(s_out, 16)
            sp.wait_ge(s_out, 16)

        @block.gpsimd
        def _(pool):
            def setup(n, ins):
                ins.then_inc(s_setup, 1)
                pool.wait_ge(s_setup, n)
            setup(1, pool.iota(iota[:, :], [[1, P]], base=0, channel_multiplier=0, allow_small_or_imprecise_dtypes=True))
            setup(2, pool.memset(ident[:, :], 0.0))
            setup(3, pool.affine_select(out=ident[:, :], in_=ident[:, :], compare_op=ALU.not_equal, fill=1.0, base=0,
                                        pattern=[[-1, P]], channel_multiplier=1))
            setup(4, pool.memset(dummy[:, :], 0.0))
            pool.wait_ge(s_idx, 3)
            table = d.tab.rearrange("b n c -> (b n) c")
            idx_flat = idxT[:, :, :].rearrange("p k b -> p (k b)")
            with pool.Fori(0, SLOTS // 32) as i:
                for b in range(2):
                    pool.wait_ge(s_copied, i * 2 + b + 1)
                    pool.tensor_copy(sidx[:, b, :], idx_flat[:, bass.ds(i * 32 + b * 16, 16)]).then_inc(s_stage, 1)
                    pool.wait_ge(s_stage, i * 4 + 2 * b + 1)
                    pool.tensor_tensor(dummy[:, 1 + b:2 + b], dummy[:, 0:1], dummy[:, 0:1], ALU.add).then_inc(s_stage, 1)
                    for c in range(16):
                        pool.indirect_dma_start(stage[:, b, c, :], None, table, bass.IndirectOffsetOnAxis(ap=sidx[:, b, c:c + 1], axis=0),
                                                bounds_check=LAST, oob_is_err=False).then_inc(s_g[b], 16)

        @block.scalar
        def _(act):
            with act.Fori(0, SLOTS // 32) as i:
                for b in range(2):
                    act.wait_ge(s_g[b], i * 256 + 256)
                    act.activation(G[:, bass.ds(i * 32 + b * 16, 16), :], stage[:, b, :, 0:24], ACT.Copy).then_inc(s_copied, 1)
            act.wait_ge(s_pre, 1)
            act.activation(s[:, :, :], s[:, :, :], ACT.Exp).then_inc(s_exp, 1)
            act.wait_ge(s_pre, 2)
            act.activation(A[:, :, 20:24], A[:, :, 20:24], ACT.Exp).then_inc(s_exp, 1)
            act.activation(rows[:, :, 20:24], rows[:, :, 20:24], ACT.Exp).then_inc(s_exp, 1)

        @block.tensor
        def _(pe):
            pe.wait_ge(s_setup, 4)
            pe.wait_ge(s_idx, 2)
            for n, t in enumerate((idx, low)):
                for k in range(KT):
                    last = pe.transpose(ps[:, 2 * n + k // 4, (k % 4) * P:(k % 4 + 1) * P], t[:, k * P:(k + 1) * P], ident[:, :])
                last.then_inc(s_tr, 1)
            pe.wait_ge(s_copied, SLOTS // 16 + 2)
            pe.wait_ge(s_idx, 3)
            for k in range(KT):
                for n in range(2):
                    if 2 * k + n >= 8:
                        pe.wait_ge(s_sd, 2 * k + n - 7)
                    for hd in range(4):
                        last = pe.transpose(ps[:, (2 * k + n) % 8, hd * P:(hd + 1) * P], G[:, k * P:(k + 1) * P, 16 + 4 * n + hd], ident[:, :])
                    last.then_inc(s_back, 1)
            pe.wait_ge(s_w, 1)
            for k in range(KT):
                for n, t in enumerate((s, f)):
                    if 2 * k + n >= 8:
                        pe.wait_ge(s_bk, 2 * k + n - 7)
                    for hd in range(4):
                        last = pe.transpose(ps[:, (2 * k + n) % 8, hd * P:(hd + 1) * P], t[:, hd, k * P:(k + 1) * P], ident[:, :])
                    last.then_inc(s_back, 1)
            pe.wait_ge(s_w, 2)
            sums = ps[:, :, :].rearrange("p b (c n) -> p (b c) n", n=32)
            with pe.Fori(0, P // 2) as i:
                for b in range(2):
                    pe.wait_ge(s_hot, i * 2 + b + 1)
                    for k in range(KT):
                        last = pe.matmul(sums[:, bass.ds(i * 2 + b, 1), 0:24].rearrange("p a n -> p (a n)"), hot[:, b, k, :],
                                         G[:, bass.ds(i * 2 + (b + k * P), 1), :].rearrange("p a n -> p (a n)"), start=k == 0, stop=k == KT - 1)
                    last.then_inc(s_used, 1)

        @block.vector
        def _(dve):
            link = Chain(dve, s_v)
            dve.wait_ge(s_setup, 4)
            dve.wait_ge(s_in, 64)
            link(dve.memset(dst[:, :], -2.0))
            link(dve.tensor_scalar(ki[:, :], slots[:, :].bitcast(I32), LAST, None, ALU.bitwise_and))
            link(dve.tensor_scalar(head[:, :], ki[:, :], float(LAST), None, ALU.is_equal))
            link(dve.tensor_scalar(dsti[:, :], slots[:, :].bitcast(I32), 14, LAST, ALU.logical_shift_right, ALU.bitwise_and))
            link(dve.tensor_scalar(live[:, :], slots[:, :], 0.0, None, ALU.is_gt))
            link(dve.scalar_tensor_tensor(out=idx[:, :], in0=dsti[:, :], scalar=-float(LAST), in1=head[:, :], op0=ALU.add, op1=ALU.mult))
            link(dve.tensor_tensor(idx[:, :], idx[:, :], ki[:, :], ALU.add))
            link(dve.scalar_tensor_tensor(out=dst[:, 1:SLOTS + 1], in0=dsti[:, :], scalar=1.0, in1=live[:, :], op0=ALU.add, op1=ALU.mult))
            link(dve.tensor_scalar(dst[:, 1:SLOTS + 1], dst[:, 1:SLOTS + 1], 1.0, None, ALU.subtract))
            link(dve.tensor_scalar(dsti[:, :], dsti[:, :], P - 1, None, ALU.bitwise_and))
            link(dve.tensor_scalar(low[:, :], live[:, :], -512.0, 512.0, ALU.mult, ALU.add))
            link(dve.tensor_tensor(low[:, :], low[:, :], dsti[:, :], ALU.add))
            link(dve.tensor_tensor(same[:, :], dst[:, 1:SLOTS + 1], dst[:, 0:SLOTS], ALU.is_equal))
            link(dve.tensor_scalar(pen[:, 0, :], same[:, :], 1.0, -MASKED, ALU.subtract, ALU.mult))
            link(dve.tensor_tensor(pen[:, 1, :], dst[:, 1:SLOTS + 1], dst[:, 2:SLOTS + 2], ALU.is_equal))
            link(dve.tensor_scalar(pen[:, 1, :], pen[:, 1, :], 1.0, -MASKED, ALU.subtract, ALU.mult))
            dve.memset(dummy2[:, 0:1], 0.0).then_inc(s_copied, 2)
            dve.memset(dummy2[:, 6:7], 0.0).then_inc(s_used, 2)
            dve.memset(dummy2[:, 1:2], 0.0).then_inc(s_idx, 2)
            dve.wait_ge(s_tr, 2)
            psk = ps[:, 0:4, :].rearrange("p (n b) m -> p n (b m)", n=2)
            link(dve.tensor_copy(idxT[:, :, :].rearrange("p k b -> p (k b)"), psk[:, 0, 0:SLOTS]))
            link(dve.tensor_copy(lowT[:, :, :].rearrange("p k b -> p (k b)"), psk[:, 1, 0:SLOTS]))
            dve.memset(dummy2[:, 2:3], 0.0).then_inc(s_idx, 1)
            for k in range(KT):
                for n, t in enumerate((s, dd)):
                    dve.wait_ge(s_back, 2 * k + n + 1)
                    dve.tensor_copy(t[:, :, k * P:(k + 1) * P], ps[:, (2 * k + n) % 8, :].rearrange("p (h b) -> p h b", h=4)).then_inc(s_sd, 1)
            dve.wait_ge(s_sd, 2 * KT)
            link(dve.tensor_tensor(dd[:, :, :], dd[:, :, :], head[:, None, :].to_broadcast([P, 4, SLOTS]), ALU.mult))
            for hd in range(4):
                dve.tensor_tensor_scan(r[:, hd, :], same[:, :], dd[:, hd, :], 0.0, ALU.mult, ALU.add)
                last = dve.tensor_tensor_scan(f[:, hd, :], pen[:, 0, :], s[:, hd, :], MASKED, ALU.add, ALU.max)
            link(last)
            for hd in range(4):
                last = dve.tensor_tensor_scan(dd[:, hd, ::-1], pen[:, 1, ::-1], f[:, hd, ::-1], MASKED, ALU.add, ALU.max)
            link(last)
            link(dve.tensor_copy(f[:, :, :], dd[:, :, :]))
            link(dve.tensor_tensor(s[:, :, :], s[:, :, :], r[:, :, :], ALU.add))
            link(dve.tensor_tensor(r[:, :, :], r[:, :, :], f[:, :, :], ALU.add))
            link(dve.scalar_tensor_tensor(out=s[:, :, :], in0=s[:, :, :], scalar=LEAK, in1=s[:, :, :], op0=ALU.mult, op1=ALU.max))
            link(dve.scalar_tensor_tensor(out=r[:, :, :], in0=r[:, :, :], scalar=LEAK, in1=r[:, :, :], op0=ALU.mult, op1=ALU.max))
            dve.tensor_tensor(s[:, :, :], s[:, :, :], r[:, :, :], ALU.subtract).then_inc(s_pre, 1)
            link(dve.tensor_tensor(f[:, :, :], f[:, :, :], head[:, None, :].to_broadcast([P, 4, SLOTS]), ALU.mult))
            dve.wait_ge(s_exp, 1)
            dve.memset(dummy2[:, 3:4], 0.0).then_inc(s_w, 1)
            for k in range(KT):
                for n in range(2):
                    dve.wait_ge(s_back, 2 * KT + 2 * k + n + 1)
                    dve.tensor_copy(G[:, k * P:(k + 1) * P, 16 + 4 * n:20 + 4 * n],
                                    ps[:, (2 * k + n) % 8, :].rearrange("p (h b) -> p b h", h=4)).then_inc(s_bk, 1)
            dve.wait_ge(s_bk, 2 * KT)
            dve.tensor_tensor(G[:, :, 0:16].rearrange("p t (h e) -> p t h e", h=4), G[:, :, 0:16].rearrange("p t (h e) -> p t h e", h=4),
                              G[:, :, 16:20][:, :, :, None].to_broadcast([P, SLOTS, 4, 4]), ALU.mult).then_inc(s_w, 1)
            with dve.Fori(0, P // 2) as i:
                for b in range(2):
                    dve.wait_ge(s_used, i * 2 + b + 1)
                    dve.tensor_tensor(hot[:, b, :, :], iota[:, None, :].to_broadcast([P, KT, P]),
                                      lowT[:, :, bass.ds(i * 2 + b, 1)].to_broadcast([P, KT, P]), ALU.is_equal).then_inc(s_hot, 1)
            dve.wait_ge(s_used, P + 2)
            for b in range(8):
                last = dve.tensor_copy(A[:, 16 * b:16 * b + 16, :], ps[:, b, :].rearrange("p (c n) -> p c n", n=32)[:, :, 0:24])
            link(last)
            def wide(x):
                return x.to_broadcast([P, P, 4])
            m, l, ad = A[:, :, 20:24], A[:, :, 16:20], rows[:, :, 20:24]
            en, ec = rows[:, :, 0:4], rows[:, :, 4:8]
            cs = crow[:, None, 16:20].to_broadcast([P, P, 4])
            link(dve.tensor_scalar(rows[:, :, 8:9], cnt[:, :, None], 0.0, MASKED, ALU.is_le, ALU.mult))
            link(dve.tensor_tensor(en, cs, wide(rows[:, :, 8:9]), ALU.add))
            link(dve.tensor_tensor(en, en, m, ALU.max))
            link(dve.tensor_tensor(en, en, ad, ALU.add))
            link(dve.tensor_tensor(m, m, ad, ALU.add))
            link(dve.tensor_tensor(ec, cs, ad, ALU.add))
            for x in (en, m, ec):
                link(dve.scalar_tensor_tensor(out=x, in0=x, scalar=LEAK, in1=x, op0=ALU.mult, op1=ALU.max))
            link(dve.tensor_tensor(m, m, en, ALU.subtract))
            link(dve.tensor_tensor(ec, ec, en, ALU.subtract))
            link(dve.tensor_scalar(ad, ec, 0.0, None, ALU.min))
            dve.memset(dummy2[:, 4:5], 0.0).then_inc(s_pre, 1)
            dve.wait_ge(s_exp, 3)
            link(dve.tensor_tensor(ad, ad, wide(cnt[:, :, None]), ALU.mult))
            link(dve.tensor_tensor(l, l, m, ALU.mult))
            link(dve.tensor_tensor(l, l, ad, ALU.add))
            for hd in range(4):
                acc = A[:, :, 4 * hd:4 * hd + 4]
                link(dve.tensor_tensor(acc, acc, wide(m[:, :, hd:hd + 1]), ALU.mult))
                link(dve.tensor_tensor(en, crow[:, None, 4 * hd:4 * hd + 4].to_broadcast([P, P, 4]), wide(ad[:, :, hd:hd + 1]), ALU.mult))
                link(dve.tensor_tensor(acc, acc, en, ALU.add))
            dve.memset(dummy2[:, 5:6], 0.0).then_inc(s_done, 1)


DEAD = 20000.0


def general_phase(nc, d, edges=E):
    with ExitStack() as ctx:
        def sb(name, shape, dt=F32):
            return ctx.enter_context(nc.sbuf_tensor(name, shape, dt))

        def sem(name):
            return ctx.enter_context(nc.semaphore(name))

        over, flag = sb("g_over", [P, 1]), sb("g_flag", [P, 1], I32)
        ident, low = sb("g_ident", [P, P]), sb("g_low", [P, P])
        cnt = sb("g_cnt", [P, P])
        crow = sb("g_crow", [P, ROW])
        rows = sb("g_rows", [P, P, ROW])
        state = sb("g_state", [P, P, ROW])
        e3 = sb("g_e3", [P, P, 12])
        esrc, edst = sb("g_esrc", [P, 1], I32), sb("g_edst", [P, 1], I32)
        keep, dst = sb("g_keep", [P, 1]), sb("g_dst", [P, 1])
        si, di, oi = sb("g_si", [P, 1], I32), sb("g_di", [P, 1], I32), sb("g_oi", [P, 1], I32)
        dup = sb("g_dup", [P, 1])
        g, old, new = sb("g_g", [P, ROW]), sb("g_old", [P, ROW]), sb("g_new", [P, ROW])
        eq, pen, t1 = sb("g_eq", [P, P]), sb("g_pen", [P, P]), sb("g_t1", [P, P])
        sm = sb("g_sm", [P, 4, P])
        x = sb("g_x", [P, 12])
        y = sb("g_y", [P, 8])
        v = sb("g_v", [P, 20])
        dummy = sb("g_dummy", [P, 8])
        ps = ctx.enter_context(nc.psum_tensor("g_ps", [P, 3, 512], F32))
        s_in, s_setup, s_flag, s_v, s_pre, s_exp, s_init, s_stored = (
            sem("g_s_" + n) for n in ("in", "setup", "flag", "v", "pre", "exp", "init", "stored"))
        s_e, s_next, s_idx, s_g, s_row, s_vv, s_sum, s_new, s_xx, s_yy, s_pool = (
            sem("g_s_" + n) for n in ("e", "next", "idx", "g", "row", "vv", "sum", "new", "xx", "yy", "pool"))
        s_back, s_sums, s_out = sem("g_s_back"), sem("g_s_sums"), sem("g_s_out")
        block = ctx.enter_context(nc.Block())
        TILES = edges // P
        table = d.tab.rearrange("b n c -> (b n) c")

        def by_tile(t):
            return t.rearrange("(t p) c -> p t c", p=P)

        def column(n, i):
            return d.edges[n, bass.ds(i * P, P)].rearrange("(p a) -> p a", a=1)

        @block.sync
        def _(sp):
            sp.dma_start(over[:, :], d.over).then_inc(s_in, 16)
            sp.wait_ge(s_flag, 1)
            overflow = sp.value_load(flag[0:1, 0:1], min_val=0, max_val=1)
            with sp.If(overflow > 0):
                sp.dma_start(cnt[:, :], d.cnt).then_inc(s_in, 16)
                sp.dma_start(rows[:, :, :], by_tile(table)).then_inc(s_in, 16)
                sp.dma_start(crow[:, :], table[LAST:LAST + 1, :].to_broadcast([P, ROW])).then_inc(s_in, 16)
                sp.wait_ge(s_init, 1)
                sp.dma_start(by_tile(d.state), state[:, :, :]).then_inc(s_stored, 16)
                with sp.Fori(0, TILES) as i:
                    sp.wait_ge(s_idx, i * 1 + 1)
                    sp.dma_start(esrc[:, :], column(0, i)).then_inc(s_e, 16)
                    sp.dma_start(edst[:, :], column(1, i)).then_inc(s_e, 16)
                sp.wait_ge(s_new, 16 * TILES + 16)
                sp.dma_start(state[:, :, :], by_tile(d.state)).then_inc(s_back, 16)
                sp.wait_ge(s_back, 16)
                sp.dma_start(d.sums, state[:, :, 0:20]).then_inc(s_out, 16)
                sp.wait_ge(s_out, 16)

        @block.gpsimd
        def _(pool):
            def setup(n, ins):
                ins.then_inc(s_setup, 1)
                pool.wait_ge(s_setup, n)
            pool.wait_ge(s_in, 16)
            pool.partition_all_reduce(flag[:, :], over[:, :], P, bass.bass_isa.ReduceOp.max).then_inc(s_flag, 1)
            pool.wait_ge(s_flag, 1)
            overflow = pool.value_load(flag[0:1, 0:1], min_val=0, max_val=1)
            with pool.If(overflow > 0):
                setup(1, pool.memset(ident[:, :], 0.0))
                setup(2, pool.affine_select(out=ident[:, :], in_=ident[:, :], compare_op=ALU.not_equal, fill=1.0, base=0,
                                            pattern=[[-1, P]], channel_multiplier=1))
                setup(3, pool.memset(low[:, :], 1.0))
                setup(4, pool.affine_select(out=low[:, :], in_=low[:, :], compare_op=ALU.is_gt, fill=0.0, base=0,
                                            pattern=[[-1, P]], channel_multiplier=1))
                setup(5, pool.memset(dummy[:, :], 0.0))
                pool.wait_ge(s_stored, 16)
                pool.dma_start(d.scrap[:, 0:8], ident[:, 0:8]).then_inc(s_new, 16)
                with pool.Fori(0, TILES) as i:
                    pool.wait_ge(s_idx, i * 1 + 2)
                    pool.tensor_tensor(dummy[:, 1:2], dummy[:, 0:1], dummy[:, 0:1], ALU.add).then_inc(s_pool, 1)
                    pool.indirect_dma_start(g[:, :], None, table, bass.IndirectOffsetOnAxis(ap=si[:, 0:1], axis=0),
                                            bounds_check=LAST, oob_is_err=False).then_inc(s_g, 16)
                    pool.wait_ge(s_new, i * 16 + 16)
                    pool.tensor_tensor(dummy[:, 2:3], dummy[:, 0:1], dummy[:, 0:1], ALU.add).then_inc(s_pool, 1)
                    pool.indirect_dma_start(old[:, :], None, d.state, bass.IndirectOffsetOnAxis(ap=di[:, 0:1], axis=0),
                                            bounds_check=LAST, oob_is_err=False).then_inc(s_g, 16)
                    pool.wait_ge(s_next, i * 1 + 1)
                    pool.tensor_tensor(dummy[:, 3:4], dummy[:, 0:1], dummy[:, 0:1], ALU.add).then_inc(s_pool, 1)
                    pool.indirect_dma_start(d.state, bass.IndirectOffsetOnAxis(ap=oi[:, 0:1], axis=0), new[:, :], None,
                                            bounds_check=LAST, oob_is_err=False).then_inc(s_new, 16)
                    pool.wait_ge(s_pool, i * 3 + 3)

        @block.scalar
        def _(act):
            act.wait_ge(s_flag, 1)
            overflow = act.value_load(flag[0:1, 0:1], min_val=0, max_val=1)
            with act.If(overflow > 0):
                act.wait_ge(s_pre, 1)
                act.activation(e3[:, :, 0:8], e3[:, :, 0:8], ACT.Exp).then_inc(s_exp, 1)
                with act.Fori(0, TILES) as i:
                    act.wait_ge(s_xx, i * 1 + 1)
                    act.activation(y[:, :], y[:, :], ACT.Exp).then_inc(s_yy, 1)

        @block.tensor
        def _(pe):
            pe.wait_ge(s_flag, 1)
            overflow = pe.value_load(flag[0:1, 0:1], min_val=0, max_val=1)
            with pe.If(overflow > 0):
                pe.wait_ge(s_setup, 5)
                with pe.Fori(0, TILES) as i:
                    pe.wait_ge(s_idx, i * 1 + 2)
                    pe.transpose(ps[:, 0, 0:P], dst[:, 0:1].to_broadcast([P, P]), ident[:, :]).then_inc(s_row, 1)
                    pe.wait_ge(s_g, i * 32 + 32)
                    for hd in range(4):
                        last = pe.transpose(ps[:, 1, hd * P:(hd + 1) * P], g[:, 16 + hd:17 + hd].to_broadcast([P, P]), ident[:, :])
                    last.then_inc(s_row, 1)
                    pe.wait_ge(s_vv, i * 1 + 1)
                    pe.matmul(ps[:, 2, 0:20], eq[:, :], v[:, :], start=True, stop=True).then_inc(s_sum, 1)

        @block.vector
        def _(dve):
            dve.wait_ge(s_flag, 1)
            overflow = dve.value_load(flag[0:1, 0:1], min_val=0, max_val=1)
            with dve.If(overflow > 0):
                link = Chain(dve, s_v)
                dve.wait_ge(s_setup, 5)
                dve.wait_ge(s_in, 64)
                def wide(t):
                    return t.to_broadcast([P, P, 4])
                ec, es, en, pn = e3[:, :, 0:4], e3[:, :, 4:8], e3[:, :, 8:12], state[:, :, 0:1]
                a, ad = rows[:, :, 16:20], rows[:, :, 20:24]
                acc, l, m = state[:, :, 0:16], state[:, :, 16:20], state[:, :, 20:24]
                cs = crow[:, None, 16:20].to_broadcast([P, P, 4])
                link(dve.memset(state[:, :, :], 0.0))
                link(dve.tensor_copy(state[:, :, 24:28], ad))
                link(dve.tensor_scalar(pn, cnt[:, :, None], 0.0, MASKED, ALU.is_le, ALU.mult))
                link(dve.tensor_tensor(m, cs, wide(pn), ALU.add))
                link(dve.tensor_tensor(m, m, a, ALU.max))
                link(dve.tensor_tensor(en, m, ad, ALU.add))
                link(dve.tensor_tensor(es, a, ad, ALU.add))
                link(dve.tensor_tensor(ec, cs, ad, ALU.add))
                link(dve.scalar_tensor_tensor(out=e3[:, :, :], in0=e3[:, :, :], scalar=LEAK, in1=e3[:, :, :], op0=ALU.mult, op1=ALU.max))
                link(dve.tensor_tensor(es, es, en, ALU.subtract))
                link(dve.tensor_tensor(ec, ec, en, ALU.subtract))
                link(dve.tensor_scalar(ec, ec, 0.0, None, ALU.min))
                dve.memset(dummy[:, 6:7], 0.0).then_inc(s_pre, 1)
                dve.wait_ge(s_exp, 1)
                link(dve.tensor_tensor(ec, ec, wide(cnt[:, :, None]), ALU.mult))
                link(dve.tensor_tensor(l, ec, es, ALU.add))
                for hd in range(4):
                    part = state[:, :, 4 * hd:4 * hd + 4]
                    link(dve.tensor_tensor(part, rows[:, :, 4 * hd:4 * hd + 4], wide(es[:, :, hd:hd + 1]), ALU.mult))
                    link(dve.tensor_tensor(en, crow[:, None, 4 * hd:4 * hd + 4].to_broadcast([P, P, 4]), wide(ec[:, :, hd:hd + 1]), ALU.mult))
                    link(dve.tensor_tensor(part, part, en, ALU.add))
                dve.memset(dummy[:, 7:8], 0.0).then_inc(s_init, 1)
                dve.memset(keep[:, :], 0.0).then_inc(s_idx, 1)

                def tile(i):
                    dve.wait_ge(s_e, i * 32 + 32)
                    link(dve.tensor_scalar(keep[:, :], esrc[:, :], float(LAST), None, ALU.is_lt))
                    link(dve.scalar_tensor_tensor(out=keep[:, :], in0=edst[:, :], scalar=float(M), in1=keep[:, :], op0=ALU.is_lt, op1=ALU.mult))
                    link(dve.scalar_tensor_tensor(out=dst[:, :], in0=edst[:, :], scalar=-DEAD, in1=keep[:, :], op0=ALU.add, op1=ALU.mult))
                    link(dve.tensor_scalar(dst[:, :], dst[:, :], DEAD, None, ALU.add))
                    link(dve.tensor_scalar(si[:, :], esrc[:, :], float(LAST), None, ALU.min))
                    link(dve.tensor_scalar(di[:, :], dst[:, :], float(LAST), None, ALU.min))
                    dve.memset(y[:, 0:1], 0.0).then_inc(s_idx, 1)
                    dve.wait_ge(s_row, i * 2 + 1)
                    link(dve.tensor_scalar(eq[:, :], ps[:, 0, 0:P], dst[:, 0:1], None, ALU.is_equal))
                    link(dve.tensor_scalar(pen[:, :], eq[:, :], 1.0, -MASKED, ALU.subtract, ALU.mult))
                    link(dve.tensor_tensor(t1[:, :], eq[:, :], low[:, :], ALU.mult))
                    link(dve.tensor_reduce(dup[:, :], t1[:, :], AX_X, ALU.max))
                    link(dve.tensor_scalar(dup[:, :], dup[:, :], DEAD, dst[:, 0:1], ALU.mult, ALU.add))
                    link(dve.tensor_copy(oi[:, :], dup[:, :]))
                    dve.wait_ge(s_row, i * 2 + 2)
                    link(dve.tensor_tensor(sm[:, :, :], ps[:, 1, :].rearrange("p (h n) -> p h n", h=4), pen[:, None, :].to_broadcast([P, 4, P]), ALU.add))
                    link(dve.tensor_reduce(x[:, 0:4], sm[:, :, :], AX_X, ALU.max))
                    dve.wait_ge(s_g, i * 32 + 32)
                    link(dve.tensor_tensor(new[:, 20:24], x[:, 0:4], old[:, 20:24], ALU.max))
                    link(dve.tensor_tensor(x[:, 8:12], new[:, 20:24], old[:, 24:28], ALU.add))
                    link(dve.tensor_tensor(x[:, 4:8], old[:, 20:24], old[:, 24:28], ALU.add))
                    link(dve.tensor_tensor(x[:, 0:4], g[:, 16:20], old[:, 24:28], ALU.add))
                    link(dve.scalar_tensor_tensor(out=x[:, :], in0=x[:, :], scalar=LEAK, in1=x[:, :], op0=ALU.mult, op1=ALU.max))
                    dve.tensor_tensor(y[:, :].rearrange("p (a b) -> p a b", a=2), x[:, 0:8].rearrange("p (a b) -> p a b", a=2),
                                      x[:, None, 8:12].to_broadcast([P, 2, 4]), ALU.subtract).then_inc(s_xx, 1)
                    dve.wait_ge(s_yy, i * 1 + 1)
                    link(dve.tensor_scalar(y[:, 0:4], y[:, 0:4], 1.0, keep[:, 0:1], ALU.min, ALU.mult))
                    link(dve.tensor_copy(v[:, 16:20], y[:, 0:4]))
                    dve.tensor_tensor(v[:, 0:16].rearrange("p (h e) -> p h e", h=4), g[:, 0:16].rearrange("p (h e) -> p h e", h=4),
                                      y[:, 0:4, None].to_broadcast([P, 4, 4]), ALU.mult).then_inc(s_vv, 1)
                    link(dve.tensor_tensor(new[:, 0:16].rearrange("p (h e) -> p h e", h=4), old[:, 0:16].rearrange("p (h e) -> p h e", h=4),
                                           y[:, 4:8, None].to_broadcast([P, 4, 4]), ALU.mult))
                    link(dve.tensor_tensor(new[:, 16:20], old[:, 16:20], y[:, 4:8], ALU.mult))
                    link(dve.tensor_copy(new[:, 24:32], old[:, 24:32]))
                    dve.wait_ge(s_sum, i * 1 + 1)
                    link(dve.tensor_tensor(new[:, 0:20], new[:, 0:20], ps[:, 2, 0:20], ALU.add))
                    dve.memset(dummy[:, 6:7], 0.0).then_inc(s_next, 1)
                    dve.wait_ge(s_new, i * 16 + 32)
                link.loop(TILES, tile)


F = 2 * D
NE = 4
FT = F // P
CHUNK = 512
CT = CHUNK // P


def expert_phase(nc, d):
    with ExitStack() as ctx:
        def sb(name, shape, dt=F32):
            return ctx.enter_context(nc.sbuf_tensor(name, shape, dt))

        def sem(name):
            return ctx.enter_context(nc.semaphore(name))

        w1 = sb("x_w1", [P, NE, 2, F])
        w2 = sb("x_w2", [P, NE, FT, D])
        b1 = sb("x_b1", [P, NE, FT])
        b2 = sb("x_b2", [P, NE, D])
        gpar = sb("x_gpar", [P, 3, GC])
        sums = sb("x_sums", [P, P, 20])
        agg = sb("x_agg", [P, P, GC])
        sq = sb("x_sq", [P, P, GC])
        st = sb("x_st", [P, P, 4])
        score = sb("x_score", [P, P, NE])
        sel = sb("x_sel", [P, P, NE])
        gate = sb("x_gate", [P, P, NE])
        tri = sb("x_tri", [P, NE, NE])
        eps = sb("x_eps", [P, 1])
        xT = sb("x_xT", [P, 2, 2, CHUNK])
        res = sb("x_res", [P, 2, CT, D])
        hid = sb("x_hid", [P, 2, FT, CHUNK])
        y = sb("x_y", [P, 2, CT, D])
        dummy2, zeros = sb("x_dummy2", [P, 8]), sb("x_zeros", [P, 8])
        ps = ctx.enter_context(nc.psum_tensor("x_ps", [P, 8, 512], F32))
        s_w, s_setup, s_v, s_std, s_var, s_gate = (sem("x_s_" + n) for n in ("w", "setup", "v", "std", "var", "gate"))
        s_in = [sem("x_s_in0"), sem("x_s_in1")]
        s_up, s_act, s_down, s_y, s_fin = (sem("x_s_" + n) for n in ("up", "act", "down", "y", "fin"))
        s_out = [sem("x_s_out0"), sem("x_s_out1")]
        block = ctx.enter_context(nc.Block())
        NW = 7
        BODY = 2 * NE

        def node_rows(t, b, half):
            return t[bass.ds(b, 1), half * CHUNK:(half + 1) * CHUNK, :].rearrange("a (t p) n -> p (a t) n", p=P)

        @block.sync
        def _(sp):
            sp.dma_start(sums[:, :, :], d.sums).then_inc(s_w, 16)
            for n, t in enumerate((d.b_gat, d.gamma, d.beta)):
                sp.dma_start(gpar[:, n, :], t.rearrange("(a n) -> a n", a=1).to_broadcast([P, GC])).then_inc(s_w, 16)
            sp.dma_start(w1[:, :, :, :], d.w1.rearrange("e (c p) f -> p e c f", p=P)).then_inc(s_w, 16)
            sp.dma_start(w2[:, :, :, :], d.w2.rearrange("e (c p) n -> p e c n", p=P)).then_inc(s_w, 16)
            sp.dma_start(b2[:, :, :].rearrange("p e n -> p (e n)"),
                         d.b2.rearrange("e n -> (e n)").rearrange("(a n) -> a n", a=1).to_broadcast([P, NE * D])).then_inc(s_w, 16)
            for e in range(NE):
                for f in range(FT):
                    sp.dma_start(b1[:, e, f:f + 1], d.b1[e, f * P:(f + 1) * P].rearrange("(p a) -> p a", a=1)).then_inc(s_w, 16)
            with sp.Fori(0, 16) as i:
                for h in range(2):
                    sp.wait_ge(s_fin, i * 2 + h + 1)
                    sp.dma_start(xT[:, h, :, :], d.xnT[bass.ds(i, 1), :, :, h * CHUNK:(h + 1) * CHUNK].rearrange("a p c n -> p (a c) n"))\
                        .then_inc(s_in[h], 16)
                    sp.wait_ge(s_out[h], i * 16 + 16)
                    sp.dma_start(res[:, h, :, :], node_rows(d.x1, i, h)).then_inc(s_in[h], 16)
            sp.wait_ge(s_out[0], 16 * 17)
            sp.wait_ge(s_out[1], 16 * 17)

        @block.gpsimd
        def _(pool):
            def setup(n, ins):
                ins.then_inc(s_setup, 1)
                pool.wait_ge(s_setup, n)
            setup(1, pool.memset(eps[:, :], LN_EPS))
            setup(2, pool.memset(tri[:, :, :], 1.0))
            setup(3, pool.affine_select(out=tri[:, :, :], in_=tri[:, :, :], compare_op=ALU.is_gt, fill=0.0, base=0,
                                        pattern=[[1, NE], [-1, NE]], channel_multiplier=0))
            setup(4, pool.memset(zeros[:, :], 0.0))
            for h in range(2):
                pool.dma_start(d.scrap[:, h * 8:h * 8 + 8], zeros[:, :]).then_inc(s_out[h], 16)
            with pool.Fori(0, 16) as i:
                for h in range(2):
                    pool.wait_ge(s_fin, i * 2 + h + 3)
                    pool.dma_start(node_rows(d.out, i, h), res[:, h, :, :]).then_inc(s_out[h], 16)

        @block.scalar
        def _(act):
            act.wait_ge(s_setup, 3)
            act.wait_ge(s_var, 1)
            act.activation(st[:, :, 2], st[:, :, 1], ACT.Sqrt, bias=eps[:, 0:1]).then_inc(s_std, 1)
            act.wait_ge(s_var, 2)
            act.activation(gate[:, :, :], gate[:, :, :], ACT.Exp).then_inc(s_std, 1)
            act.wait_ge(s_w, 16 * (NW + 16))
            with act.Fori(0, 16) as i:
                for n in range(BODY):
                    e = n % NE
                    act.wait_ge(s_down, i * BODY + n + 1)
                    for f in range(FT):
                        act.wait_ge(s_up, (i * BODY + n) * FT + f + 1)
                        act.activation(hid[:, n % 2, f, :], ps[:, f, :], ACT.Gelu, bias=b1[:, e, f:f + 1]).then_inc(s_act, 1)

        @block.tensor
        def _(pe):
            pe.wait_ge(s_w, 16 * (NW + 16))
            pe.wait_ge(s_gate, 1)

            def up(i, n):
                h, e = n // NE, n % NE
                if e == 0:
                    pe.wait_ge(s_in[h], i * 32 + 32)
                for f in range(FT):
                    pe.wait_ge(s_act, (i * BODY + n) * FT + f + 1)
                    for c in range(2):
                        last = pe.matmul(ps[:, f, :], w1[:, e, c, f * P:(f + 1) * P], xT[:, h, c, :], start=c == 0, stop=c == 1)
                    last.then_inc(s_up, 1)

            def down(i, n):
                e, at = n % NE, 4 + 2 * (n % 2)
                pe.wait_ge(s_act, (i * BODY + n) * FT + FT + 4)
                pe.wait_ge(s_y, i * BODY + n + 1)
                for t in range(CT):
                    for f in range(FT):
                        last = pe.matmul(ps[:, at + t // 2, (t % 2) * D:(t % 2 + 1) * D], hid[:, n % 2, f, t * P:(t + 1) * P], w2[:, e, f, :],
                                         start=f == 0, stop=f == FT - 1)
                last.then_inc(s_down, 1)

            with pe.Fori(0, 16) as i:
                up(i, 0)
                for n in range(BODY):
                    if n + 1 < BODY:
                        up(i, n + 1)
                    down(i, n)

        @block.vector
        def _(dve):
            link = Chain(dve, s_v)
            dve.wait_ge(s_setup, 3)
            dve.memset(dummy2[:, 0:1], 0.0).then_inc(s_fin, 2)
            dve.memset(dummy2[:, 1:2], 0.0).then_inc(s_y, 2)
            dve.memset(dummy2[:, 2:3], 0.0).then_inc(s_down, 2)
            dve.memset(dummy2[:, 3:4], 0.0).then_inc(s_act, 4)
            dve.wait_ge(s_w, 16 * (NW + 16))

            def wide(x, n):
                return x.to_broadcast([P, P, n])
            link(dve.tensor_scalar(st[:, :, :], sums[:, :, 16:20], 1e-16, None, ALU.add))
            link(dve.reciprocal(st[:, :, :], st[:, :, :]))
            link(dve.tensor_tensor(agg[:, :, :].rearrange("p t (h e) -> p t h e", h=4), sums[:, :, 0:16].rearrange("p t (h e) -> p t h e", h=4),
                                   st[:, :, :, None].to_broadcast([P, P, 4, 4]), ALU.mult))
            link(dve.tensor_tensor(agg[:, :, :], agg[:, :, :], gpar[:, None, 0, :].to_broadcast([P, P, GC]), ALU.add))
            link(dve.tensor_reduce(st[:, :, 0], agg[:, :, :], AX_X, ALU.add))
            link(dve.tensor_scalar(st[:, :, 0], st[:, :, 0], 1.0 / GC, None, ALU.mult))
            link(dve.tensor_tensor(agg[:, :, :], agg[:, :, :], wide(st[:, :, 0:1], GC), ALU.subtract))
            link(dve.tensor_tensor(sq[:, :, :], agg[:, :, :], agg[:, :, :], ALU.mult))
            link(dve.tensor_reduce(st[:, :, 1], sq[:, :, :], AX_X, ALU.add))
            dve.tensor_scalar(st[:, :, 1], st[:, :, 1], 1.0 / GC, None, ALU.mult).then_inc(s_var, 1)
            dve.wait_ge(s_std, 1)
            link(dve.reciprocal(st[:, :, 2], st[:, :, 2]))
            link(dve.tensor_tensor(agg[:, :, :], agg[:, :, :], wide(st[:, :, 2:3], GC), ALU.mult))
            link(dve.tensor_tensor(agg[:, :, :], agg[:, :, :], gpar[:, None, 1, :].to_broadcast([P, P, GC]), ALU.mult))
            link(dve.tensor_tensor(agg[:, :, :], agg[:, :, :], gpar[:, None, 2, :].to_broadcast([P, P, GC]), ALU.add))
            link(dve.tensor_reduce(score[:, :, :], agg[:, :, :].rearrange("p t (h e) -> p t e h", h=4), AX_X, ALU.add))
            link(dve.tensor_scalar(score[:, :, :], score[:, :, :], 0.25, None, ALU.mult))
            mine = score[:, :, :, None].to_broadcast([P, P, NE, NE])
            theirs = score[:, :, None, :].to_broadcast([P, P, NE, NE])
            pairs, ties = (t[:, :, :].rearrange("p t (a b) -> p t a b", a=NE) for t in (agg, sq))
            link(dve.tensor_tensor(pairs, theirs, mine, ALU.is_gt))
            link(dve.tensor_tensor(ties, theirs, mine, ALU.is_equal))
            link(dve.tensor_tensor(ties, ties, tri[:, None, :, :].to_broadcast([P, P, NE, NE]), ALU.mult))
            link(dve.tensor_tensor(pairs, pairs, ties, ALU.add))
            link(dve.tensor_reduce(sel[:, :, :], pairs, AX_X, ALU.add))
            link(dve.tensor_scalar(sel[:, :, :], sel[:, :, :], 1.5, None, ALU.is_lt))
            link(dve.tensor_reduce(st[:, :, 0], score[:, :, :], AX_X, ALU.max))
            dve.tensor_tensor(gate[:, :, :], score[:, :, :], wide(st[:, :, 0:1], NE), ALU.subtract).then_inc(s_var, 1)
            dve.wait_ge(s_std, 2)
            link(dve.tensor_tensor(gate[:, :, :], gate[:, :, :], sel[:, :, :], ALU.mult))
            link(dve.tensor_reduce(st[:, :, 0], gate[:, :, :], AX_X, ALU.add))
            link(dve.reciprocal(st[:, :, 0], st[:, :, 0]))
            link(dve.tensor_tensor(gate[:, :, :], gate[:, :, :], wide(st[:, :, 0:1], NE), ALU.mult))
            dve.memset(dummy2[:, 4:5], 0.0).then_inc(s_gate, 1)

            def combine(i):
                for n in range(BODY):
                    h, e, at = n // NE, n % NE, 4 + 2 * (n % 2)
                    if e == 0:
                        dve.wait_ge(s_in[h], i * 32 + 32)
                    dve.wait_ge(s_down, i * BODY + n + 3)
                    ins = dve.tensor_tensor(y[:, n % 2, :, :], ps[:, at:at + 2, :].rearrange("p b (c n) -> p (b c) n", c=2),
                                            b2[:, None, e, :].to_broadcast([P, CT, D]), ALU.add)
                    ins.then_inc(s_y, 1)
                    dve.wait_ge(s_y, i * BODY + n + 3)
                    for t in range(CT):
                        last = dve.scalar_tensor_tensor(out=res[:, h, t, :], in0=y[:, n % 2, t, :],
                                                        scalar=gate[:, bass.ds(i * 8 + (h * CT + t), 1), e],
                                                        in1=res[:, h, t, :], op0=ALU.mult, op1=ALU.add)
                    if e == NE - 1:
                        last.then_inc(s_fin, 1)
                    else:
                        link(last)
            link.loop(16, combine)


def build(nc, a, out):
    def scratch(name, shape, dt=F32):
        return nc.dram_tensor(name, shape, dt, kind="Internal").ap()

    d = Arrays()
    d.x, d.adj, d.out, d.edges = a["x"], a["adj"], out, a["L0_ffn_edge_index"]
    d.wqT, d.wkT, d.wvT, d.woT = a["WqT"], a["WkT"], a["WvT"], a["WoT"]
    d.bq, d.bk, d.bv, d.bo = a["L0_gnn_bq"], a["L0_gnn_bk"], a["L0_gnn_bv"], a["L0_gnn_bo"]
    d.wgat, d.att_src, d.att_dst, d.b_gat = a["L0_ffn_W_gat"], a["L0_ffn_att_src"], a["L0_ffn_att_dst"], a["L0_ffn_b_gat"]
    d.gamma, d.beta = a["L0_ffn_ln_gamma"], a["L0_ffn_ln_beta"]
    d.w1, d.b1, d.w2, d.b2 = a["L0_ffn_W1"], a["L0_ffn_b1"], a["L0_ffn_W2"], a["L0_ffn_b2"]
    d.x1 = scratch("x1_scratch", (16, N, D))
    d.xnT = scratch("xnT_scratch", (16, P, 2, N))
    d.tab = scratch("tab_scratch", (16, N, ROW))
    d.cells = scratch("cells_scratch", (P * CELLS, 1))
    d.slots = scratch("slots_scratch", (P, SLOTS))
    d.cnt = scratch("cnt_scratch", (P, P))
    d.over = scratch("over_scratch", (P, 1))
    d.sums = scratch("sums_scratch", (P, P, 20))
    d.state = scratch("state_scratch", (M, ROW))
    d.scrap = scratch("scrap_scratch", (P, 16))
    edge_phase(nc, d)
    attention_phase(nc, d, 16)
    message_phase(nc, d)
    general_phase(nc, d)
    expert_phase(nc, d)


_INS = ["x", "adj", "L0_gnn_bq", "L0_gnn_bk", "L0_gnn_bv", "L0_gnn_bo", "L0_ffn_W_gat", "L0_ffn_att_src", "L0_ffn_att_dst",
        "L0_ffn_b_gat", "L0_ffn_ln_gamma", "L0_ffn_ln_beta", "L0_ffn_W1", "L0_ffn_b1", "L0_ffn_W2", "L0_ffn_b2", "L0_ffn_edge_index"]
_TRANSPOSED = {"WqT": "L0_gnn_Wq", "WkT": "L0_gnn_Wk", "WvT": "L0_gnn_Wv", "WoT": "L0_gnn_Wo"}


def kernel(**inputs):
    import numpy as _np
    import concourse.bacc as _bacc
    from concourse import mybir as _mybir
    from concourse.bass_utils import run_bass_kernel_spmd as _run

    nc = _bacc.Bacc("TRN2", target_bir_lowering=False, num_devices=1)
    arrays, args = {}, {}
    laid = {n: _np.ascontiguousarray(inputs[n]) for n in _INS}
    laid.update({n: _np.ascontiguousarray(_np.asarray(inputs[s]).T) for n, s in _TRANSPOSED.items()})
    for name, a in laid.items():
        arrays[f"in_{name}"] = a
        args[name] = nc.dram_tensor(f"in_{name}", a.shape, _mybir.dt.from_np(a.dtype), kind="ExternalInput").ap()
    out = nc.dram_tensor("out_0", (16, N, D), _mybir.dt.float32, kind="ExternalOutput").ap()
    build(nc, args, out)
    r = _run(nc, [arrays], core_ids=[0])
    return r.results[0]["out_0"]
```

```python
from contextlib import ExitStack

import concourse.bass as bass
from concourse import mybir

P = 128
H, HD = 8, 32
SCALE = HD ** -0.5
LN_EPS = 1e-5
GC = 16
ROW = 32
MASKED = -1.0e30
LEAK = 0.2
NO_KEY = -1.0e29

ALU = mybir.AluOpType
ACT = mybir.ActivationFunctionType
F32, BF16, I32 = mybir.dt.float32, mybir.dt.bfloat16, mybir.dt.int32
AX_X = mybir.AxisListType.X
N, D = 1024, 256
TN = N // P


class Arrays:
    pass


class Chain:

    def __init__(self, engine, sem):
        self.engine, self.sem, self.count = engine, sem, 0

    def __call__(self, ins):
        self.count += 1
        ins.then_inc(self.sem, 1)
        self.engine.wait_ge(self.sem, self.count)

    def restart(self):
        self.engine.sem_clear(self.sem)
        self.count = 0

    def loop(self, times, body):
        with self.engine.Fori(0, times) as i:
            self.restart()
            body(i)
        self.restart()


M = 16 * N
E = 1048576
EC = E // P
LAST = M - 1
KEY_BIT = 0x40000000
NSEG = 16
SEG, SEG_CAP = EC // NSEG, 72
CL_CAP = 144
HC = 8
ROW_CAP = 672
CELL = 20
CELLS = P * CELL
BSEG, BSEG_CAP = 512, 152
NBSEG = CELLS // BSEG
SLOTS = 768
KT = SLOTS // P
FAR = 4194304.0
STAGES = (("segments", 8), ("rows", 2), ("cells", 3), ("buckets", 1), ("slots", 2))


def attention_phase(nc, d, B):
    with ExitStack() as ctx:
        def sb(name, shape, dt=F32):
            return ctx.enter_context(nc.sbuf_tensor(name, shape, dt))

        def sem(name):
            return ctx.enter_context(nc.semaphore(name))

        wq, wk, wv, wo = (sb(n, [P, 2, D]) for n in ("wq", "wk", "wv", "wo"))
        wgat = sb("wgat", [P, 2, GC])
        bqk = sb("bqk", [P, 2, 2])
        bv, bo = sb("bv", [P, D]), sb("bo", [P, D])
        att = sb("att", [P, 2, GC])
        ident = sb("ident", [P, P])
        ident16 = sb("ident16", [P, P], BF16)
        ones32 = sb("ones32", [P, 32])
        eps = sb("eps", [P, 1])
        xb = sb("xb", [P, TN, D])
        xn = sb("xn", [P, TN, D])
        xnT = sb("xnT", [P, 2, N])
        stats = sb("stats", [P, TN, 6])
        mv = sb("mv", [P, TN, 2])
        rstd = sb("rstd", [P, TN])
        qf = sb("qf", [P, 2, N])
        kf = sb("kf", [P, 2, N])
        x1 = qf[:, :, :].rearrange("p g (t d) -> p (g t) d", d=D)
        qp = sb("qp", [P, 3, 2, N], BF16)
        kp = sb("kp", [P, 3, 2, N], BF16)
        q1s, k1s = sb("q1s", [P, H, N], BF16), sb("k1s", [P, H, N], BF16)
        q2s, k2s = sb("q2s", [96, H, N], BF16), sb("k2s", [96, H, N], BF16)
        vt = sb("vt", [P, TN, D])
        adjb = sb("adjb", [P, 2, N], I32)
        mb = sb("mb", [P, TN, N], BF16)
        mT = sb("mT", [P, TN, N], BF16)
        junk = sb("junk", [P, 4, 512], BF16)
        mx = sb("mx", [P, 2, TN, 2])
        m3 = sb("m3", [P, 2, TN, 96], BF16)
        mneg = sb("mneg", [P, TN])
        mrem = sb("mrem", [P, TN])
        pt = xn[:, :, :].rearrange("p t d -> p (t d)").rearrange("p (r n) -> p r n", r=2)
        den = kf
        oT = xnT
        tab = sb("tab", [P, TN, ROW])
        tmp16 = kf[:, 0, 0:TN * GC].rearrange("p (t n) -> p t n", t=TN)
        iota8 = sb("iota8", [P, P, HC], BF16)
        cnt = sb("a_cnt", [P, P])
        heads = sb("heads", [P, P], I32)
        left, over = sb("left", [P, 8]), sb("a_over", [P, 1])
        pcol = sb("pcol", [P, 1])
        sidx, skey = sb("sidx", [P, 16], I32), sb("skey", [P, 16])
        dummy = sb("a_dummy", [P, 3])
        store = sb("store", [P, NSEG * SEG_CAP + ROW_CAP])
        kept, row = store[:, 0:NSEG * SEG_CAP], store[:, NSEG * SEG_CAP:NSEG * SEG_CAP + ROW_CAP]
        place = store[:, 0:ROW_CAP].bitcast(I32)
        MERGED = NBSEG * BSEG_CAP + P
        merged, slots = store[:, 0:MERGED], store[:, MERGED:MERGED + SLOTS]
        esrc, edst = adjb[:, 0, :], adjb[:, 1, :]
        adj_flat = adjb[:, :, :].rearrange("p a n -> p (a n)")
        found, found_cl = adj_flat[:, 0:2 * SEG_CAP].bitcast(F32), adj_flat[:, 256:256 + 2 * CL_CAP].bitcast(F32)
        low_int, high_int = adj_flat[:, 1024:1024 + 2 * CL_CAP], adj_flat[:, 1408:1408 + 2 * CL_CAP]
        parts = adj_flat[:, 1728:1728 + 2 * CL_CAP].bitcast(BF16).rearrange("p (a n) -> p a n", a=2)
        live, clamped = qf[:, 0, :], qf[:, 1, :]
        onehot = qp[:, 0:2, :, :].rearrange("p b a (v c) -> p b a v c", c=HC)
        rows_cells = [adj_flat[:, BSEG * n:BSEG * n + BSEG].bitcast(F32) for n in range(4)] + [qf[:, 0, 0:BSEG]]
        RSTEP, SSTEP = ROW_CAP // 2, SLOTS // 2
        in_order = qf[:, 1, :]
        ps = ctx.enter_context(nc.psum_tensor("ps", [P, 8, 512], F32))
        A0 = 6
        O0 = 4

        s_w, s_setup, s_ready = sem("s_w"), sem("s_setup"), sem("s_ready")
        s_arrived, s_clearing, s_go, s_left = sem("s_arrived"), sem("s_clearing"), sem("s_go"), sem("s_left")
        s_empty, s_scat, s_placed, s_between, s_over, s_kept = (sem("s_" + n) for n in ("empty", "scat", "placed", "between", "over", "kept"))
        first_sem = sem("s_first")
        s_x, s_rstd, s_xn, s_tr, s_xnT, s_q, s_k, s_v = (sem("s_" + n) for n in ("x", "rstd", "xn", "tr", "xnT", "q", "k", "v"))
        s_adj = [sem("s_adj0"), sem("s_adj1")]
        s_mb, s_mtp = sem("s_mb"), sem("s_mtp")
        s_mT = [sem("s_mT0"), sem("s_mT1")]
        s_qf, s_kf, s_vt, s_qp, s_kp = sem("s_qf"), sem("s_kf"), sem("s_vt"), sem("s_qp"), sem("s_kp")
        s_qst = [sem(f"s_qst{n}") for n in range(4)]
        s_kst = [sem(f"s_kst{n}") for n in range(4)]
        s_sc, s_mx, s_m3, s_nmp, s_nm = sem("s_sc"), sem("s_mx"), sem("s_m3"), sem("s_nmp"), sem("s_nm")
        s_st, s_exp, s_pv, s_o, s_dve = sem("s_st"), sem("s_exp"), sem("s_pv"), sem("s_o"), sem("s_dve")
        s_num, s_den = sem("s_num"), sem("s_den")
        s_stage = sem("s_stage")
        s_edges, s_hot, s_counted, s_added = sem("s_edges"), sem("s_hot"), sem("s_counted"), sem("s_added")
        s_wo, s_x1, s_mv, s_xn2, s_tr2, s_xn2T, s_h, s_tab, s_out = (
            sem("s_" + n) for n in ("wo", "x1", "mv", "xn2", "tr2", "xn2T", "h", "tab", "out"))
        s_xbo = sem("s_xbo")
        last_sem = sem("s_last")
        assert last_sem.num - first_sem.num < 60
        block = ctx.enter_context(nc.Block())

        SORTS = [0, 20, 20, 14, 14, 12, 10, 0, 0]
        CHUNKS = [0, 0, 0, 5, 5, 4, 4, 9, 9]
        assert sum(CHUNKS) * HC == 2 * CL_CAP and sum(SORTS) == (2 * CL_CAP + SEG_CAP) // 4
        AFTER = {4: (5, 7, 9, 11), 5: (5, 7, 9, 11, 13), 9: (2, 4, 6, 8, 9, 11, 12, 14, 15)}
        WITH = {4: (2, 3, 4, 4), 5: (2, 3, 4, 4, 5), 9: (1, 2, 2, 3, 4, 4, 5, 6, 6)}
        HALVES = [3, 3, 3, 3, 2, 2, 0, 0]

        def next_batch(engine, i):
            engine.sem_inc(s_arrived, 1)
            engine.wait_ge(s_go, i + 1)
            engine.sem_inc(s_left, 1)

        def stages():
            first = 0
            for stage, batches in STAGES:
                yield stage, first, min(first + batches, B)
                first += batches
                if first >= B:
                    break

        @block.sync
        def _(sp):
            for dst, src in ((wq, d.wqT), (wk, d.wkT), (wv, d.wvT), (wo, d.woT)):
                sp.dma_start(dst[:, :, :], src.rearrange("(c p) n -> p c n", p=P)).then_inc(s_w, 16)
            sp.dma_start(wgat[:, :, :], d.wgat.rearrange("(c p) n -> p c n", p=P)).then_inc(s_w, 16)
            sp.dma_start(bv[:, :], d.bv.rearrange("(a n) -> a n", a=1).to_broadcast([P, D])).then_inc(s_w, 16)
            sp.dma_start(bo[:, :], d.bo.rearrange("(a n) -> a n", a=1).to_broadcast([P, D])).then_inc(s_w, 16)
            for n, b in enumerate((d.bq, d.bk)):
                for c in range(2):
                    sp.dma_start(bqk[:, n, c:c + 1], b[c * P:(c + 1) * P].rearrange("(p a) -> p a", a=1)).then_inc(s_w, 16)
            for n, a in enumerate((d.att_src, d.att_dst)):
                sp.dma_start(att[:, n, :], a.rearrange("h e -> (h e)").rearrange("(a n) -> a n", a=1)
                             .to_broadcast([P, GC])).then_inc(s_w, 16)
            sp.wait_ge(s_setup, 14)
            for n in range(NBSEG):
                sp.dma_start(d.cells.rearrange("(b c) a -> b (c a)", b=P)[:, n * BSEG:(n + 1) * BSEG], qf[:, 0, 0:BSEG]).then_inc(s_empty, 16)
            sp.wait_ge(s_empty, 16 * NBSEG)
            for stage, first, end in stages():
                with sp.Fori(first, end) as i:
                    sp.dma_start(xb[:, :, :], d.x[bass.ds(i, 1), :, :].rearrange("a (t p) n -> p (a t) n", p=P)).then_inc(s_x, 16)
                    for t in range(TN):
                        if t >= 2:
                            sp.wait_ge(s_mb, t - 1)
                        sp.dma_start(adjb[:, t % 2, :], d.adj[bass.ds(i, 1), t * P:(t + 1) * P, :].rearrange("a p n -> p (a n)"))\
                            .then_inc(s_adj[t % 2], 16)
                    sp.wait_ge(s_qp, 3)
                    for a in range(4):
                        rows = slice(32 * a, 32 * a + 32)
                        for dst, r, part in ((q1s, 0, 0), (q1s, 1, 0), (q1s, 2, 1), (q1s, 3, 1), (q2s, 0, 0), (q2s, 1, 2)):
                            sp.dma_start(dst[32 * r:32 * r + 32, :, :].rearrange("p (g a) n -> p a g n", a=4)[:, a, :, :],
                                         qp[rows, part, :, :]).then_inc(s_qst[a], 16)
                    sp.wait_ge(s_x1, TN)
                    sp.dma_start(d.x1[bass.ds(i, 1), :, :].rearrange("a (t p) n -> p (a t) n", p=P), x1[:, :, :]).then_inc(s_out, 16)
                    sp.wait_ge(s_xn2T, 2)
                    sp.dma_start(d.xnT[bass.ds(i, 1), :, :, :].rearrange("a p c n -> p (a c) n"), xnT[:, :, :]).then_inc(s_out, 16)
                    sp.wait_ge(s_tab, 1)
                    sp.dma_start(d.tab[bass.ds(i, 1), :, :].rearrange("a (t p) n -> p (a t) n", p=P), tab[:, :, :]).then_inc(s_out, 16)
                    sp.wait_ge(s_out, 48)
                    sp.wait_ge(s_arrived, i * 4 + 4)
                    sp.sem_inc(s_clearing, 1)
                    sp.sem_clear(range(first_sem.num, last_sem.num + 1))
                    sp.sem_inc(s_go, 1)
            sp.wait_ge(s_over, 1)
            sp.dma_start(d.slots, slots).then_inc(s_kept, 16)
            sp.dma_start(d.over, over[:, :]).then_inc(s_kept, 16)
            sp.dma_start(d.cnt, cnt[:, :]).then_inc(s_kept, 16)
            sp.wait_ge(s_kept, 48)

        @block.gpsimd
        def _(pool):
            def setup(n, ins):
                ins.then_inc(s_setup, 1)
                pool.wait_ge(s_setup, n)

            setup(1, pool.memset(ident[:, :], 0.0))
            setup(2, pool.memset(m3[:, :, :, :], 0.0))
            setup(3, pool.affine_select(out=ident[:, :], in_=ident[:, :], compare_op=ALU.not_equal, fill=1.0, base=0,
                                        pattern=[[-1, P]], channel_multiplier=1))
            setup(4, pool.memset(ones32[:, :], 1.0))
            setup(5, pool.memset(k2s[64:96, :, :], 1.0))
            setup(6, pool.memset(eps[:, :], LN_EPS))
            setup(7, pool.tensor_copy(ident16[:, :], ident[:, :]))
            setup(8, pool.iota(iota8[:, :, :], [[1, P], [0, HC]], base=0, channel_multiplier=0, allow_small_or_imprecise_dtypes=True))
            setup(9, pool.memset(cnt[:, :], 0.0))
            setup(10, pool.memset(left[:, :], 0.0))
            setup(11, pool.memset(dummy[:, :], 0.0))
            setup(12, pool.iota(heads[:, :], [[1, P]], base=0, channel_multiplier=P))
            setup(13, pool.iota(pcol[:, :], [[0, 1]], base=0, channel_multiplier=CELL, allow_small_or_imprecise_dtypes=True))
            setup(14, pool.memset(qf[:, 0, 0:BSEG], 0.0))
            pool.memset(tab[:, :, :], 0.0).then_inc(s_ready, 1)

            def scatter_keys(b):
                times = ROW_CAP // 16 // 3
                with pool.Fori(0, times) as k:
                    at = bass.ds((b * times + k) * 16, 16)
                    pool.tensor_copy(sidx[:, :], place[:, at]).then_inc(s_stage, 1)
                    pool.tensor_copy(skey[:, :], row[:, at]).then_inc(s_stage, 1)
                    pool.wait_ge(s_stage, k * 4 + 2)
                    pool.tensor_tensor(dummy[:, 1:2], dummy[:, 0:1], dummy[:, 0:1], ALU.add).then_inc(s_stage, 1)
                    for c in range(16):
                        pool.indirect_dma_start(d.cells, bass.IndirectOffsetOnAxis(ap=sidx[:, c:c + 1], axis=0), skey[:, c:c + 1], None,
                                                bounds_check=P * CELLS - 1, oob_is_err=False).then_inc(s_scat, 16)
                    pool.wait_ge(s_scat, (b * times + k) * 256 + 256)
                    pool.tensor_tensor(dummy[:, 2:3], dummy[:, 0:1], dummy[:, 0:1], ALU.add).then_inc(s_stage, 1)
                pool.wait_ge(s_stage, times * 4)

            for stage, first, end in stages():
                if stage == "cells":
                    pool.wait_ge(s_placed, 1)
                with pool.Fori(first, end) as i:
                    for t in range(TN):
                        pool.wait_ge(s_adj[t % 2], 16 * (t // 2) + 16)
                        pool.tensor_scalar(mb[:, t, :], adjb[:, t % 2, :], 0, MASKED, ALU.is_equal, ALU.mult).then_inc(s_mb, 1)
                    pool.wait_ge(s_kf, 2)
                    pool.tensor_copy(kp[:, 0, :, :], kf[:, :, :]).then_inc(s_kp, 1)
                    pool.wait_ge(s_kp, 1)
                    pool.tensor_tensor(kf[:, :, :], kf[:, :, :], kp[:, 0, :, :], ALU.subtract).then_inc(s_kp, 1)
                    pool.wait_ge(s_kp, 2)
                    pool.tensor_copy(kp[:, 1, :, :], kf[:, :, :]).then_inc(s_kp, 1)
                    pool.wait_ge(s_kp, 3)
                    pool.tensor_tensor(kp[:, 2, :, :], kf[:, :, :], kp[:, 1, :, :], ALU.subtract).then_inc(s_kp, 2)
                    pool.wait_ge(s_xn, TN)
                    pool.tensor_tensor(xb[:, :, :], xb[:, :, :], bo[:, None, :].to_broadcast([P, TN, D]), ALU.add).then_inc(s_xbo, 1)
                    pool.wait_ge(s_xbo, 1)
                    if stage == "cells":
                        scatter_keys(i - first)
                    next_batch(pool, i)

        @block.scalar
        def _(act):
            act.wait_ge(s_ready, 1)
            act.wait_ge(s_w, 16 * 13)
            for stage, first, end in stages():
                with act.Fori(first, end) as i:
                    act.wait_ge(s_mv, 1)
                    act.activation(rstd[:, :], mv[:, :, 1], ACT.Sqrt, bias=eps[:, 0:1]).then_inc(s_rstd, 1)
                    act.wait_ge(s_tr, TN)
                    act.activation(xnT[:, 0, :].rearrange("p (b n) -> p b n", b=2), ps[:, 0:2, :], ACT.Copy).then_inc(s_xnT, 1)
                    for g in range(2):
                        act.wait_ge(s_q, g + 1)
                        act.activation(qf[:, g, :].rearrange("p (b n) -> p b n", b=2), ps[:, 4 + 2 * g:6 + 2 * g, :],
                                       ACT.Identity, bias=bqk[:, 0, g:g + 1]).then_inc(s_qf, 1)
                    for g in range(2):
                        act.wait_ge(s_k, g + 1)
                        act.activation(kf[:, g, :].rearrange("p (b n) -> p b n", b=2), ps[:, 2 * g:2 * g + 2, :],
                                       ACT.Identity, bias=bqk[:, 1, g:g + 1]).then_inc(s_kf, 1)
                    for c in range(0, TN, 2):
                        act.wait_ge(s_mtp, c + 1)
                        act.activation(mT[:, c, :], ps[:, c % 2, :].bitcast(BF16), ACT.Copy).then_inc(s_mT[0], 1)
                    if stage == "segments":
                        act.wait_ge(s_mb, TN)
                        for n, t in enumerate((esrc, edst)):
                            act.dma_start(t, d.edges[n, :].rearrange("(p c) -> p c", p=P)[:, bass.ds((i - first) * (2 * SEG), 2 * SEG)])\
                                .then_inc(s_edges, 16)
                    if stage == "buckets":
                        act.wait_ge(s_mb, TN)
                        act.wait_ge(s_qp, 3)
                        for n in range(NBSEG):
                            act.dma_start(rows_cells[n], d.cells.rearrange("(b c) a -> b (c a)", b=P)[:, n * BSEG:(n + 1) * BSEG])\
                                .then_inc(s_edges, 16)
                    act.wait_ge(s_kp, 5)
                    for a in range(4):
                        rows = slice(32 * a, 32 * a + 32)
                        for dst, r, part in ((k1s, 0, 0), (k1s, 1, 1), (k1s, 2, 0), (k1s, 3, 1), (k2s, 0, 2), (k2s, 1, 0)):
                            act.dma_start(dst[32 * r:32 * r + 32, :, :].rearrange("p (g a) n -> p a g n", a=4)[:, a, :, :],
                                          kp[rows, part, :, :]).then_inc(s_kst[a], 16)
                    def take_numerators(j):
                        g, a = j // 4, j % 4
                        act.wait_ge(s_pv, (j + 1) * TN)
                        for nh in range(2):
                            act.activation(oT[32 * a:32 * a + 32, g, nh * 512:nh * 512 + 512], ps[64 * nh:64 * nh + 32, O0 + j % 2, :],
                                           ACT.Copy).then_inc(s_num, 1)

                    for j in range(H):
                        act.wait_ge(s_nmp, j + 1)
                        act.activation(q2s[64:96, j, :], ps[64:96, A0, :].bitcast(BF16), ACT.Copy).then_inc(s_nm, 1)
                        for c in range(TN):
                            n = j * TN + c
                            act.wait_ge(s_st, n + 1)
                            if n >= 2:
                                act.wait_ge(s_pv, n - 1)
                            act.activation(pt[:, n % 2, :].rearrange("p (b n) -> p b n", b=2),
                                           ps[:, 2 * (n % 2):2 * (n % 2) + 2, :], ACT.Exp).then_inc(s_exp, 1)
                            if j and c == 1:
                                take_numerators(j - 1)
                    take_numerators(H - 1)
                    act.wait_ge(s_mv, 2)
                    act.activation(rstd[:, :], mv[:, :, 1], ACT.Sqrt, bias=eps[:, 0:1]).then_inc(s_rstd, 1)
                    act.wait_ge(s_tr2, TN)
                    act.activation(xnT[:, 0, :].rearrange("p (b n) -> p b n", b=2), ps[:, 4:6, :], ACT.Copy).then_inc(s_xn2T, 1)
                    next_batch(act, i)

        @block.vector
        def _(dve):
            dve.wait_ge(s_ready, 1)
            dve.wait_ge(s_w, 16 * 13)
            link = Chain(dve, s_dve)

            def layernorm(src, scale_at):
                for t in range(TN):
                    last = dve.bn_stats(stats[:, t, :], src[:, t, :])
                link(last)
                for t in range(TN):
                    last = dve.bn_aggr(mv[:, t, :], stats[:, t, :])
                last.then_inc(s_mv, 1)
                dve.wait_ge(s_rstd, scale_at)
                link(dve.reciprocal(rstd[:, :], rstd[:, :]))

            between = Chain(dve, s_between)

            def note_left(link, values):
                link(dve.tensor_reduce(left[:, 1:2], values, AX_X, ALU.max))
                link(dve.tensor_tensor(left[:, 0:1], left[:, 0:1], left[:, 1:2], ALU.max))

            def place_keys():
                note_left(between, kept)
                bi = kp[:, 0, :, :].rearrange("p g n -> p (g n)").bitcast(I32)[:, 0:ROW_CAP]
                same, rank = (kp[:, n, :, :].rearrange("p g n -> p (g n)").bitcast(F32)[:, 0:ROW_CAP] for n in (1, 2))
                bucket, pos = qf[:, 0, 0:ROW_CAP + 1], qf[:, 1, 0:ROW_CAP]
                low = float(KEY_BIT >> 21)
                between(dve.tensor_scalar(bi, row.bitcast(I32), 21, None, ALU.logical_shift_right))
                between(dve.memset(bucket[:, 0:1], -1.0))
                between(dve.tensor_copy(bucket[:, 1:ROW_CAP + 1], bi))
                between(dve.tensor_tensor(same, bucket[:, 1:ROW_CAP + 1], bucket[:, 0:ROW_CAP], ALU.is_equal))
                between(dve.tensor_tensor_scan(rank, same, same, 0.0, ALU.mult, ALU.add))
                between(dve.tensor_scalar(same, bucket[:, 1:ROW_CAP + 1], low, None, ALU.is_ge))
                between(dve.tensor_tensor(pos, rank, same, ALU.mult))
                between(dve.tensor_scalar(pos, pos, float(CELL), None, ALU.is_ge))
                note_left(between, pos)
                between(dve.tensor_tensor(pos, pos, same, ALU.subtract))
                between(dve.tensor_scalar(pos, pos, FAR, FAR, ALU.mult, ALU.add))
                between(dve.tensor_scalar(bucket[:, 1:ROW_CAP + 1], bucket[:, 1:ROW_CAP + 1], low, 0.0, ALU.subtract, ALU.max))
                between(dve.tensor_scalar(bucket[:, 1:ROW_CAP + 1], bucket[:, 1:ROW_CAP + 1], float(CELLS), pcol[:, 0:1], ALU.mult, ALU.add))
                between(dve.tensor_tensor(rank, rank, bucket[:, 1:ROW_CAP + 1], ALU.add))
                between(dve.tensor_tensor(place, rank, pos, ALU.add))
                dve.sem_inc(s_placed, 1)

            between(dve.tensor_scalar(heads[:, :], heads[:, :], 14, KEY_BIT, ALU.logical_shift_left, ALU.bitwise_or))
            between(dve.tensor_scalar(heads[:, :], heads[:, :], LAST, None, ALU.bitwise_or))
            for stage, first, end in stages():
                if stage == "cells":
                    place_keys()
                if stage == "buckets":
                    between(dve.tensor_copy(merged[:, NBSEG * BSEG_CAP:MERGED], heads[:, :].bitcast(F32)))
                with dve.Fori(first, end) as i:
                    link.count = 0
                    dve.wait_ge(s_x, 16)
                    layernorm(xb, 1)
                    for t in range(TN):
                        dve.tensor_scalar(xn[:, t, :], xb[:, t, :], mv[:, t, 0:1], rstd[:, t:t + 1], ALU.subtract, ALU.mult)\
                            .then_inc(s_xn, 1)
                    dve.wait_ge(s_tr, TN)
                    dve.tensor_copy(xnT[:, 1, :].rearrange("p (b n) -> p b n", b=2), ps[:, 2:4, :]).then_inc(s_xnT, 1)
                    dve.wait_ge(s_qf, 2)
                    link(dve.tensor_scalar(qf[:, :, :], qf[:, :, :], SCALE, None, ALU.mult))
                    link(dve.tensor_copy(qp[:, 0, :, :], qf[:, :, :]))
                    link(dve.tensor_tensor(qf[:, :, :], qf[:, :, :], qp[:, 0, :, :], ALU.subtract))
                    link(dve.tensor_copy(qp[:, 1, :, :], qf[:, :, :]))
                    dve.tensor_tensor(qp[:, 2, :, :], qf[:, :, :], qp[:, 1, :, :], ALU.subtract).then_inc(s_qp, 3)
                    dve.wait_ge(s_v, 1)
                    dve.tensor_tensor(vt[:, :, :], ps[:, 4:8, :].rearrange("p b (c n) -> p (b c) n", c=2),
                                      bv[:, None, :].to_broadcast([P, TN, D]), ALU.add).then_inc(s_vt, 1)
                    for c in range(1, TN, 2):
                        dve.wait_ge(s_mtp, c + 1)
                        dve.tensor_copy(mT[:, c, :], ps[:, c % 2, :].bitcast(BF16)).then_inc(s_mT[1], 1)

                    def take_denominators(j):
                        g, a = j // 4, j % 4
                        dve.wait_ge(s_pv, (j + 1) * TN)
                        for nh in range(2):
                            dve.tensor_copy(den[32 * a:32 * a + 32, g, nh * 512:nh * 512 + 512],
                                            ps[64 * nh + 32:64 * nh + 64, O0 + j % 2, :]).then_inc(s_den, 1)

                    def normalise(g):
                        dve.wait_ge(s_den, 8 * g + 8)
                        link(dve.reciprocal(den[:, g, :], den[:, g, :]))
                        dve.wait_ge(s_num, 8 * g + 8)
                        dve.scalar_tensor_tensor(out=oT[:, g, :], in0=den[:, g, :], scalar=1.0e30, in1=oT[:, g, :],
                                                 op0=ALU.min, op1=ALU.mult).then_inc(s_o, 1)

                    def make_keys():
                        link(dve.tensor_scalar(clamped, esrc, float(LAST), None, ALU.is_ge))
                        link(dve.tensor_scalar(live, esrc, float(LAST), None, ALU.is_lt))
                        for t in (clamped, live):
                            link(dve.scalar_tensor_tensor(out=t, in0=edst, scalar=float(M), in1=t, op0=ALU.is_lt, op1=ALU.mult))
                        link(dve.scalar_tensor_tensor(out=clamped, in0=edst, scalar=1.0, in1=clamped, op0=ALU.add, op1=ALU.mult))
                        link(dve.tensor_scalar(edst, edst, M - 1, 14, ALU.bitwise_and, ALU.logical_shift_left))
                        link(dve.scalar_tensor_tensor(out=edst, in0=edst, scalar=KEY_BIT, in1=esrc, op0=ALU.bitwise_or, op1=ALU.bitwise_or))
                        link(dve.tensor_tensor(live, edst.bitcast(F32), live, ALU.mult))

                    def find(values, out, step):
                        at = out[:, 8 * (step // 2):8 * (step // 2) + 8]
                        link(dve.match_replace(values, at, values, 0.0) if step % 2 else dve.max(at, values))

                    def split_destinations(g):
                        at = slice(g * CL_CAP, (g + 1) * CL_CAP)
                        link(dve.tensor_scalar(high_int[:, at], found_cl[:, at], 1.0, None, ALU.subtract))
                        link(dve.tensor_scalar(low_int[:, at], high_int[:, at], P - 1, None, ALU.bitwise_and))
                        link(dve.tensor_scalar(high_int[:, at], high_int[:, at], 7, None, ALU.logical_shift_right))
                        link(dve.tensor_copy(parts[:, 0, at], low_int[:, at]))
                        link(dve.tensor_copy(parts[:, 1, at], high_int[:, at]))

                    def one_hots(j, k):
                        q = sum(CHUNKS[:j]) + k
                        if q >= 2:
                            dve.wait_ge(s_counted, q - 1)
                        else:
                            for n in range(4):
                                dve.wait_ge(s_qst[n], 96)
                        for a in range(2):
                            dve.tensor_tensor(onehot[:, q % 2, a, :, :], iota8[:, :, :],
                                              parts[:, a, None, q * HC:q * HC + HC].to_broadcast([P, P, HC]), ALU.is_equal).then_inc(s_hot, 1)

                    def add_counts(j):
                        dve.wait_ge(s_counted, sum(CHUNKS[:j + 1]))
                        dve.tensor_tensor(cnt[:, :], cnt[:, :], ps[:, O0 + j % 2, 0:P], ALU.add).then_inc(s_added, 1)
                        dve.wait_ge(s_added, j - 2)

                    def segment_step(j, n):
                        if n == 0 and j == 3:
                            split_destinations(0)
                        if n == 0 and j == 7:
                            split_destinations(1)
                            note_left(link, clamped)
                            note_left(link, live)
                            link(dve.tensor_copy(kept[:, bass.ds((i - first) * (2 * SEG_CAP), 2 * SEG_CAP)], found))
                        done, clamp_steps, live_steps = sum(SORTS[:j]), CL_CAP // 4, SEG_CAP // 4
                        for step in range(done + SORTS[j] * n // 16, done + SORTS[j] * (n + 1) // 16):
                            if step < clamp_steps:
                                find(clamped[:, 0:SEG], found_cl[:, 0:CL_CAP], step)
                            elif step < clamp_steps + live_steps:
                                find(live[:, SEG:2 * SEG], found[:, SEG_CAP:2 * SEG_CAP], step - clamp_steps)
                            else:
                                find(clamped[:, SEG:2 * SEG], found_cl[:, CL_CAP:2 * CL_CAP], step - clamp_steps - live_steps)
                        if CHUNKS[j] and n in AFTER[CHUNKS[j]]:
                            one_hots(j, AFTER[CHUNKS[j]].index(n))

                    def row_step(step):
                        if step < RSTEP // 4:
                            find(kept, in_order, step)

                    def bucket_step(step):
                        n = step // (BSEG_CAP // 4)
                        if n < NBSEG:
                            find(rows_cells[n], merged[:, n * BSEG_CAP:(n + 1) * BSEG_CAP], step % (BSEG_CAP // 4))

                    def slot_step(step):
                        if step < SSTEP // 4:
                            find(merged, in_order, step)

                    EVEN = {"rows": (row_step, 14, 10), "buckets": (bucket_step, 28, 22), "slots": (slot_step, 16, 12)}

                    def edges_before():
                        if stage == "segments":
                            dve.wait_ge(s_edges, 32)
                            make_keys()
                            for step in range(SEG_CAP // 4):
                                find(live[:, 0:SEG], found[:, 0:SEG_CAP], step)
                        elif stage in EVEN:
                            if stage == "buckets":
                                dve.wait_ge(s_edges, 16 * NBSEG)
                            for step in range(EVEN[stage][1]):
                                EVEN[stage][0](step)

                    def edges_within(j, n):
                        if stage == "segments":
                            segment_step(j, n)
                        elif stage in EVEN and j:
                            step, before, each = EVEN[stage]
                            for m in range(each * n // 16, each * (n + 1) // 16):
                                step(before + (j - 1) * each + m)

                    def edges_after():
                        if stage == "segments":
                            for k in range(CHUNKS[H]):
                                one_hots(H, k)
                            add_counts(H)
                        elif stage == "rows":
                            link(dve.tensor_copy(row[:, bass.ds((i - first) * RSTEP, RSTEP)], in_order[:, 0:RSTEP]))
                        elif stage == "buckets":
                            step, before, each = EVEN[stage]
                            for m in range(before + 7 * each, NBSEG * (BSEG_CAP // 4)):
                                step(m)
                            for values in rows_cells:
                                note_left(link, values)
                        elif stage == "slots":
                            link(dve.tensor_copy(slots[:, bass.ds((i - first) * SSTEP, SSTEP)], in_order[:, 0:SSTEP]))

                    def maxima(j):
                        for n in range(2 * TN):
                            t, mh = n // 2, n % 2
                            if n >= 4:
                                dve.wait_ge(s_mx, j * 2 * TN + n - 3)
                            dve.wait_ge(s_sc, j * 2 * TN + n + 1)
                            last = dve.tensor_tensor_reduce(out=junk[:, n % 4, :], in0=ps[:, A0 + n % 2, :], in1=mb[:, t, mh * 512:mh * 512 + 512],
                                                            scale=1.0, scalar=-3.0e38, op0=ALU.add, op1=ALU.max,
                                                            accum_out=mx[:, j % 2, t, mh:mh + 1])
                            last.then_inc(s_mx, 1)
                            if j >= 2 and n == 5:
                                take_denominators(j - 2)
                            if j == 6 and n == 12:
                                normalise(0)
                            edges_within(j, n)
                        dve.wait_ge(s_mx, (j + 1) * 2 * TN)
                        link(dve.tensor_tensor(mneg[:, :], mx[:, j % 2, :, 0], mx[:, j % 2, :, 1], ALU.max))
                        link(dve.tensor_scalar(mneg[:, :], mneg[:, :], NO_KEY, -1.0, ALU.max, ALU.mult))
                        part = [m3[:, j % 2, :, 64 + n] for n in range(3)]
                        link(dve.tensor_copy(part[0], mneg[:, :]))
                        link(dve.tensor_tensor(mrem[:, :], mneg[:, :], part[0], ALU.subtract))
                        link(dve.tensor_copy(part[1], mrem[:, :]))
                        dve.tensor_tensor(part[2], mrem[:, :], part[1], ALU.subtract).then_inc(s_m3, 1)
                        if stage == "segments" and CHUNKS[j]:
                            add_counts(j)

                    edges_before()
                    for j in range(H):
                        maxima(j)
                    take_denominators(H - 2)
                    edges_after()
                    take_denominators(H - 1)
                    normalise(1)
                    dve.wait_ge(s_xbo, 1)
                    for t in range(0, TN, 2):
                        dve.wait_ge(s_wo, t + 2)
                        dve.tensor_tensor(x1[:, t:t + 2, :], ps[:, t // 2, :].rearrange("p (a n) -> p a n", a=2), xb[:, t:t + 2, :],
                                          ALU.add).then_inc(s_x1, 2)
                    dve.wait_ge(s_x1, TN)
                    layernorm(x1, 2)
                    for t in range(TN):
                        dve.tensor_scalar(xn[:, t, :], x1[:, t, :], mv[:, t, 0:1], rstd[:, t:t + 1], ALU.subtract, ALU.mult)\
                            .then_inc(s_xn2, 1)
                    dve.wait_ge(s_tr2, TN)
                    dve.tensor_copy(xnT[:, 1, :].rearrange("p (b n) -> p b n", b=2), ps[:, 6:8, :]).then_inc(s_xn2T, 1)
                    dve.wait_ge(s_h, 1)
                    link(dve.tensor_copy(tab[:, :, 0:GC], ps[:, 0, 0:TN * GC].rearrange("p (t n) -> p t n", t=TN)))
                    for n in range(2):
                        link(dve.tensor_tensor(tmp16[:, :, :], tab[:, :, 0:GC], att[:, n, None, :].to_broadcast([P, TN, GC]), ALU.mult))
                        link(dve.tensor_reduce(tab[:, :, GC + 4 * n:GC + 4 * n + 4], tmp16[:, :, :].rearrange("p t (h e) -> p t h e", h=4),
                                                  AX_X, ALU.add))
                    dve.sem_inc(s_tab, 1)
                    next_batch(dve, i)
            note_left(between, merged)
            dve.tensor_scalar(over[:, :], left[:, 0:1], 0.0, None, ALU.is_gt).then_inc(s_over, 1)

        @block.tensor
        def _(pe):
            pe.wait_ge(s_ready, 1)
            pe.wait_ge(s_w, 16 * 13)
            for stage, first, end in stages():
                with pe.Fori(first, end) as i:
                    for t in range(TN):
                        pe.wait_ge(s_xn, t + 1)
                        for c in range(2):
                            last = pe.transpose(ps[:, 2 * c + t // 4, (t % 4) * P:(t % 4 + 1) * P], xn[:, t, c * P:(c + 1) * P], ident[:, :])
                        last.then_inc(s_tr, 1)
                    pe.wait_ge(s_xnT, 2)

                    def project(w, g, bank):
                        for nh in range(2):
                            for c in range(2):
                                last = pe.matmul(ps[:, bank + nh, :], w[:, c, g * P:(g + 1) * P], xnT[:, c, nh * 512:nh * 512 + 512],
                                                 start=c == 0, stop=c == 1)
                        return last

                    for g in range(2):
                        project(wq, g, 4 + 2 * g).then_inc(s_q, 1)
                    for g in range(2):
                        project(wk, g, 2 * g).then_inc(s_k, 1)
                    pe.wait_ge(s_qf, 2)
                    for t in range(TN):
                        for c in range(2):
                            last = pe.matmul(ps[:, 4 + t // 2, (t % 2) * D:(t % 2 + 1) * D], xnT[:, c, t * P:(t + 1) * P], wv[:, c, :],
                                             start=c == 0, stop=c == 1)
                    last.then_inc(s_v, 1)
                    pe.wait_ge(s_mb, TN)
                    pe.wait_ge(s_kf, 2)
                    for c in range(TN):
                        if c >= 2:
                            pe.wait_ge(s_mT[c % 2], c // 2)
                        for t in range(TN):
                            last = pe.transpose(ps[:, c % 2, :].bitcast(BF16)[:, t * P:(t + 1) * P], mb[:, t, c * P:(c + 1) * P], ident16[:, :])
                        last.then_inc(s_mtp, 1)
                    pe.wait_ge(s_vt, 1)

                    def score_half(j, n):
                        h, t, mh = j, n // 2, n % 2
                        if n == 0:
                            pe.wait_ge(s_qst[h % 4], 96)
                            pe.wait_ge(s_kst[h % 4], 96)
                            if j >= 1:
                                pe.wait_ge(s_nm, j)
                        if n >= 2:
                            pe.wait_ge(s_mx, j * 2 * TN + n - 1)
                        elif n == 1 and j >= 1:
                            pe.wait_ge(s_mx, j * 2 * TN)
                        pe.matmul(ps[:, A0 + n % 2, :], q1s[:, h, t * P:(t + 1) * P], k1s[:, h, mh * 512:mh * 512 + 512],
                                  start=True, stop=True).then_inc(s_sc, 1)

                    def maxima_rows(j):
                        pe.wait_ge(s_m3, j + 1)
                        for t in range(TN):
                            last = pe.transpose(ps[0:96, A0, :].bitcast(BF16)[:, t * P:(t + 1) * P], m3[:, j % 2, t, :], ident16[:, :])
                        last.then_inc(s_nmp, 1)

                    def shifted_scores(j, c):
                        h, n = j, j * TN + c
                        if n >= 2:
                            pe.wait_ge(s_exp, n - 1)
                        else:
                            pe.wait_ge(s_mT[0], 4)
                            pe.wait_ge(s_mT[1], 4)
                        if c == 0:
                            pe.wait_ge(s_nm, j + 1)
                        for lhs, rhs in ((k1s, q1s), (k2s, q2s)):
                            for nh in range(2):
                                pe.matmul(ps[:, 2 * (n % 2) + nh, :], lhs[:, h, c * P:(c + 1) * P], rhs[:, h, nh * 512:nh * 512 + 512],
                                          start=lhs is k1s, stop=False)
                        for nh in range(2):
                            last = pe.matmul(ps[:, 2 * (n % 2) + nh, :], ident16[:, :], mT[:, c, nh * 512:nh * 512 + 512],
                                             start=False, stop=True)
                        last.then_inc(s_st, 1)

                    def weighted_values(j, c):
                        h, n = j, j * TN + c
                        if stage == "segments" and c == 0 and CHUNKS[j]:
                            pe.wait_ge(s_added, j - 2)
                        if c == 0 and j >= 2:
                            pe.wait_ge(s_num, 2 * j - 2)
                            pe.wait_ge(s_den, 2 * j - 2)
                        pe.wait_ge(s_exp, n + 1)
                        for nh in range(2):
                            for r, lhs in enumerate((vt[:, c, 32 * h:32 * h + 32], ones32[:, :])):
                                at = 64 * nh + 32 * r
                                last = pe.matmul(ps[at:at + 32, O0 + j % 2, :], lhs, pt[:, n % 2, nh * 512:nh * 512 + 512],
                                                 start=c == 0, stop=c == TN - 1, tile_position=(0, at))
                        last.then_inc(s_pv, 1)

                    def count_edges(j, k):
                        q = sum(CHUNKS[:j]) + k
                        if k == 0:
                            pe.wait_ge(s_num, 2 * j - 2)
                            pe.wait_ge(s_den, 2 * j - 2)
                        pe.wait_ge(s_hot, 2 * q + 2)
                        for c in range(HC):
                            last = pe.matmul(ps[:, O0 + j % 2, 0:P], onehot[:, q % 2, 0, :, c], onehot[:, q % 2, 1, :, c],
                                             start=k == 0 and c == 0, stop=k == CHUNKS[j] - 1 and c == HC - 1)
                        last.then_inc(s_counted, 1)

                    for n in range(2 * TN):
                        score_half(0, n)
                    maxima_rows(0)
                    for j in range(H):
                        for c in range(TN):
                            shifted_scores(j, c)
                            if c == 0 and j:
                                weighted_values(j - 1, TN - 1)
                            if j + 1 < H:
                                for n in range(sum(HALVES[:c]), sum(HALVES[:c + 1])):
                                    score_half(j + 1, n)
                            if stage == "segments" and CHUNKS[j + 1]:
                                for k in range(CHUNKS[j + 1]):
                                    if WITH[CHUNKS[j + 1]][k] == c:
                                        count_edges(j + 1, k)
                            if c:
                                weighted_values(j, c - 1)
                        if j + 1 < H:
                            maxima_rows(j + 1)
                    weighted_values(H - 1, TN - 1)
                    pe.wait_ge(s_exp, H * TN)
                    pe.wait_ge(s_o, 2)
                    for t in range(TN):
                        for g in range(2):
                            last = pe.matmul(ps[:, t // 2, (t % 2) * D:(t % 2 + 1) * D], oT[:, g, t * P:(t + 1) * P], wo[:, g, :],
                                             start=g == 0, stop=g == 1)
                        last.then_inc(s_wo, 1)
                    for t in range(TN):
                        pe.wait_ge(s_xn2, t + 1)
                        for c in range(2):
                            last = pe.transpose(ps[:, 4 + 2 * c + t // 4, (t % 4) * P:(t % 4 + 1) * P], xn[:, t, c * P:(c + 1) * P], ident[:, :])
                        last.then_inc(s_tr2, 1)
                    pe.wait_ge(s_xn2T, 2)
                    pe.wait_ge(s_x1, TN)
                    for t in range(TN):
                        for c in range(2):
                            last = pe.matmul(ps[:, 0, t * GC:(t + 1) * GC], xnT[:, c, t * P:(t + 1) * P], wgat[:, c, :],
                                             start=c == 0, stop=c == 1)
                    last.then_inc(s_h, 1)
                    next_batch(pe, i)


F = 2 * D
NE = 4
FT = F // P
CHUNK = 512
CT = CHUNK // P
BODY = 2 * NE
EARLY = 8


class Experts:

    def __init__(self, nc, ctx, name):
        def sb(n, shape):
            return ctx.enter_context(nc.sbuf_tensor(name + n, shape, F32))

        self.w1, self.w2 = sb("w1", [P, NE, 2, F]), sb("w2", [P, NE, FT, D])
        self.b1, self.b2 = sb("b1", [P, NE, FT]), sb("b2", [P, NE, D])
        self.xT = sb("xT", [P, 2, 2, CHUNK])
        self.hid = sb("hid", [P, 2, FT, CHUNK])
        self.ps = ctx.enter_context(nc.psum_tensor(name + "ps", [P, 8, 512], F32))
        self.s_w, self.s_up, self.s_act, self.s_down, self.s_y = (
            ctx.enter_context(nc.semaphore(name + n)) for n in ("s_w", "s_up", "s_act", "s_down", "s_y"))
        self.s_in = [ctx.enter_context(nc.semaphore(name + n)) for n in ("s_in0", "s_in1")]
        self.LOADED = 16 * (3 + NE * FT)

    def load(self, sp, d):
        sp.dma_start(self.w1[:, :, :, :], d.w1.rearrange("e (c p) f -> p e c f", p=P)).then_inc(self.s_w, 16)
        sp.dma_start(self.w2[:, :, :, :], d.w2.rearrange("e (c p) n -> p e c n", p=P)).then_inc(self.s_w, 16)
        sp.dma_start(self.b2[:, :, :].rearrange("p e n -> p (e n)"),
                     d.b2.rearrange("e n -> (e n)").rearrange("(a n) -> a n", a=1).to_broadcast([P, NE * D])).then_inc(self.s_w, 16)
        for e in range(NE):
            for f in range(FT):
                sp.dma_start(self.b1[:, e, f:f + 1], d.b1[e, f * P:(f + 1) * P].rearrange("(p a) -> p a", a=1)).then_inc(self.s_w, 16)

    def load_nodes(self, sp, graphs, i, h):
        sp.wait_ge(self.s_up, i * (BODY * FT) + (h + 1) * NE * FT)
        at = slice(i, i + 1) if isinstance(i, int) else bass.ds(i, 1)
        sp.dma_start(self.xT[:, h, :, :], graphs[at, :, :, h * CHUNK:(h + 1) * CHUNK].rearrange("a p c n -> p (a c) n"))\
            .then_inc(self.s_in[h], 16)

    def begin(self, dve, cells):
        dve.memset(cells[:, 0:1], 0.0).then_inc(self.s_up, BODY * FT)
        dve.memset(cells[:, 1:2], 0.0).then_inc(self.s_y, 2)
        dve.memset(cells[:, 2:3], 0.0).then_inc(self.s_down, 2)
        dve.memset(cells[:, 3:4], 0.0).then_inc(self.s_act, 4)

    def activate(self, act, i, n):
        act.wait_ge(self.s_down, i * BODY + n + 1)
        for f in range(FT):
            act.wait_ge(self.s_up, (i * BODY + n) * FT + BODY * FT + f + 1)
            act.activation(self.hid[:, n % 2, f, :], self.ps[:, f, :], ACT.Gelu, bias=self.b1[:, n % NE, f:f + 1]).then_inc(self.s_act, 1)

    def up(self, pe, i, n):
        h, e = n // NE, n % NE
        if e == 0:
            pe.wait_ge(self.s_in[h], i * 16 + 16)
        for f in range(FT):
            pe.wait_ge(self.s_act, (i * BODY + n) * FT + f + 1)
            for c in range(2):
                last = pe.matmul(self.ps[:, f, :], self.w1[:, e, c, f * P:(f + 1) * P], self.xT[:, h, c, :], start=c == 0, stop=c == 1)
            last.then_inc(self.s_up, 1)

    def down(self, pe, i, n):
        e, at = n % NE, 4 + 2 * (n % 2)
        pe.wait_ge(self.s_act, (i * BODY + n) * FT + FT + 4)
        pe.wait_ge(self.s_y, i * BODY + n + 1)
        for t in range(CT):
            for f in range(FT):
                last = pe.matmul(self.ps[:, at + t // 2, (t % 2) * D:(t % 2 + 1) * D], self.hid[:, n % 2, f, t * P:(t + 1) * P],
                                 self.w2[:, e, f, :], start=f == 0, stop=f == FT - 1)
        last.then_inc(self.s_down, 1)

    def graph(self, pe, i):
        self.up(pe, i, 0)
        for n in range(BODY):
            if n + 1 < BODY:
                self.up(pe, i, n + 1)
            self.down(pe, i, n)

    def take(self, dve, y, i, n):
        at = 4 + 2 * (n % 2)
        dve.wait_ge(self.s_down, i * BODY + n + 3)
        return dve.tensor_tensor(y, self.ps[:, at:at + 2, :].rearrange("p b (c n) -> p (b c) n", c=2),
                                 self.b2[:, None, n % NE, :].to_broadcast([P, CT, D]), ALU.add)


def message_phase(nc, d):
    with ExitStack() as ctx:
        class Slots:
            pass

        m = Slots()
        m.head = ctx.enter_context(nc.sbuf_tensor("m_head", [P, SLOTS], F32))
        m.same = ctx.enter_context(nc.sbuf_tensor("m_same", [P, SLOTS], F32))
        m.pen = ctx.enter_context(nc.sbuf_tensor("m_pen", [P, 2, SLOTS], F32))
        m.lowT = ctx.enter_context(nc.sbuf_tensor("m_lowT", [P, KT, P], F32))
        m.G = ctx.enter_context(nc.sbuf_tensor("m_G", [P, SLOTS, 24], F32))
        m.iota = ctx.enter_context(nc.sbuf_tensor("m_iota", [P, P], F32))
        m.ident = ctx.enter_context(nc.sbuf_tensor("m_ident", [P, P], F32))
        gather_rows(nc, d, m)
        sum_messages(nc, d, m)


def gather_rows(nc, d, m):
    with ExitStack() as ctx:
        def sb(name, shape, dt=F32):
            return ctx.enter_context(nc.sbuf_tensor(name, shape, dt))

        def sem(name):
            return ctx.enter_context(nc.semaphore(name))

        head, same, pen, lowT, G, iota, ident = m.head, m.same, m.pen, m.lowT, m.G, m.iota, m.ident
        x = Experts(nc, ctx, "early_")
        y = sb("m_y", [P, 2, CT, D])
        slots = sb("m_slots", [P, SLOTS])
        ki = sb("m_ki", [P, SLOTS], I32)
        dsti = sb("m_dsti", [P, SLOTS], I32)
        live = sb("m_live", [P, SLOTS])
        dst = sb("m_dst", [P, SLOTS + 2])
        low = sb("m_low", [P, SLOTS])
        idx = sb("m_idx", [P, SLOTS])
        idxT = sb("m_idxT", [P, KT, P], I32)
        sidx = sb("m_sidx", [P, 2, 16], I32)
        stage = sb("m_stage", [P, 2, 16, ROW])
        dummy, dummy2, zeros = sb("m_dummy", [P, 3]), sb("m_dummy2", [P, 8]), sb("m_zeros", [P, 8])
        ps = x.ps
        s_in, s_setup, s_v, s_idx, s_tr, s_stage, s_copied = (
            sem("m_s_" + n) for n in ("in", "setup", "v", "idx", "tr", "stage", "copied"))
        s_g = [sem("m_s_g0"), sem("m_s_g1")]
        s_stored = [sem("m_s_st0"), sem("m_s_st1")]
        block = ctx.enter_context(nc.Block())
        HALVES = SLOTS // 16 // EARLY
        COPY_AFTER = (1, 2, 3, 5, 6, 7)
        assert len(COPY_AFTER) == HALVES

        @block.sync
        def _(sp):
            sp.dma_start(slots[:, :], d.slots).then_inc(s_in, 16)
            x.load(sp, d)
            sp.wait_ge(s_setup, 5)
            for b in range(2):
                sp.dma_start(d.scrap[:, b * 8:b * 8 + 8], zeros[:, :]).then_inc(s_stored[b], 16)
            for h in range(2):
                x.load_nodes(sp, d.xnT, 0, h)
            with sp.Fori(0, EARLY) as i:
                for h in range(2):
                    for n in range(h * NE, h * NE + NE):
                        sp.wait_ge(x.s_y, i * BODY + n + 3)
                        sp.dma_start(d.early[bass.ds(i, 1), h, :, n % NE, :, :].rearrange("a p t c -> p (a t) c"), y[:, n % 2, :, :])\
                            .then_inc(s_stored[n % 2], 16)
                    x.load_nodes(sp, d.xnT, i + 1, h)
            for h in range(2):
                sp.wait_ge(x.s_in[h], 16 * (EARLY + 1))
            for b in range(2):
                sp.wait_ge(s_stored[b], 16 * (EARLY * NE + 1))

        @block.gpsimd
        def _(pool):
            def setup(n, ins):
                ins.then_inc(s_setup, 1)
                pool.wait_ge(s_setup, n)
            setup(1, pool.iota(iota[:, :], [[1, P]], base=0, channel_multiplier=0, allow_small_or_imprecise_dtypes=True))
            setup(2, pool.memset(ident[:, :], 0.0))
            setup(3, pool.affine_select(out=ident[:, :], in_=ident[:, :], compare_op=ALU.not_equal, fill=1.0, base=0,
                                        pattern=[[-1, P]], channel_multiplier=1))
            setup(4, pool.memset(dummy[:, :], 0.0))
            setup(5, pool.memset(zeros[:, :], 0.0))
            pool.wait_ge(s_idx, 3)
            table = d.tab.rearrange("b n c -> (b n) c")
            idx_flat = idxT[:, :, :].rearrange("p k b -> p (k b)")
            with pool.Fori(0, SLOTS // 32) as i:
                for b in range(2):
                    pool.wait_ge(s_copied, i * 2 + b + 1)
                    pool.tensor_copy(sidx[:, b, :], idx_flat[:, bass.ds(i * 32 + b * 16, 16)]).then_inc(s_stage, 1)
                    pool.wait_ge(s_stage, i * 4 + 2 * b + 1)
                    pool.tensor_tensor(dummy[:, 1 + b:2 + b], dummy[:, 0:1], dummy[:, 0:1], ALU.add).then_inc(s_stage, 1)
                    for c in range(16):
                        pool.indirect_dma_start(stage[:, b, c, :], None, table, bass.IndirectOffsetOnAxis(ap=sidx[:, b, c:c + 1], axis=0),
                                                bounds_check=LAST, oob_is_err=False).then_inc(s_g[b], 16)

        @block.scalar
        def _(act):
            act.wait_ge(x.s_w, x.LOADED)
            with act.Fori(0, EARLY) as i:
                for n in range(BODY):
                    x.activate(act, i, n)
                    if n in COPY_AFTER:
                        half = COPY_AFTER.index(n)
                        act.wait_ge(s_g[half % 2], i * (128 * HALVES) + (half // 2 * 256 + 256))
                        act.activation(G[:, bass.ds(i * (16 * HALVES) + half * 16, 16), :], stage[:, half % 2, :, 0:24], ACT.Copy)\
                            .then_inc(s_copied, 1)

        @block.tensor
        def _(pe):
            pe.wait_ge(s_setup, 4)
            pe.wait_ge(s_idx, 2)
            for n, t in enumerate((idx, low)):
                for k in range(KT):
                    last = pe.transpose(ps[:, 2 * n + k // 4, (k % 4) * P:(k % 4 + 1) * P], t[:, k * P:(k + 1) * P], ident[:, :])
                last.then_inc(s_tr, 1)
            pe.wait_ge(s_idx, 3)
            pe.wait_ge(x.s_w, x.LOADED)
            with pe.Fori(0, EARLY) as i:
                x.graph(pe, i)

        @block.vector
        def _(dve):
            link = Chain(dve, s_v)
            dve.wait_ge(s_setup, 4)
            dve.wait_ge(s_in, 16)
            link(dve.memset(dst[:, :], -2.0))
            link(dve.tensor_scalar(ki[:, :], slots[:, :].bitcast(I32), LAST, None, ALU.bitwise_and))
            link(dve.tensor_scalar(head[:, :], ki[:, :], float(LAST), None, ALU.is_equal))
            link(dve.tensor_scalar(dsti[:, :], slots[:, :].bitcast(I32), 14, LAST, ALU.logical_shift_right, ALU.bitwise_and))
            link(dve.tensor_scalar(live[:, :], slots[:, :], 0.0, None, ALU.is_gt))
            link(dve.scalar_tensor_tensor(out=idx[:, :], in0=dsti[:, :], scalar=-float(LAST), in1=head[:, :], op0=ALU.add, op1=ALU.mult))
            link(dve.tensor_tensor(idx[:, :], idx[:, :], ki[:, :], ALU.add))
            link(dve.scalar_tensor_tensor(out=dst[:, 1:SLOTS + 1], in0=dsti[:, :], scalar=1.0, in1=live[:, :], op0=ALU.add, op1=ALU.mult))
            link(dve.tensor_scalar(dst[:, 1:SLOTS + 1], dst[:, 1:SLOTS + 1], 1.0, None, ALU.subtract))
            link(dve.tensor_scalar(dsti[:, :], dsti[:, :], P - 1, None, ALU.bitwise_and))
            link(dve.tensor_scalar(low[:, :], live[:, :], -512.0, 512.0, ALU.mult, ALU.add))
            link(dve.tensor_tensor(low[:, :], low[:, :], dsti[:, :], ALU.add))
            link(dve.tensor_tensor(same[:, :], dst[:, 1:SLOTS + 1], dst[:, 0:SLOTS], ALU.is_equal))
            link(dve.tensor_scalar(pen[:, 0, :], same[:, :], 1.0, -MASKED, ALU.subtract, ALU.mult))
            link(dve.tensor_tensor(pen[:, 1, :], dst[:, 1:SLOTS + 1], dst[:, 2:SLOTS + 2], ALU.is_equal))
            link(dve.tensor_scalar(pen[:, 1, :], pen[:, 1, :], 1.0, -MASKED, ALU.subtract, ALU.mult))
            dve.memset(dummy2[:, 0:1], 0.0).then_inc(s_copied, 2)
            dve.memset(dummy2[:, 1:2], 0.0).then_inc(s_idx, 2)
            dve.wait_ge(s_tr, 2)
            psk = ps[:, 0:4, :].rearrange("p (n b) m -> p n (b m)", n=2)
            link(dve.tensor_copy(idxT[:, :, :].rearrange("p k b -> p (k b)"), psk[:, 0, 0:SLOTS]))
            link(dve.tensor_copy(lowT[:, :, :].rearrange("p k b -> p (k b)"), psk[:, 1, 0:SLOTS]))
            dve.memset(dummy2[:, 2:3], 0.0).then_inc(s_idx, 1)
            x.begin(dve, dummy2[:, 4:8])
            dve.wait_ge(x.s_w, x.LOADED)
            with dve.Fori(0, EARLY) as i:
                for n in range(BODY):
                    dve.wait_ge(s_stored[n % 2], i * (16 * NE) + (n // 2 * 16 + 16))
                    x.take(dve, y[:, n % 2, :, :], i, n).then_inc(x.s_y, 1)


def sum_messages(nc, d, m):
    with ExitStack() as ctx:
        def sb(name, shape, dt=F32):
            return ctx.enter_context(nc.sbuf_tensor(name, shape, dt))

        def sem(name):
            return ctx.enter_context(nc.semaphore(name))

        head, same, pen, lowT, G, iota, ident = m.head, m.same, m.pen, m.lowT, m.G, m.iota, m.ident
        s, dd = sb("m_s", [P, 4, SLOTS]), sb("m_d", [P, 4, SLOTS])
        f, r = sb("m_f", [P, 4, SLOTS]), sb("m_r", [P, 4, SLOTS])
        hot = sb("m_hot", [P, 2, KT, P])
        rows = sb("m_rows", [P, P, ROW])
        crow = sb("m_crow", [P, ROW])
        cnt = sb("m_cnt", [P, P])
        A = sb("m_A", [P, P, 24])
        dummy2 = sb("m_dummy3", [P, 8])
        ps = ctx.enter_context(nc.psum_tensor("m_ps", [P, 8, 512], F32))
        s_in, s_v, s_sd, s_back, s_bk, s_hot, s_used, s_pre, s_exp, s_w, s_done, s_out = (
            sem("n_s_" + n) for n in ("in", "v", "sd", "back", "bk", "hot", "used", "pre", "exp", "w", "done", "out"))
        block = ctx.enter_context(nc.Block())

        @block.sync
        def _(sp):
            sp.dma_start(cnt[:, :], d.cnt).then_inc(s_in, 16)
            sp.dma_start(rows[:, :, :], d.tab.rearrange("b n c -> (b n) c").rearrange("(t p) c -> p t c", p=P)).then_inc(s_in, 16)
            sp.dma_start(crow[:, :], d.tab.rearrange("b n c -> (b n) c")[LAST:LAST + 1, :].to_broadcast([P, ROW])).then_inc(s_in, 16)
            sp.wait_ge(s_done, 1)
            sp.dma_start(d.sums, A[:, :, 0:20]).then_inc(s_out, 16)
            sp.wait_ge(s_out, 16)

        @block.scalar
        def _(act):
            act.wait_ge(s_pre, 1)
            act.activation(s[:, :, :], s[:, :, :], ACT.Exp).then_inc(s_exp, 1)
            act.wait_ge(s_pre, 2)
            act.activation(A[:, :, 20:24], A[:, :, 20:24], ACT.Exp).then_inc(s_exp, 1)
            act.activation(rows[:, :, 20:24], rows[:, :, 20:24], ACT.Exp).then_inc(s_exp, 1)

        @block.tensor
        def _(pe):
            for k in range(KT):
                for n in range(2):
                    if 2 * k + n >= 8:
                        pe.wait_ge(s_sd, 2 * k + n - 7)
                    for hd in range(4):
                        last = pe.transpose(ps[:, (2 * k + n) % 8, hd * P:(hd + 1) * P], G[:, k * P:(k + 1) * P, 16 + 4 * n + hd], ident[:, :])
                    last.then_inc(s_back, 1)
            pe.wait_ge(s_w, 1)
            for k in range(KT):
                for n, t in enumerate((s, f)):
                    if 2 * k + n >= 8:
                        pe.wait_ge(s_bk, 2 * k + n - 7)
                    for hd in range(4):
                        last = pe.transpose(ps[:, (2 * k + n) % 8, hd * P:(hd + 1) * P], t[:, hd, k * P:(k + 1) * P], ident[:, :])
                    last.then_inc(s_back, 1)
            pe.wait_ge(s_w, 2)
            sums = ps[:, :, :].rearrange("p b (c n) -> p (b c) n", n=32)
            with pe.Fori(0, P // 2) as i:
                for b in range(2):
                    pe.wait_ge(s_hot, i * 2 + b + 1)
                    for k in range(KT):
                        last = pe.matmul(sums[:, bass.ds(i * 2 + b, 1), 0:24].rearrange("p a n -> p (a n)"), hot[:, b, k, :],
                                         G[:, bass.ds(i * 2 + (b + k * P), 1), :].rearrange("p a n -> p (a n)"), start=k == 0, stop=k == KT - 1)
                    last.then_inc(s_used, 1)

        @block.vector
        def _(dve):
            link = Chain(dve, s_v)
            dve.memset(dummy2[:, 6:7], 0.0).then_inc(s_used, 2)
            dve.wait_ge(s_in, 48)
            for k in range(KT):
                for n, t in enumerate((s, dd)):
                    dve.wait_ge(s_back, 2 * k + n + 1)
                    dve.tensor_copy(t[:, :, k * P:(k + 1) * P], ps[:, (2 * k + n) % 8, :].rearrange("p (h b) -> p h b", h=4)).then_inc(s_sd, 1)
            dve.wait_ge(s_sd, 2 * KT)
            link(dve.tensor_tensor(dd[:, :, :], dd[:, :, :], head[:, None, :].to_broadcast([P, 4, SLOTS]), ALU.mult))
            for hd in range(4):
                dve.tensor_tensor_scan(r[:, hd, :], same[:, :], dd[:, hd, :], 0.0, ALU.mult, ALU.add)
                last = dve.tensor_tensor_scan(f[:, hd, :], pen[:, 0, :], s[:, hd, :], MASKED, ALU.add, ALU.max)
            link(last)
            for hd in range(4):
                last = dve.tensor_tensor_scan(dd[:, hd, ::-1], pen[:, 1, ::-1], f[:, hd, ::-1], MASKED, ALU.add, ALU.max)
            link(last)
            link(dve.tensor_copy(f[:, :, :], dd[:, :, :]))
            link(dve.tensor_tensor(s[:, :, :], s[:, :, :], r[:, :, :], ALU.add))
            link(dve.tensor_tensor(r[:, :, :], r[:, :, :], f[:, :, :], ALU.add))
            link(dve.scalar_tensor_tensor(out=s[:, :, :], in0=s[:, :, :], scalar=LEAK, in1=s[:, :, :], op0=ALU.mult, op1=ALU.max))
            link(dve.scalar_tensor_tensor(out=r[:, :, :], in0=r[:, :, :], scalar=LEAK, in1=r[:, :, :], op0=ALU.mult, op1=ALU.max))
            dve.tensor_tensor(s[:, :, :], s[:, :, :], r[:, :, :], ALU.subtract).then_inc(s_pre, 1)
            link(dve.tensor_tensor(f[:, :, :], f[:, :, :], head[:, None, :].to_broadcast([P, 4, SLOTS]), ALU.mult))
            dve.wait_ge(s_exp, 1)
            dve.memset(dummy2[:, 3:4], 0.0).then_inc(s_w, 1)
            for k in range(KT):
                for n in range(2):
                    dve.wait_ge(s_back, 2 * KT + 2 * k + n + 1)
                    dve.tensor_copy(G[:, k * P:(k + 1) * P, 16 + 4 * n:20 + 4 * n],
                                    ps[:, (2 * k + n) % 8, :].rearrange("p (h b) -> p b h", h=4)).then_inc(s_bk, 1)
            dve.wait_ge(s_bk, 2 * KT)
            dve.tensor_tensor(G[:, :, 0:16].rearrange("p t (h e) -> p t h e", h=4), G[:, :, 0:16].rearrange("p t (h e) -> p t h e", h=4),
                              G[:, :, 16:20][:, :, :, None].to_broadcast([P, SLOTS, 4, 4]), ALU.mult).then_inc(s_w, 1)
            with dve.Fori(0, P // 2) as i:
                for b in range(2):
                    dve.wait_ge(s_used, i * 2 + b + 1)
                    dve.tensor_tensor(hot[:, b, :, :], iota[:, None, :].to_broadcast([P, KT, P]),
                                      lowT[:, :, bass.ds(i * 2 + b, 1)].to_broadcast([P, KT, P]), ALU.is_equal).then_inc(s_hot, 1)
            dve.wait_ge(s_used, P + 2)
            for b in range(8):
                last = dve.tensor_copy(A[:, 16 * b:16 * b + 16, :], ps[:, b, :].rearrange("p (c n) -> p c n", n=32)[:, :, 0:24])
            link(last)
            def wide(x):
                return x.to_broadcast([P, P, 4])
            m, l, ad = A[:, :, 20:24], A[:, :, 16:20], rows[:, :, 20:24]
            en, ec = rows[:, :, 0:4], rows[:, :, 4:8]
            cs = crow[:, None, 16:20].to_broadcast([P, P, 4])
            link(dve.tensor_scalar(rows[:, :, 8:9], cnt[:, :, None], 0.0, MASKED, ALU.is_le, ALU.mult))
            link(dve.tensor_tensor(en, cs, wide(rows[:, :, 8:9]), ALU.add))
            link(dve.tensor_tensor(en, en, m, ALU.max))
            link(dve.tensor_tensor(en, en, ad, ALU.add))
            link(dve.tensor_tensor(m, m, ad, ALU.add))
            link(dve.tensor_tensor(ec, cs, ad, ALU.add))
            for x in (en, m, ec):
                link(dve.scalar_tensor_tensor(out=x, in0=x, scalar=LEAK, in1=x, op0=ALU.mult, op1=ALU.max))
            link(dve.tensor_tensor(m, m, en, ALU.subtract))
            link(dve.tensor_tensor(ec, ec, en, ALU.subtract))
            link(dve.tensor_scalar(ad, ec, 0.0, None, ALU.min))
            dve.memset(dummy2[:, 4:5], 0.0).then_inc(s_pre, 1)
            dve.wait_ge(s_exp, 3)
            link(dve.tensor_tensor(ad, ad, wide(cnt[:, :, None]), ALU.mult))
            link(dve.tensor_tensor(l, l, m, ALU.mult))
            link(dve.tensor_tensor(l, l, ad, ALU.add))
            for hd in range(4):
                acc = A[:, :, 4 * hd:4 * hd + 4]
                link(dve.tensor_tensor(acc, acc, wide(m[:, :, hd:hd + 1]), ALU.mult))
                link(dve.tensor_tensor(en, crow[:, None, 4 * hd:4 * hd + 4].to_broadcast([P, P, 4]), wide(ad[:, :, hd:hd + 1]), ALU.mult))
                link(dve.tensor_tensor(acc, acc, en, ALU.add))
            dve.memset(dummy2[:, 5:6], 0.0).then_inc(s_done, 1)


DEAD = 20000.0


def general_phase(nc, d, edges=E):
    with ExitStack() as ctx:
        def sb(name, shape, dt=F32):
            return ctx.enter_context(nc.sbuf_tensor(name, shape, dt))

        def sem(name):
            return ctx.enter_context(nc.semaphore(name))

        over, flag = sb("g_over", [P, 1]), sb("g_flag", [P, 1], I32)
        ident, low = sb("g_ident", [P, P]), sb("g_low", [P, P])
        cnt = sb("g_cnt", [P, P])
        crow = sb("g_crow", [P, ROW])
        rows = sb("g_rows", [P, P, ROW])
        state = sb("g_state", [P, P, ROW])
        e3 = sb("g_e3", [P, P, 12])
        esrc, edst = sb("g_esrc", [P, 1], I32), sb("g_edst", [P, 1], I32)
        keep, dst = sb("g_keep", [P, 1]), sb("g_dst", [P, 1])
        si, di, oi = sb("g_si", [P, 1], I32), sb("g_di", [P, 1], I32), sb("g_oi", [P, 1], I32)
        dup = sb("g_dup", [P, 1])
        g, old, new = sb("g_g", [P, ROW]), sb("g_old", [P, ROW]), sb("g_new", [P, ROW])
        eq, pen, t1 = sb("g_eq", [P, P]), sb("g_pen", [P, P]), sb("g_t1", [P, P])
        sm = sb("g_sm", [P, 4, P])
        x = sb("g_x", [P, 12])
        y = sb("g_y", [P, 8])
        v = sb("g_v", [P, 20])
        dummy = sb("g_dummy", [P, 8])
        ps = ctx.enter_context(nc.psum_tensor("g_ps", [P, 3, 512], F32))
        s_in, s_setup, s_flag, s_v, s_pre, s_exp, s_init, s_stored = (
            sem("g_s_" + n) for n in ("in", "setup", "flag", "v", "pre", "exp", "init", "stored"))
        s_e, s_next, s_idx, s_g, s_row, s_vv, s_sum, s_new, s_xx, s_yy, s_pool = (
            sem("g_s_" + n) for n in ("e", "next", "idx", "g", "row", "vv", "sum", "new", "xx", "yy", "pool"))
        s_back, s_sums, s_out = sem("g_s_back"), sem("g_s_sums"), sem("g_s_out")
        block = ctx.enter_context(nc.Block())
        TILES = edges // P
        table = d.tab.rearrange("b n c -> (b n) c")

        def by_tile(t):
            return t.rearrange("(t p) c -> p t c", p=P)

        def column(n, i):
            return d.edges[n, bass.ds(i * P, P)].rearrange("(p a) -> p a", a=1)

        @block.sync
        def _(sp):
            sp.dma_start(over[:, :], d.over).then_inc(s_in, 16)
            sp.wait_ge(s_flag, 1)
            overflow = sp.value_load(flag[0:1, 0:1], min_val=0, max_val=1)
            with sp.If(overflow > 0):
                sp.dma_start(cnt[:, :], d.cnt).then_inc(s_in, 16)
                sp.dma_start(rows[:, :, :], by_tile(table)).then_inc(s_in, 16)
                sp.dma_start(crow[:, :], table[LAST:LAST + 1, :].to_broadcast([P, ROW])).then_inc(s_in, 16)
                sp.wait_ge(s_init, 1)
                sp.dma_start(by_tile(d.state), state[:, :, :]).then_inc(s_stored, 16)
                with sp.Fori(0, TILES) as i:
                    sp.wait_ge(s_idx, i * 1 + 1)
                    sp.dma_start(esrc[:, :], column(0, i)).then_inc(s_e, 16)
                    sp.dma_start(edst[:, :], column(1, i)).then_inc(s_e, 16)
                sp.wait_ge(s_new, 16 * TILES + 16)
                sp.dma_start(state[:, :, :], by_tile(d.state)).then_inc(s_back, 16)
                sp.wait_ge(s_back, 16)
                sp.dma_start(d.sums, state[:, :, 0:20]).then_inc(s_out, 16)
                sp.wait_ge(s_out, 16)

        @block.gpsimd
        def _(pool):
            def setup(n, ins):
                ins.then_inc(s_setup, 1)
                pool.wait_ge(s_setup, n)
            pool.wait_ge(s_in, 16)
            pool.partition_all_reduce(flag[:, :], over[:, :], P, bass.bass_isa.ReduceOp.max).then_inc(s_flag, 1)
            pool.wait_ge(s_flag, 1)
            overflow = pool.value_load(flag[0:1, 0:1], min_val=0, max_val=1)
            with pool.If(overflow > 0):
                setup(1, pool.memset(ident[:, :], 0.0))
                setup(2, pool.affine_select(out=ident[:, :], in_=ident[:, :], compare_op=ALU.not_equal, fill=1.0, base=0,
                                            pattern=[[-1, P]], channel_multiplier=1))
                setup(3, pool.memset(low[:, :], 1.0))
                setup(4, pool.affine_select(out=low[:, :], in_=low[:, :], compare_op=ALU.is_gt, fill=0.0, base=0,
                                            pattern=[[-1, P]], channel_multiplier=1))
                setup(5, pool.memset(dummy[:, :], 0.0))
                pool.wait_ge(s_stored, 16)
                pool.dma_start(d.scrap[:, 0:8], ident[:, 0:8]).then_inc(s_new, 16)
                with pool.Fori(0, TILES) as i:
                    pool.wait_ge(s_idx, i * 1 + 2)
                    pool.tensor_tensor(dummy[:, 1:2], dummy[:, 0:1], dummy[:, 0:1], ALU.add).then_inc(s_pool, 1)
                    pool.indirect_dma_start(g[:, :], None, table, bass.IndirectOffsetOnAxis(ap=si[:, 0:1], axis=0),
                                            bounds_check=LAST, oob_is_err=False).then_inc(s_g, 16)
                    pool.wait_ge(s_new, i * 16 + 16)
                    pool.tensor_tensor(dummy[:, 2:3], dummy[:, 0:1], dummy[:, 0:1], ALU.add).then_inc(s_pool, 1)
                    pool.indirect_dma_start(old[:, :], None, d.state, bass.IndirectOffsetOnAxis(ap=di[:, 0:1], axis=0),
                                            bounds_check=LAST, oob_is_err=False).then_inc(s_g, 16)
                    pool.wait_ge(s_next, i * 1 + 1)
                    pool.tensor_tensor(dummy[:, 3:4], dummy[:, 0:1], dummy[:, 0:1], ALU.add).then_inc(s_pool, 1)
                    pool.indirect_dma_start(d.state, bass.IndirectOffsetOnAxis(ap=oi[:, 0:1], axis=0), new[:, :], None,
                                            bounds_check=LAST, oob_is_err=False).then_inc(s_new, 16)
                    pool.wait_ge(s_pool, i * 3 + 3)

        @block.scalar
        def _(act):
            act.wait_ge(s_flag, 1)
            overflow = act.value_load(flag[0:1, 0:1], min_val=0, max_val=1)
            with act.If(overflow > 0):
                act.wait_ge(s_pre, 1)
                act.activation(e3[:, :, 0:8], e3[:, :, 0:8], ACT.Exp).then_inc(s_exp, 1)
                with act.Fori(0, TILES) as i:
                    act.wait_ge(s_xx, i * 1 + 1)
                    act.activation(y[:, :], y[:, :], ACT.Exp).then_inc(s_yy, 1)

        @block.tensor
        def _(pe):
            pe.wait_ge(s_flag, 1)
            overflow = pe.value_load(flag[0:1, 0:1], min_val=0, max_val=1)
            with pe.If(overflow > 0):
                pe.wait_ge(s_setup, 5)
                with pe.Fori(0, TILES) as i:
                    pe.wait_ge(s_idx, i * 1 + 2)
                    pe.transpose(ps[:, 0, 0:P], dst[:, 0:1].to_broadcast([P, P]), ident[:, :]).then_inc(s_row, 1)
                    pe.wait_ge(s_g, i * 32 + 32)
                    for hd in range(4):
                        last = pe.transpose(ps[:, 1, hd * P:(hd + 1) * P], g[:, 16 + hd:17 + hd].to_broadcast([P, P]), ident[:, :])
                    last.then_inc(s_row, 1)
                    pe.wait_ge(s_vv, i * 1 + 1)
                    pe.matmul(ps[:, 2, 0:20], eq[:, :], v[:, :], start=True, stop=True).then_inc(s_sum, 1)

        @block.vector
        def _(dve):
            dve.wait_ge(s_flag, 1)
            overflow = dve.value_load(flag[0:1, 0:1], min_val=0, max_val=1)
            with dve.If(overflow > 0):
                link = Chain(dve, s_v)
                dve.wait_ge(s_setup, 5)
                dve.wait_ge(s_in, 64)
                def wide(t):
                    return t.to_broadcast([P, P, 4])
                ec, es, en, pn = e3[:, :, 0:4], e3[:, :, 4:8], e3[:, :, 8:12], state[:, :, 0:1]
                a, ad = rows[:, :, 16:20], rows[:, :, 20:24]
                acc, l, m = state[:, :, 0:16], state[:, :, 16:20], state[:, :, 20:24]
                cs = crow[:, None, 16:20].to_broadcast([P, P, 4])
                link(dve.memset(state[:, :, :], 0.0))
                link(dve.tensor_copy(state[:, :, 24:28], ad))
                link(dve.tensor_scalar(pn, cnt[:, :, None], 0.0, MASKED, ALU.is_le, ALU.mult))
                link(dve.tensor_tensor(m, cs, wide(pn), ALU.add))
                link(dve.tensor_tensor(m, m, a, ALU.max))
                link(dve.tensor_tensor(en, m, ad, ALU.add))
                link(dve.tensor_tensor(es, a, ad, ALU.add))
                link(dve.tensor_tensor(ec, cs, ad, ALU.add))
                link(dve.scalar_tensor_tensor(out=e3[:, :, :], in0=e3[:, :, :], scalar=LEAK, in1=e3[:, :, :], op0=ALU.mult, op1=ALU.max))
                link(dve.tensor_tensor(es, es, en, ALU.subtract))
                link(dve.tensor_tensor(ec, ec, en, ALU.subtract))
                link(dve.tensor_scalar(ec, ec, 0.0, None, ALU.min))
                dve.memset(dummy[:, 6:7], 0.0).then_inc(s_pre, 1)
                dve.wait_ge(s_exp, 1)
                link(dve.tensor_tensor(ec, ec, wide(cnt[:, :, None]), ALU.mult))
                link(dve.tensor_tensor(l, ec, es, ALU.add))
                for hd in range(4):
                    part = state[:, :, 4 * hd:4 * hd + 4]
                    link(dve.tensor_tensor(part, rows[:, :, 4 * hd:4 * hd + 4], wide(es[:, :, hd:hd + 1]), ALU.mult))
                    link(dve.tensor_tensor(en, crow[:, None, 4 * hd:4 * hd + 4].to_broadcast([P, P, 4]), wide(ec[:, :, hd:hd + 1]), ALU.mult))
                    link(dve.tensor_tensor(part, part, en, ALU.add))
                dve.memset(dummy[:, 7:8], 0.0).then_inc(s_init, 1)
                dve.memset(keep[:, :], 0.0).then_inc(s_idx, 1)

                def tile(i):
                    dve.wait_ge(s_e, i * 32 + 32)
                    link(dve.tensor_scalar(keep[:, :], esrc[:, :], float(LAST), None, ALU.is_lt))
                    link(dve.scalar_tensor_tensor(out=keep[:, :], in0=edst[:, :], scalar=float(M), in1=keep[:, :], op0=ALU.is_lt, op1=ALU.mult))
                    link(dve.scalar_tensor_tensor(out=dst[:, :], in0=edst[:, :], scalar=-DEAD, in1=keep[:, :], op0=ALU.add, op1=ALU.mult))
                    link(dve.tensor_scalar(dst[:, :], dst[:, :], DEAD, None, ALU.add))
                    link(dve.tensor_scalar(si[:, :], esrc[:, :], float(LAST), None, ALU.min))
                    link(dve.tensor_scalar(di[:, :], dst[:, :], float(LAST), None, ALU.min))
                    dve.memset(y[:, 0:1], 0.0).then_inc(s_idx, 1)
                    dve.wait_ge(s_row, i * 2 + 1)
                    link(dve.tensor_scalar(eq[:, :], ps[:, 0, 0:P], dst[:, 0:1], None, ALU.is_equal))
                    link(dve.tensor_scalar(pen[:, :], eq[:, :], 1.0, -MASKED, ALU.subtract, ALU.mult))
                    link(dve.tensor_tensor(t1[:, :], eq[:, :], low[:, :], ALU.mult))
                    link(dve.tensor_reduce(dup[:, :], t1[:, :], AX_X, ALU.max))
                    link(dve.tensor_scalar(dup[:, :], dup[:, :], DEAD, dst[:, 0:1], ALU.mult, ALU.add))
                    link(dve.tensor_copy(oi[:, :], dup[:, :]))
                    dve.wait_ge(s_row, i * 2 + 2)
                    link(dve.tensor_tensor(sm[:, :, :], ps[:, 1, :].rearrange("p (h n) -> p h n", h=4), pen[:, None, :].to_broadcast([P, 4, P]), ALU.add))
                    link(dve.tensor_reduce(x[:, 0:4], sm[:, :, :], AX_X, ALU.max))
                    dve.wait_ge(s_g, i * 32 + 32)
                    link(dve.tensor_tensor(new[:, 20:24], x[:, 0:4], old[:, 20:24], ALU.max))
                    link(dve.tensor_tensor(x[:, 8:12], new[:, 20:24], old[:, 24:28], ALU.add))
                    link(dve.tensor_tensor(x[:, 4:8], old[:, 20:24], old[:, 24:28], ALU.add))
                    link(dve.tensor_tensor(x[:, 0:4], g[:, 16:20], old[:, 24:28], ALU.add))
                    link(dve.scalar_tensor_tensor(out=x[:, :], in0=x[:, :], scalar=LEAK, in1=x[:, :], op0=ALU.mult, op1=ALU.max))
                    dve.tensor_tensor(y[:, :].rearrange("p (a b) -> p a b", a=2), x[:, 0:8].rearrange("p (a b) -> p a b", a=2),
                                      x[:, None, 8:12].to_broadcast([P, 2, 4]), ALU.subtract).then_inc(s_xx, 1)
                    dve.wait_ge(s_yy, i * 1 + 1)
                    link(dve.tensor_scalar(y[:, 0:4], y[:, 0:4], 1.0, keep[:, 0:1], ALU.min, ALU.mult))
                    link(dve.tensor_copy(v[:, 16:20], y[:, 0:4]))
                    dve.tensor_tensor(v[:, 0:16].rearrange("p (h e) -> p h e", h=4), g[:, 0:16].rearrange("p (h e) -> p h e", h=4),
                                      y[:, 0:4, None].to_broadcast([P, 4, 4]), ALU.mult).then_inc(s_vv, 1)
                    link(dve.tensor_tensor(new[:, 0:16].rearrange("p (h e) -> p h e", h=4), old[:, 0:16].rearrange("p (h e) -> p h e", h=4),
                                           y[:, 4:8, None].to_broadcast([P, 4, 4]), ALU.mult))
                    link(dve.tensor_tensor(new[:, 16:20], old[:, 16:20], y[:, 4:8], ALU.mult))
                    link(dve.tensor_copy(new[:, 24:32], old[:, 24:32]))
                    dve.wait_ge(s_sum, i * 1 + 1)
                    link(dve.tensor_tensor(new[:, 0:20], new[:, 0:20], ps[:, 2, 0:20], ALU.add))
                    dve.memset(dummy[:, 6:7], 0.0).then_inc(s_next, 1)
                    dve.wait_ge(s_new, i * 16 + 32)
                link.loop(TILES, tile)


def expert_phase(nc, d):
    with ExitStack() as ctx:
        def sb(name, shape, dt=F32):
            return ctx.enter_context(nc.sbuf_tensor(name, shape, dt))

        def sem(name):
            return ctx.enter_context(nc.semaphore(name))

        x = Experts(nc, ctx, "late_")
        gpar = sb("x_gpar", [P, 3, GC])
        sums = sb("x_sums", [P, P, 20])
        agg = sb("x_agg", [P, P, GC])
        sq = sb("x_sq", [P, P, GC])
        st = sb("x_st", [P, P, 4])
        score = sb("x_score", [P, P, NE])
        sel = sb("x_sel", [P, P, NE])
        gate = sb("x_gate", [P, P, NE])
        tri = sb("x_tri", [P, NE, NE])
        eps = sb("x_eps", [P, 1])
        res = sb("x_res", [P, 2, CT, D])
        early = sb("x_early", [P, 2, NE, CT, D])
        res2 = sb("x_res2", [P, 2, CT, D])
        y = sb("x_y", [P, 2, CT, D])
        dummy2, zeros = sb("x_dummy2", [P, 8]), sb("x_zeros", [P, 8])
        s_w, s_setup, s_v, s_std, s_var = (sem("x_s_" + n) for n in ("w", "setup", "v", "std", "var"))
        s_added, s_fin, s_fin2 = sem("x_s_added"), sem("x_s_fin"), sem("x_s_fin2")
        s_res, s_out, s_early = ([sem(f"x_s_{n}0"), sem(f"x_s_{n}1")] for n in ("res", "out", "early"))
        block = ctx.enter_context(nc.Block())
        NW = 4

        def node_rows(t, b, half):
            return t[bass.ds(b, 1), half * CHUNK:(half + 1) * CHUNK, :].rearrange("a (t p) n -> p (a t) n", p=P)

        @block.sync
        def _(sp):
            sp.dma_start(sums[:, :, :], d.sums).then_inc(s_w, 16)
            for n, t in enumerate((d.b_gat, d.gamma, d.beta)):
                sp.dma_start(gpar[:, n, :], t.rearrange("(a n) -> a n", a=1).to_broadcast([P, GC])).then_inc(s_w, 16)
            x.load(sp, d)
            with sp.Fori(0, 16 - EARLY) as i:
                for h in range(2):
                    x.load_nodes(sp, d.xnT[EARLY:, :, :, :], i, h)
                    sp.wait_ge(s_out[h], i * 32 + 32)
                    sp.dma_start(res[:, h, :, :], node_rows(d.x1[EARLY:, :, :], i, h)).then_inc(s_res[h], 16)
                    sp.dma_start(res2[:, h, :, :], node_rows(d.x1, i, h)).then_inc(s_early[h], 16)
                    sp.dma_start(early[:, h, :, :, :].rearrange("p e t c -> p (e t c)"),
                                 d.early[bass.ds(i, 1), h, :, :, :, :].rearrange("a p e t c -> p (a e t c)")).then_inc(s_early[h], 16)
            for h in range(2):
                sp.wait_ge(s_out[h], 32 * (17 - EARLY))

        @block.gpsimd
        def _(pool):
            def setup(n, ins):
                ins.then_inc(s_setup, 1)
                pool.wait_ge(s_setup, n)
            setup(1, pool.memset(eps[:, :], LN_EPS))
            setup(2, pool.memset(tri[:, :, :], 1.0))
            setup(3, pool.affine_select(out=tri[:, :, :], in_=tri[:, :, :], compare_op=ALU.is_gt, fill=0.0, base=0,
                                        pattern=[[1, NE], [-1, NE]], channel_multiplier=0))
            setup(4, pool.memset(zeros[:, :], 0.0))
            for h in range(2):
                pool.dma_start(d.scrap[:, h * 16:h * 16 + 8], zeros[:, :]).then_inc(s_out[h], 16)
                pool.dma_start(d.scrap[:, h * 16 + 8:h * 16 + 16], zeros[:, :]).then_inc(s_out[h], 16)
            with pool.Fori(0, 16 - EARLY) as i:
                for h in range(2):
                    pool.wait_ge(s_fin, i * 2 + h + 1)
                    pool.dma_start(node_rows(d.out[EARLY:, :, :], i, h), res[:, h, :, :]).then_inc(s_out[h], 16)
                    pool.wait_ge(s_fin2, i * 2 + h + 1)
                    pool.dma_start(node_rows(d.out, i, h), res2[:, h, :, :]).then_inc(s_out[h], 16)

        @block.scalar
        def _(act):
            act.wait_ge(s_setup, 3)
            act.wait_ge(s_var, 1)
            act.activation(st[:, :, 2], st[:, :, 1], ACT.Sqrt, bias=eps[:, 0:1]).then_inc(s_std, 1)
            act.wait_ge(s_var, 2)
            act.activation(gate[:, :, :], gate[:, :, :], ACT.Exp).then_inc(s_std, 1)
            act.wait_ge(x.s_w, x.LOADED)
            with act.Fori(0, 16 - EARLY) as i:
                for n in range(BODY):
                    x.activate(act, i, n)

        @block.tensor
        def _(pe):
            pe.wait_ge(x.s_w, x.LOADED)
            with pe.Fori(0, 16 - EARLY) as i:
                x.graph(pe, i)

        @block.vector
        def _(dve):
            link = Chain(dve, s_v)
            dve.wait_ge(s_setup, 3)
            x.begin(dve, dummy2[:, 4:8])
            dve.wait_ge(s_w, 16 * NW)

            def wide(x, n):
                return x.to_broadcast([P, P, n])
            link(dve.tensor_scalar(st[:, :, :], sums[:, :, 16:20], 1e-16, None, ALU.add))
            link(dve.reciprocal(st[:, :, :], st[:, :, :]))
            link(dve.tensor_tensor(agg[:, :, :].rearrange("p t (h e) -> p t h e", h=4), sums[:, :, 0:16].rearrange("p t (h e) -> p t h e", h=4),
                                   st[:, :, :, None].to_broadcast([P, P, 4, 4]), ALU.mult))
            link(dve.tensor_tensor(agg[:, :, :], agg[:, :, :], gpar[:, None, 0, :].to_broadcast([P, P, GC]), ALU.add))
            link(dve.tensor_reduce(st[:, :, 0], agg[:, :, :], AX_X, ALU.add))
            link(dve.tensor_scalar(st[:, :, 0], st[:, :, 0], 1.0 / GC, None, ALU.mult))
            link(dve.tensor_tensor(agg[:, :, :], agg[:, :, :], wide(st[:, :, 0:1], GC), ALU.subtract))
            link(dve.tensor_tensor(sq[:, :, :], agg[:, :, :], agg[:, :, :], ALU.mult))
            link(dve.tensor_reduce(st[:, :, 1], sq[:, :, :], AX_X, ALU.add))
            dve.tensor_scalar(st[:, :, 1], st[:, :, 1], 1.0 / GC, None, ALU.mult).then_inc(s_var, 1)
            dve.wait_ge(s_std, 1)
            link(dve.reciprocal(st[:, :, 2], st[:, :, 2]))
            link(dve.tensor_tensor(agg[:, :, :], agg[:, :, :], wide(st[:, :, 2:3], GC), ALU.mult))
            link(dve.tensor_tensor(agg[:, :, :], agg[:, :, :], gpar[:, None, 1, :].to_broadcast([P, P, GC]), ALU.mult))
            link(dve.tensor_tensor(agg[:, :, :], agg[:, :, :], gpar[:, None, 2, :].to_broadcast([P, P, GC]), ALU.add))
            link(dve.tensor_reduce(score[:, :, :], agg[:, :, :].rearrange("p t (h e) -> p t e h", h=4), AX_X, ALU.add))
            link(dve.tensor_scalar(score[:, :, :], score[:, :, :], 0.25, None, ALU.mult))
            mine = score[:, :, :, None].to_broadcast([P, P, NE, NE])
            theirs = score[:, :, None, :].to_broadcast([P, P, NE, NE])
            pairs, ties = (t[:, :, :].rearrange("p t (a b) -> p t a b", a=NE) for t in (agg, sq))
            link(dve.tensor_tensor(pairs, theirs, mine, ALU.is_gt))
            link(dve.tensor_tensor(ties, theirs, mine, ALU.is_equal))
            link(dve.tensor_tensor(ties, ties, tri[:, None, :, :].to_broadcast([P, P, NE, NE]), ALU.mult))
            link(dve.tensor_tensor(pairs, pairs, ties, ALU.add))
            link(dve.tensor_reduce(sel[:, :, :], pairs, AX_X, ALU.add))
            link(dve.tensor_scalar(sel[:, :, :], sel[:, :, :], 1.5, None, ALU.is_lt))
            link(dve.tensor_reduce(st[:, :, 0], score[:, :, :], AX_X, ALU.max))
            dve.tensor_tensor(gate[:, :, :], score[:, :, :], wide(st[:, :, 0:1], NE), ALU.subtract).then_inc(s_var, 1)
            dve.wait_ge(s_std, 2)
            link(dve.tensor_tensor(gate[:, :, :], gate[:, :, :], sel[:, :, :], ALU.mult))
            link(dve.tensor_reduce(st[:, :, 0], gate[:, :, :], AX_X, ALU.add))
            link(dve.reciprocal(st[:, :, 0], st[:, :, 0]))
            link(dve.tensor_tensor(gate[:, :, :], gate[:, :, :], wide(st[:, :, 0:1], NE), ALU.mult))
            dve.wait_ge(x.s_w, x.LOADED)

            def combine(i):
                for n in range(BODY):
                    h, e = n // NE, n % NE
                    if e == 0:
                        dve.wait_ge(s_res[h], i * 16 + 16)
                    ins = x.take(dve, y[:, n % 2, :, :], i, n)
                    ins.then_inc(x.s_y, 1)
                    dve.wait_ge(x.s_y, i * BODY + n + 3)
                    for t in range(CT):
                        last = dve.scalar_tensor_tensor(out=res[:, h, t, :], in0=y[:, n % 2, t, :],
                                                        scalar=gate[:, bass.ds(i * 8 + (EARLY * 8 + h * CT + t), 1), e],
                                                        in1=res[:, h, t, :], op0=ALU.mult, op1=ALU.add)
                    if e == NE - 1:
                        last.then_inc(s_fin, 1)
                    else:
                        link(last)
                    if e == 0:
                        dve.wait_ge(s_early[h], i * 32 + 32)
                    for t in range(CT):
                        last = dve.scalar_tensor_tensor(out=res2[:, h, t, :], in0=early[:, h, e, t, :],
                                                        scalar=gate[:, bass.ds(i * 8 + (h * CT + t), 1), e],
                                                        in1=res2[:, h, t, :], op0=ALU.mult, op1=ALU.add)
                    if e == NE - 1:
                        last.then_inc(s_fin2, 1)
                    else:
                        link(last)
            link.loop(16 - EARLY, combine)


def build(nc, a, out):
    def scratch(name, shape, dt=F32):
        return nc.dram_tensor(name, shape, dt, kind="Internal").ap()

    d = Arrays()
    d.x, d.adj, d.out, d.edges = a["x"], a["adj"], out, a["L0_ffn_edge_index"]
    d.wqT, d.wkT, d.wvT, d.woT = a["WqT"], a["WkT"], a["WvT"], a["WoT"]
    d.bq, d.bk, d.bv, d.bo = a["L0_gnn_bq"], a["L0_gnn_bk"], a["L0_gnn_bv"], a["L0_gnn_bo"]
    d.wgat, d.att_src, d.att_dst, d.b_gat = a["L0_ffn_W_gat"], a["L0_ffn_att_src"], a["L0_ffn_att_dst"], a["L0_ffn_b_gat"]
    d.gamma, d.beta = a["L0_ffn_ln_gamma"], a["L0_ffn_ln_beta"]
    d.w1, d.b1, d.w2, d.b2 = a["L0_ffn_W1"], a["L0_ffn_b1"], a["L0_ffn_W2"], a["L0_ffn_b2"]
    d.x1 = scratch("x1_scratch", (16, N, D))
    d.xnT = scratch("xnT_scratch", (16, P, 2, N))
    d.tab = scratch("tab_scratch", (16, N, ROW))
    d.cells = scratch("cells_scratch", (P * CELLS, 1))
    d.slots = scratch("slots_scratch", (P, SLOTS))
    d.cnt = scratch("cnt_scratch", (P, P))
    d.over = scratch("over_scratch", (P, 1))
    d.sums = scratch("sums_scratch", (P, P, 20))
    d.state = scratch("state_scratch", (M, ROW))
    d.early = scratch("early_scratch", (EARLY, 2, P, NE, CT, D))
    d.scrap = scratch("scrap_scratch", (P, 32))
    attention_phase(nc, d, 16)
    message_phase(nc, d)
    general_phase(nc, d)
    expert_phase(nc, d)


_INS = ["x", "adj", "L0_gnn_bq", "L0_gnn_bk", "L0_gnn_bv", "L0_gnn_bo", "L0_ffn_W_gat", "L0_ffn_att_src", "L0_ffn_att_dst",
        "L0_ffn_b_gat", "L0_ffn_ln_gamma", "L0_ffn_ln_beta", "L0_ffn_W1", "L0_ffn_b1", "L0_ffn_W2", "L0_ffn_b2", "L0_ffn_edge_index"]
_TRANSPOSED = {"WqT": "L0_gnn_Wq", "WkT": "L0_gnn_Wk", "WvT": "L0_gnn_Wv", "WoT": "L0_gnn_Wo"}


def kernel(**inputs):
    import numpy as _np
    import concourse.bacc as _bacc
    from concourse import mybir as _mybir
    from concourse.bass_utils import run_bass_kernel_spmd as _run

    nc = _bacc.Bacc("TRN2", target_bir_lowering=False, num_devices=1)
    arrays, args = {}, {}
    laid = {n: _np.ascontiguousarray(inputs[n]) for n in _INS}
    laid.update({n: _np.ascontiguousarray(_np.asarray(inputs[s]).T) for n, s in _TRANSPOSED.items()})
    for name, a in laid.items():
        arrays[f"in_{name}"] = a
        args[name] = nc.dram_tensor(f"in_{name}", a.shape, _mybir.dt.from_np(a.dtype), kind="ExternalInput").ap()
    out = nc.dram_tensor("out_0", (16, N, D), _mybir.dt.float32, kind="ExternalOutput").ap()
    build(nc, args, out)
    r = _run(nc, [arrays], core_ids=[0])
    return r.results[0]["out_0"]
```

```python
from contextlib import ExitStack

import concourse.bass as bass
from concourse import mybir

P = 128
H, HD = 8, 32
SCALE = HD ** -0.5
LN_EPS = 1e-5
GC = 16
ROW = 32
MASKED = -1.0e30
LEAK = 0.2
NO_KEY = -1.0e29

ALU = mybir.AluOpType
ACT = mybir.ActivationFunctionType
F32, BF16, I32 = mybir.dt.float32, mybir.dt.bfloat16, mybir.dt.int32
AX_X = mybir.AxisListType.X
N, D = 1024, 256
TN = N // P


class Arrays:
    pass


class Chain:

    def __init__(self, engine, sem):
        self.engine, self.sem, self.count = engine, sem, 0

    def __call__(self, ins):
        self.count += 1
        ins.then_inc(self.sem, 1)
        self.engine.wait_ge(self.sem, self.count)

    def restart(self):
        self.engine.sem_clear(self.sem)
        self.count = 0

    def loop(self, times, body):
        with self.engine.Fori(0, times) as i:
            self.restart()
            body(i)
        self.restart()


M = 16 * N
E = 1048576
EC = E // P
LAST = M - 1
KEY_BIT = 0x40000000
NSEG = 16
SEG, SEG_CAP = EC // NSEG, 64
CL_CAP = 144
HC = 8
ROW_CAP = 624
CELL = 20
CELLS = P * CELL
BSEG, BSEG_CAP = 512, 152
NBSEG = CELLS // BSEG
SLOTS = 768
KT = SLOTS // P
FAR = 4194304.0
STAGES = (("segments", 8), ("rows", 2), ("cells", 3), ("buckets", 1), ("slots", 2))


def attention_phase(nc, d, B):
    with ExitStack() as ctx:
        def sb(name, shape, dt=F32):
            return ctx.enter_context(nc.sbuf_tensor(name, shape, dt))

        def sem(name):
            return ctx.enter_context(nc.semaphore(name))

        wq, wk, wv, wo = (sb(n, [P, 2, D]) for n in ("wq", "wk", "wv", "wo"))
        wgat = sb("wgat", [P, 2, GC])
        bqk = sb("bqk", [P, 2, 2])
        bv, bo = sb("bv", [P, D]), sb("bo", [P, D])
        att = sb("att", [P, 2, GC])
        ident = sb("ident", [P, P])
        ident16 = sb("ident16", [P, P], BF16)
        ones32 = sb("ones32", [P, 32])
        eps = sb("eps", [P, 1])
        xb = sb("xb", [P, TN, D])
        xn = sb("xn", [P, TN, D])
        xnT = sb("xnT", [P, 2, N])
        stats = sb("stats", [P, TN, 6])
        mv = sb("mv", [P, TN, 2])
        rstd = sb("rstd", [P, TN])
        qf = sb("qf", [P, 2, N])
        kf = sb("kf", [P, 2, N])
        x1 = qf[:, :, :].rearrange("p g (t d) -> p (g t) d", d=D)
        qp = sb("qp", [P, 3, 2, N], BF16)
        kp = sb("kp", [P, 3, 2, N], BF16)
        q1s, k1s = sb("q1s", [P, H, N], BF16), sb("k1s", [P, H, N], BF16)
        q2s, k2s = sb("q2s", [96, H, N], BF16), sb("k2s", [96, H, N], BF16)
        vt = sb("vt", [P, TN, D])
        adjb = sb("adjb", [P, 2, N], I32)
        mb = sb("mb", [P, TN, N], BF16)
        mT = sb("mT", [P, TN, N], BF16)
        junk = sb("junk", [P, 4, 512], BF16)
        mx = sb("mx", [P, 2, TN, 2])
        m3 = sb("m3", [P, 2, TN, 96], BF16)
        mneg = sb("mneg", [P, TN])
        mrem = sb("mrem", [P, TN])
        pt = xn[:, :, :].rearrange("p t d -> p (t d)").rearrange("p (r n) -> p r n", r=2)
        den = kf
        oT = xnT
        tab = sb("tab", [P, TN, ROW])
        tmp16 = kf[:, 0, 0:TN * GC].rearrange("p (t n) -> p t n", t=TN)
        iota8 = sb("iota8", [P, P, HC], BF16)
        cnt = sb("a_cnt", [P, P])
        heads = sb("heads", [P, P], I32)
        left, over = sb("left", [P, 8]), sb("a_over", [P, 1])
        pcol = sb("pcol", [P, 1])
        sidx, skey = sb("sidx", [P, 16], I32), sb("skey", [P, 16])
        dummy = sb("a_dummy", [P, 3])
        MERGED = NBSEG * BSEG_CAP + P
        store = sb("store", [P, max(NSEG * SEG_CAP + ROW_CAP, MERGED + SLOTS)])
        kept, row = store[:, 0:NSEG * SEG_CAP], store[:, NSEG * SEG_CAP:NSEG * SEG_CAP + ROW_CAP]
        place = store[:, 0:ROW_CAP].bitcast(I32)
        merged, slots = store[:, 0:MERGED], store[:, MERGED:MERGED + SLOTS]
        esrc, edst = adjb[:, 0, :], adjb[:, 1, :]
        adj_flat = adjb[:, :, :].rearrange("p a n -> p (a n)")
        found, found_cl = adj_flat[:, 0:2 * SEG_CAP].bitcast(F32), adj_flat[:, 256:256 + 2 * CL_CAP].bitcast(F32)
        low_int, high_int = adj_flat[:, 1024:1024 + 2 * CL_CAP], adj_flat[:, 1408:1408 + 2 * CL_CAP]
        parts = adj_flat[:, 1728:1728 + 2 * CL_CAP].bitcast(BF16).rearrange("p (a n) -> p a n", a=2)
        live, clamped = qf[:, 0, :], qf[:, 1, :]
        onehot = qp[:, 0:2, :, :].rearrange("p b a (v c) -> p b a v c", c=HC)
        rows_cells = [adj_flat[:, BSEG * n:BSEG * n + BSEG].bitcast(F32) for n in range(4)] + [qf[:, 0, 0:BSEG]]
        RSTEP, SSTEP = ROW_CAP // 2, SLOTS // 2
        in_order = qf[:, 1, :]
        ps = ctx.enter_context(nc.psum_tensor("ps", [P, 8, 512], F32))
        A0 = 6
        O0 = 4

        s_w, s_setup, s_ready, s_x = sem("s_w"), sem("s_setup"), sem("s_ready"), sem("s_x")
        s_arrived, s_clearing, s_go, s_left = sem("s_arrived"), sem("s_clearing"), sem("s_go"), sem("s_left")
        s_bias, s_empty, s_scat, s_placed, s_between, s_over, s_kept = (sem("s_" + n) for n in ("bias", "empty", "scat", "placed", "between", "over", "kept"))
        first_sem = sem("s_first")
        s_rstd, s_xn, s_tr, s_xnT, s_q, s_k, s_v = (sem("s_" + n) for n in ("rstd", "xn", "tr", "xnT", "q", "k", "v"))
        s_adj = [sem("s_adj0"), sem("s_adj1")]
        s_mb = [sem("s_mb0"), sem("s_mb1")]
        s_mtp = sem("s_mtp")
        s_mT = sem("s_mT")
        s_k1 = sem("s_k1")
        s_qf, s_kf, s_vt, s_qp, s_kp = sem("s_qf"), sem("s_kf"), sem("s_vt"), sem("s_qp"), sem("s_kp")
        s_q1s, s_q2s, s_k1s, s_k2s = ([sem(f"s_{n}_{a}") for a in range(4)] for n in ("q1s", "q2s", "k1s", "k2s"))
        s_sc, s_mx, s_m3, s_nmp, s_nm = sem("s_sc"), sem("s_mx"), sem("s_m3"), sem("s_nmp"), sem("s_nm")
        s_st, s_exp, s_pv, s_o, s_dve = sem("s_st"), sem("s_exp"), sem("s_pv"), sem("s_o"), sem("s_dve")
        s_num, s_den = sem("s_num"), sem("s_den")
        s_stage = sem("s_stage")
        s_edges, s_hot, s_counted, s_added = sem("s_edges"), sem("s_hot"), sem("s_counted"), sem("s_added")
        s_wo, s_x1, s_mv, s_xn2, s_tr2, s_xn2T, s_h, s_tab, s_out = (
            sem("s_" + n) for n in ("wo", "x1", "mv", "xn2", "tr2", "xn2T", "h", "tab", "out"))
        s_xbo = sem("s_xbo")
        last_sem = sem("s_last")
        assert last_sem.num - first_sem.num < 64
        block = ctx.enter_context(nc.Block())

        SORTS = [0, 12, 26, 18, 18, 16, 14, 0, 0]
        CHUNKS = [0, 0, 0, 5, 5, 4, 4, 9, 9]
        assert sum(CHUNKS) * HC == 2 * CL_CAP and sum(SORTS) == (CL_CAP + SEG_CAP) // 2
        AFTER = {4: (5, 7, 9, 11), 5: (5, 7, 9, 11, 13), 9: (2, 4, 6, 8, 9, 11, 12, 14, 15)}
        WITH = {4: (2, 3, 4, 4), 5: (2, 3, 4, 4, 5), 9: (1, 2, 2, 3, 4, 4, 5, 6, 6)}
        HALVES = [3, 3, 3, 3, 2, 2, 0, 0]

        def next_batch(engine, i):
            engine.sem_inc(s_arrived, 1)
            engine.wait_ge(s_go, i + 1)
            engine.sem_inc(s_left, 1)

        def stages():
            first = 0
            for stage, batches in STAGES:
                yield stage, first, min(first + batches, B)
                first += batches
                if first >= B:
                    break

        @block.sync
        def _(sp):
            for dst, src in ((wq, d.wqT), (wk, d.wkT), (wv, d.wvT), (wo, d.woT)):
                sp.dma_start(dst[:, :, :], src.rearrange("(c p) n -> p c n", p=P)).then_inc(s_w, 16)
            sp.dma_start(wgat[:, :, :], d.wgat.rearrange("(c p) n -> p c n", p=P)).then_inc(s_w, 16)
            sp.dma_start(bv[:, :], d.bv.rearrange("(a n) -> a n", a=1).to_broadcast([P, D])).then_inc(s_w, 16)
            sp.dma_start(bo[:, :], d.bo.rearrange("(a n) -> a n", a=1).to_broadcast([P, D])).then_inc(s_w, 16)
            for n, b in enumerate((d.bq, d.bk)):
                for c in range(2):
                    sp.dma_start(bqk[:, n, c:c + 1], b[c * P:(c + 1) * P].rearrange("(p a) -> p a", a=1)).then_inc(s_w, 16)
            for n, a in enumerate((d.att_src, d.att_dst)):
                sp.dma_start(att[:, n, :], a.rearrange("h e -> (h e)").rearrange("(a n) -> a n", a=1)
                             .to_broadcast([P, GC])).then_inc(s_w, 16)
            sp.wait_ge(s_setup, 14)
            for n in range(NBSEG):
                sp.dma_start(d.cells.rearrange("(b c) a -> b (c a)", b=P)[:, n * BSEG:(n + 1) * BSEG], qf[:, 0, 0:BSEG]).then_inc(s_empty, 16)
            sp.wait_ge(s_empty, 16 * NBSEG)
            sp.dma_start(xb[:, :, :], d.x[0, :, :].rearrange("(t p) n -> p t n", p=P)).then_inc(s_x, 16)

            def batch(i, last):
                for t in range(TN):
                    if t >= 2:
                        sp.wait_ge(s_mb[t % 2], t // 2)
                    sp.dma_start(adjb[:, t % 2, :], d.adj[bass.ds(i, 1), t * P:(t + 1) * P, :].rearrange("a p n -> p (a n)"))\
                        .then_inc(s_adj[t % 2], 16)
                sp.wait_ge(s_qp, 3)
                def stack(dst, src, signal, sources, places):
                    for a in places:
                        for r, part in enumerate(sources):
                            sp.dma_start(dst[32 * r:32 * r + 32, :, :].rearrange("p (g a) n -> p a g n", a=4)[:, a, :, :],
                                         src[32 * a:32 * a + 32, part, :, :]).then_inc(signal[a], 16)

                stack(q1s, qp, s_q1s, (0, 0, 1, 1), (0, 1))
                stack(q2s, qp, s_q2s, (0, 2), (0, 1))
                sp.wait_ge(s_k1, 1)
                stack(k1s, kp, s_k1s, (0, 1, 0, 1), (0, 1))
                sp.wait_ge(s_kp, 2)
                stack(k2s, kp, s_k2s, (2, 0), (0, 1))
                for a in (2, 3):
                    stack(q1s, qp, s_q1s, (0, 0, 1, 1), (a,))
                    stack(k1s, kp, s_k1s, (0, 1, 0, 1), (a,))
                    stack(q2s, qp, s_q2s, (0, 2), (a,))
                    stack(k2s, kp, s_k2s, (2, 0), (a,))
                sp.wait_ge(s_x1, TN)
                if not last:
                    sp.dma_start(xb[:, :, :], d.x[bass.ds(i + 1, 1), :, :].rearrange("a (t p) n -> p (a t) n", p=P)).then_inc(s_x, 16)
                sp.dma_start(d.x1[bass.ds(i, 1), :, :].rearrange("a (t p) n -> p (a t) n", p=P), x1[:, :, :]).then_inc(s_out, 16)
                sp.wait_ge(s_xn2T, 2)
                sp.dma_start(d.xnT[bass.ds(i, 1), :, :, :].rearrange("a p c n -> p (a c) n"), xnT[:, :, :]).then_inc(s_out, 16)
                sp.wait_ge(s_tab, 1)
                sp.dma_start(d.tab[bass.ds(i, 1), :, :].rearrange("a (t p) n -> p (a t) n", p=P), tab[:, :, :]).then_inc(s_out, 16)
                sp.wait_ge(s_out, 48)
                sp.wait_ge(s_arrived, i * 4 + 4)
                sp.sem_inc(s_clearing, 1)
                sp.sem_clear(range(first_sem.num, last_sem.num + 1))
                sp.sem_inc(s_go, 1)

            with sp.Fori(0, B - 1) as i:
                batch(i, False)
            with sp.Fori(B - 1, B) as i:
                batch(i, True)
            sp.wait_ge(s_over, 1)
            sp.dma_start(d.slots, slots).then_inc(s_kept, 16)
            sp.dma_start(d.over, over[:, :]).then_inc(s_kept, 16)
            sp.dma_start(d.cnt, cnt[:, :]).then_inc(s_kept, 16)
            sp.wait_ge(s_kept, 48)

        @block.gpsimd
        def _(pool):
            def setup(n, ins):
                ins.then_inc(s_setup, 1)
                pool.wait_ge(s_setup, n)

            setup(1, pool.memset(ident[:, :], 0.0))
            setup(2, pool.memset(m3[:, :, :, :], 0.0))
            setup(3, pool.affine_select(out=ident[:, :], in_=ident[:, :], compare_op=ALU.not_equal, fill=1.0, base=0,
                                        pattern=[[-1, P]], channel_multiplier=1))
            setup(4, pool.memset(ones32[:, :], 1.0))
            setup(5, pool.memset(k2s[64:96, :, :], 1.0))
            setup(6, pool.memset(eps[:, :], LN_EPS))
            setup(7, pool.tensor_copy(ident16[:, :], ident[:, :]))
            setup(8, pool.iota(iota8[:, :, :], [[1, P], [0, HC]], base=0, channel_multiplier=0, allow_small_or_imprecise_dtypes=True))
            setup(9, pool.memset(cnt[:, :], 0.0))
            setup(10, pool.memset(left[:, :], 0.0))
            setup(11, pool.memset(dummy[:, :], 0.0))
            setup(12, pool.iota(heads[:, :], [[1, P]], base=0, channel_multiplier=P))
            setup(13, pool.iota(pcol[:, :], [[0, 1]], base=0, channel_multiplier=CELL, allow_small_or_imprecise_dtypes=True))
            setup(14, pool.memset(qf[:, 0, 0:BSEG], 0.0))
            pool.memset(tab[:, :, :], 0.0).then_inc(s_ready, 1)

            def scatter_keys(b):
                times = ROW_CAP // 16 // 3
                with pool.Fori(0, times) as k:
                    at = bass.ds((b * times + k) * 16, 16)
                    pool.tensor_copy(sidx[:, :], place[:, at]).then_inc(s_stage, 1)
                    pool.tensor_copy(skey[:, :], row[:, at]).then_inc(s_stage, 1)
                    pool.wait_ge(s_stage, k * 4 + 2)
                    pool.tensor_tensor(dummy[:, 1:2], dummy[:, 0:1], dummy[:, 0:1], ALU.add).then_inc(s_stage, 1)
                    for c in range(16):
                        pool.indirect_dma_start(d.cells, bass.IndirectOffsetOnAxis(ap=sidx[:, c:c + 1], axis=0), skey[:, c:c + 1], None,
                                                bounds_check=P * CELLS - 1, oob_is_err=False).then_inc(s_scat, 16)
                    pool.wait_ge(s_scat, (b * times + k) * 256 + 256)
                    pool.tensor_tensor(dummy[:, 2:3], dummy[:, 0:1], dummy[:, 0:1], ALU.add).then_inc(s_stage, 1)
                pool.wait_ge(s_stage, times * 4)

            for stage, first, end in stages():
                if stage == "cells":
                    pool.wait_ge(s_placed, 1)
                with pool.Fori(first, end) as i:
                    def mask_tile(t):
                        pool.wait_ge(s_adj[0], 8 * t + 16)
                        pool.tensor_scalar(mb[:, t, :], adjb[:, 0, :], 0, MASKED, ALU.is_equal, ALU.mult).then_inc(s_mb[0], 1)

                    for t in range(0, TN - 2, 2):
                        mask_tile(t)
                    pool.wait_ge(s_kf, 4)
                    pool.tensor_tensor(kf[:, :, :], kf[:, :, :], kp[:, 0, :, :], ALU.subtract).then_inc(s_kp, 1)
                    mask_tile(TN - 2)
                    pool.wait_ge(s_k1, 1)
                    pool.tensor_tensor(kp[:, 2, :, :], kf[:, :, :], kp[:, 1, :, :], ALU.subtract).then_inc(s_kp, 1)
                    pool.wait_ge(s_xn, TN)
                    pool.tensor_tensor(xb[:, :, :], xb[:, :, :], bo[:, None, :].to_broadcast([P, TN, D]), ALU.add).then_inc(s_xbo, 1)
                    pool.wait_ge(s_xbo, 1)
                    if stage == "cells":
                        scatter_keys(i - first)
                    next_batch(pool, i)

        @block.scalar
        def _(act):
            act.wait_ge(s_ready, 1)
            act.wait_ge(s_w, 16 * 13)
            act.wait_ge(s_bias, 1)
            for stage, first, end in stages():
                with act.Fori(first, end) as i:
                    def take_mask(tiles):
                        for c in tiles:
                            act.wait_ge(s_mtp, c + 1)
                            act.activation(mT[:, c, :], ps[:, c % 2, :].bitcast(BF16), ACT.Copy).then_inc(s_mT, 1)

                    act.wait_ge(s_mv, 1)
                    act.activation(rstd[:, :], mv[:, :, 1], ACT.Sqrt, bias=eps[:, 0:1]).then_inc(s_rstd, 1)
                    act.wait_ge(s_tr, TN)
                    act.activation(xnT[:, 0, :].rearrange("p (b n) -> p b n", b=2), ps[:, 0:2, :], ACT.Copy).then_inc(s_xnT, 1)
                    for g in range(2):
                        act.wait_ge(s_q, g + 1)
                        for t in (qf[:, g, :], qp[:, 0, g, :]):
                            act.activation(t.rearrange("p (b n) -> p b n", b=2), ps[:, 4 + 2 * g:6 + 2 * g, :],
                                           ACT.Identity, bias=bqk[:, 0, g:g + 1], scale=SCALE).then_inc(s_qf, 1)
                    for g in range(2):
                        act.wait_ge(s_k, g + 1)
                        for t in (kf[:, g, :], kp[:, 0, g, :]):
                            act.activation(t.rearrange("p (b n) -> p b n", b=2), ps[:, 2 * g:2 * g + 2, :],
                                           ACT.Identity, bias=bqk[:, 1, g:g + 1]).then_inc(s_kf, 1)
                    act.wait_ge(s_kp, 1)
                    act.activation(kp[:, 1, :, :], kf[:, :, :], ACT.Copy).then_inc(s_k1, 1)
                    if stage == "segments":
                        act.wait_ge(s_mb[0], TN // 2)
                        act.wait_ge(s_mb[1], TN // 2)
                        for n, t in enumerate((esrc, edst)):
                            act.dma_start(t, d.edges[n, :].rearrange("(p c) -> p c", p=P)[:, bass.ds((i - first) * (2 * SEG), 2 * SEG)])\
                                .then_inc(s_edges, 16)
                    if stage == "buckets":
                        act.wait_ge(s_mb[0], TN // 2)
                        act.wait_ge(s_mb[1], TN // 2)
                        act.wait_ge(s_qp, 3)
                        for n in range(NBSEG):
                            act.dma_start(rows_cells[n], d.cells.rearrange("(b c) a -> b (c a)", b=P)[:, n * BSEG:(n + 1) * BSEG])\
                                .then_inc(s_edges, 16)
                    take_mask(range(TN))

                    def take_output(j):
                        g, a = j // 4, j % 4
                        act.wait_ge(s_pv, (j + 1) * TN)
                        for nh in range(2):
                            at = slice(nh * 512, nh * 512 + 512)
                            act.activation(den[32 * a:32 * a + 32, g, at], ps[64 * nh + 32:64 * nh + 64, O0 + j % 2, :], ACT.Copy)\
                                .then_inc(s_den, 1)
                            act.activation(oT[32 * a:32 * a + 32, g, at], ps[64 * nh:64 * nh + 32, O0 + j % 2, :], ACT.Copy)\
                                .then_inc(s_num, 1)

                    for j in range(H):
                        act.wait_ge(s_nmp, j + 1)
                        act.activation(q2s[64:96, j, :], ps[64:96, A0, :].bitcast(BF16), ACT.Copy).then_inc(s_nm, 1)
                        for c in range(TN):
                            n = j * TN + c
                            act.wait_ge(s_st, n + 1)
                            if n >= 2:
                                act.wait_ge(s_pv, n - 1)
                            act.activation(pt[:, n % 2, :].rearrange("p (b n) -> p b n", b=2),
                                           ps[:, 2 * (n % 2):2 * (n % 2) + 2, :], ACT.Exp).then_inc(s_exp, 1)
                            if j and c == 1:
                                take_output(j - 1)
                    take_output(H - 1)
                    act.wait_ge(s_mv, 2)
                    act.activation(rstd[:, :], mv[:, :, 1], ACT.Sqrt, bias=eps[:, 0:1]).then_inc(s_rstd, 1)
                    act.wait_ge(s_tr2, TN)
                    act.activation(xnT[:, 0, :].rearrange("p (b n) -> p b n", b=2), ps[:, 4:6, :], ACT.Copy).then_inc(s_xn2T, 1)
                    next_batch(act, i)

        @block.vector
        def _(dve):
            dve.wait_ge(s_ready, 1)
            dve.wait_ge(s_w, 16 * 13)
            link = Chain(dve, s_dve)

            def mask_tile(t):
                dve.wait_ge(s_adj[1], 8 * t + 8)
                dve.tensor_scalar(mb[:, t, :], adjb[:, 1, :], 0, MASKED, ALU.is_equal, ALU.mult).then_inc(s_mb[1], 1)

            def layernorm(src, scale_at):
                if src is xb:
                    for t in range(TN):
                        last = dve.bn_stats(stats[:, t, :], src[:, t, :])
                    link(last)
                for t in range(TN):
                    last = dve.bn_aggr(mv[:, t, :], stats[:, t, :])
                last.then_inc(s_mv, 1)
                if src is xb:
                    mask_tile(1)
                dve.wait_ge(s_rstd, scale_at)
                link(dve.reciprocal(rstd[:, :], rstd[:, :]))

            between = Chain(dve, s_between)

            def note_left(link, values):
                link(dve.tensor_reduce(left[:, 1:2], values, AX_X, ALU.max))
                link(dve.tensor_tensor(left[:, 0:1], left[:, 0:1], left[:, 1:2], ALU.max))

            def place_keys():
                note_left(between, kept)
                bi = kp[:, 0, :, :].rearrange("p g n -> p (g n)").bitcast(I32)[:, 0:ROW_CAP]
                same, rank = (kp[:, n, :, :].rearrange("p g n -> p (g n)").bitcast(F32)[:, 0:ROW_CAP] for n in (1, 2))
                bucket, pos = qf[:, 0, 0:ROW_CAP + 1], qf[:, 1, 0:ROW_CAP]
                low = float(KEY_BIT >> 21)
                between(dve.tensor_scalar(bi, row.bitcast(I32), 21, None, ALU.logical_shift_right))
                between(dve.memset(bucket[:, 0:1], -1.0))
                between(dve.tensor_copy(bucket[:, 1:ROW_CAP + 1], bi))
                between(dve.tensor_tensor(same, bucket[:, 1:ROW_CAP + 1], bucket[:, 0:ROW_CAP], ALU.is_equal))
                between(dve.tensor_tensor_scan(rank, same, same, 0.0, ALU.mult, ALU.add))
                between(dve.tensor_scalar(same, bucket[:, 1:ROW_CAP + 1], low, None, ALU.is_ge))
                between(dve.tensor_tensor(pos, rank, same, ALU.mult))
                between(dve.tensor_scalar(pos, pos, float(CELL), None, ALU.is_ge))
                note_left(between, pos)
                between(dve.tensor_tensor(pos, pos, same, ALU.subtract))
                between(dve.tensor_scalar(pos, pos, FAR, FAR, ALU.mult, ALU.add))
                between(dve.tensor_scalar(bucket[:, 1:ROW_CAP + 1], bucket[:, 1:ROW_CAP + 1], low, 0.0, ALU.subtract, ALU.max))
                between(dve.tensor_scalar(bucket[:, 1:ROW_CAP + 1], bucket[:, 1:ROW_CAP + 1], float(CELLS), pcol[:, 0:1], ALU.mult, ALU.add))
                between(dve.tensor_tensor(rank, rank, bucket[:, 1:ROW_CAP + 1], ALU.add))
                between(dve.tensor_tensor(place, rank, pos, ALU.add))
                dve.sem_inc(s_placed, 1)

            between(dve.tensor_scalar(bqk[:, 0, :], bqk[:, 0, :], SCALE, None, ALU.mult))
            dve.sem_inc(s_bias, 1)
            between(dve.tensor_scalar(heads[:, :], heads[:, :], 14, KEY_BIT, ALU.logical_shift_left, ALU.bitwise_or))
            between(dve.tensor_scalar(heads[:, :], heads[:, :], LAST, None, ALU.bitwise_or))
            for stage, first, end in stages():
                if stage == "cells":
                    place_keys()
                if stage == "buckets":
                    between(dve.tensor_copy(merged[:, NBSEG * BSEG_CAP:MERGED], heads[:, :].bitcast(F32)))
                with dve.Fori(first, end) as i:
                    link.count = 0
                    dve.wait_ge(s_x, i * 16 + 16)
                    layernorm(xb, 1)
                    for t in range(TN):
                        dve.tensor_scalar(xn[:, t, :], xb[:, t, :], mv[:, t, 0:1], rstd[:, t:t + 1], ALU.subtract, ALU.mult)\
                            .then_inc(s_xn, 1)
                    dve.wait_ge(s_tr, TN)
                    dve.tensor_copy(xnT[:, 1, :].rearrange("p (b n) -> p b n", b=2), ps[:, 2:4, :]).then_inc(s_xnT, 1)
                    mask_tile(3)
                    mask_tile(5)
                    dve.wait_ge(s_qf, 4)
                    link(dve.tensor_tensor(qf[:, :, :], qf[:, :, :], qp[:, 0, :, :], ALU.subtract))
                    link(dve.tensor_copy(qp[:, 1, :, :], qf[:, :, :]))
                    dve.tensor_tensor(qp[:, 2, :, :], qf[:, :, :], qp[:, 1, :, :], ALU.subtract).then_inc(s_qp, 3)
                    mask_tile(7)
                    dve.wait_ge(s_v, 1)
                    dve.tensor_tensor(vt[:, :, :], ps[:, 4:8, :].rearrange("p b (c n) -> p (b c) n", c=2),
                                      bv[:, None, :].to_broadcast([P, TN, D]), ALU.add).then_inc(s_vt, 1)

                    def normalise(g):
                        for nh in range(2):
                            at = slice(nh * 512, nh * 512 + 512)
                            dve.wait_ge(s_den, 8 * g + 7 + nh)
                            link(dve.reciprocal(den[:, g, at], den[:, g, at]))
                            dve.wait_ge(s_num, 8 * g + 7 + nh)
                            dve.scalar_tensor_tensor(out=oT[:, g, at], in0=den[:, g, at], scalar=1.0e30, in1=oT[:, g, at],
                                                     op0=ALU.min, op1=ALU.mult).then_inc(s_o, 1)

                    def make_keys(step):
                        if step == 0:
                            dve.wait_ge(s_edges, 32)
                            link(dve.tensor_scalar(clamped, esrc, float(LAST), None, ALU.is_ge))
                        elif step == 1:
                            link(dve.scalar_tensor_tensor(out=clamped, in0=edst, scalar=float(M), in1=clamped, op0=ALU.is_lt, op1=ALU.mult))
                        elif step == 2:
                            link(dve.scalar_tensor_tensor(out=clamped, in0=edst, scalar=1.0, in1=clamped, op0=ALU.add, op1=ALU.mult))
                        elif step == 3:
                            link(dve.tensor_scalar(live, esrc, float(LAST), None, ALU.is_lt))
                        elif step == 4:
                            link(dve.scalar_tensor_tensor(out=live, in0=edst, scalar=float(M), in1=live, op0=ALU.is_lt, op1=ALU.mult))
                        elif step == 5:
                            link(dve.tensor_scalar(edst, edst, M - 1, 14, ALU.bitwise_and, ALU.logical_shift_left))
                        elif step == 6:
                            link(dve.scalar_tensor_tensor(out=edst, in0=edst, scalar=KEY_BIT, in1=esrc, op0=ALU.bitwise_or, op1=ALU.bitwise_or))
                        else:
                            link(dve.tensor_tensor(live, edst.bitcast(F32), live, ALU.mult))

                    def find(values, out, step):
                        at = out[:, 8 * (step // 2):8 * (step // 2) + 8]
                        link(dve.match_replace(values, at, values, 0.0) if step % 2 else dve.max(at, values))

                    def split_destinations(g):
                        at = slice(g * CL_CAP, (g + 1) * CL_CAP)
                        link(dve.tensor_scalar(high_int[:, at], found_cl[:, at], 1.0, None, ALU.subtract))
                        link(dve.tensor_scalar(low_int[:, at], high_int[:, at], P - 1, None, ALU.bitwise_and))
                        link(dve.tensor_scalar(high_int[:, at], high_int[:, at], 7, None, ALU.logical_shift_right))
                        link(dve.tensor_copy(parts[:, 0, at], low_int[:, at]))
                        link(dve.tensor_copy(parts[:, 1, at], high_int[:, at]))

                    def one_hots(j, k):
                        q = sum(CHUNKS[:j]) + k
                        if q >= 2:
                            dve.wait_ge(s_counted, q - 1)
                        else:
                            for n in range(4):
                                dve.wait_ge(s_q1s[n], 64)
                                dve.wait_ge(s_q2s[n], 32)
                        for a in range(2):
                            dve.tensor_tensor(onehot[:, q % 2, a, :, :], iota8[:, :, :],
                                              parts[:, a, None, q * HC:q * HC + HC].to_broadcast([P, P, HC]), ALU.is_equal).then_inc(s_hot, 1)

                    def add_counts(j):
                        dve.wait_ge(s_counted, sum(CHUNKS[:j + 1]))
                        dve.tensor_tensor(cnt[:, :], cnt[:, :], ps[:, O0 + j % 2, 0:P], ALU.add).then_inc(s_added, 1)
                        dve.wait_ge(s_added, j - 2)

                    def segment_step(j, n):
                        if j == 1 and n < 8:
                            make_keys(n)
                        if n == 0 and j == 3:
                            split_destinations(0)
                        if n == 0 and j == 7:
                            split_destinations(1)
                            note_left(link, clamped)
                            note_left(link, live)
                            link(dve.tensor_copy(kept[:, bass.ds((i - first) * (2 * SEG_CAP), 2 * SEG_CAP)], found))
                        done, clamp_steps, live_steps = sum(SORTS[:j]), CL_CAP // 4, SEG_CAP // 4
                        slot, slots_of_head = (n - 8, 8) if j == 1 else (n, 16)
                        for step in range(done + SORTS[j] * max(slot, 0) // slots_of_head, done + SORTS[j] * max(slot + 1, 0) // slots_of_head):
                            if step < clamp_steps:
                                find(clamped[:, 0:SEG], found_cl[:, 0:CL_CAP], step)
                            elif step < clamp_steps + live_steps:
                                find(live[:, SEG:2 * SEG], found[:, SEG_CAP:2 * SEG_CAP], step - clamp_steps)
                            elif step < 2 * clamp_steps + live_steps:
                                find(clamped[:, SEG:2 * SEG], found_cl[:, CL_CAP:2 * CL_CAP], step - clamp_steps - live_steps)
                            else:
                                find(live[:, 0:SEG], found[:, 0:SEG_CAP], step - 2 * clamp_steps - live_steps)
                        if CHUNKS[j] and n in AFTER[CHUNKS[j]]:
                            one_hots(j, AFTER[CHUNKS[j]].index(n))

                    def row_step(step):
                        if step < RSTEP // 4:
                            find(kept, in_order, step)

                    def bucket_step(step):
                        n = step // (BSEG_CAP // 4)
                        if n < NBSEG:
                            find(rows_cells[n], merged[:, n * BSEG_CAP:(n + 1) * BSEG_CAP], step % (BSEG_CAP // 4))

                    def slot_step(step):
                        if step < SSTEP // 4:
                            find(merged, in_order, step)

                    EVEN = {"rows": (row_step, 12), "buckets": (bucket_step, 23), "slots": (slot_step, 14)}

                    def edges_within(j, n):
                        if stage == "segments":
                            segment_step(j, n)
                        elif stage in EVEN and j:
                            step, each = EVEN[stage]
                            if stage == "buckets" and j == 1 and n == 0:
                                dve.wait_ge(s_edges, 16 * NBSEG)
                            for m in range(each * n // 16, each * (n + 1) // 16):
                                step((j - 1) * each + m)

                    def edges_after():
                        if stage == "segments":
                            for k in range(CHUNKS[H]):
                                one_hots(H, k)
                            add_counts(H)
                        elif stage == "rows":
                            link(dve.tensor_copy(row[:, bass.ds((i - first) * RSTEP, RSTEP)], in_order[:, 0:RSTEP]))
                        elif stage == "buckets":
                            step, each = EVEN[stage]
                            for m in range(7 * each, NBSEG * (BSEG_CAP // 4)):
                                step(m)
                            for values in rows_cells:
                                note_left(link, values)
                        elif stage == "slots":
                            link(dve.tensor_copy(slots[:, bass.ds((i - first) * SSTEP, SSTEP)], in_order[:, 0:SSTEP]))

                    def maxima(j):
                        for n in range(2 * TN):
                            t, mh = n // 2, n % 2
                            if n >= 4:
                                dve.wait_ge(s_mx, j * 2 * TN + n - 3)
                            dve.wait_ge(s_sc, j * 2 * TN + n + 1)
                            last = dve.tensor_tensor_reduce(out=junk[:, n % 4, :], in0=ps[:, A0 + n % 2, :], in1=mb[:, t, mh * 512:mh * 512 + 512],
                                                            scale=1.0, scalar=-3.0e38, op0=ALU.add, op1=ALU.max,
                                                            accum_out=mx[:, j % 2, t, mh:mh + 1])
                            last.then_inc(s_mx, 1)
                            if j == 6 and n == 12:
                                normalise(0)
                            edges_within(j, n)
                        dve.wait_ge(s_mx, (j + 1) * 2 * TN)
                        link(dve.tensor_tensor(mneg[:, :], mx[:, j % 2, :, 0], mx[:, j % 2, :, 1], ALU.max))
                        link(dve.tensor_scalar(mneg[:, :], mneg[:, :], NO_KEY, -1.0, ALU.max, ALU.mult))
                        part = [m3[:, j % 2, :, 64 + n] for n in range(3)]
                        link(dve.tensor_copy(part[0], mneg[:, :]))
                        link(dve.tensor_tensor(mrem[:, :], mneg[:, :], part[0], ALU.subtract))
                        link(dve.tensor_copy(part[1], mrem[:, :]))
                        dve.tensor_tensor(part[2], mrem[:, :], part[1], ALU.subtract).then_inc(s_m3, 1)
                        if stage == "segments" and CHUNKS[j]:
                            add_counts(j)

                    for j in range(H):
                        maxima(j)
                    edges_after()
                    normalise(1)
                    dve.wait_ge(s_xbo, 1)
                    for t in range(0, TN, 2):
                        dve.wait_ge(s_wo, t + 2)
                        dve.tensor_tensor(x1[:, t:t + 2, :], ps[:, t // 2, :].rearrange("p (a n) -> p a n", a=2), xb[:, t:t + 2, :],
                                          ALU.add).then_inc(s_x1, 2)
                        dve.wait_ge(s_x1, t + 2)
                        for u in (t, t + 1):
                            last = dve.bn_stats(stats[:, u, :], x1[:, u, :])
                    link(last)
                    layernorm(x1, 2)
                    for t in range(TN):
                        dve.tensor_scalar(xn[:, t, :], x1[:, t, :], mv[:, t, 0:1], rstd[:, t:t + 1], ALU.subtract, ALU.mult)\
                            .then_inc(s_xn2, 1)
                    dve.wait_ge(s_tr2, TN)
                    dve.tensor_copy(xnT[:, 1, :].rearrange("p (b n) -> p b n", b=2), ps[:, 6:8, :]).then_inc(s_xn2T, 1)
                    dve.wait_ge(s_h, 1)
                    link(dve.tensor_copy(tab[:, :, 0:GC], ps[:, 0, 0:TN * GC].rearrange("p (t n) -> p t n", t=TN)))
                    for n in range(2):
                        link(dve.tensor_tensor(tmp16[:, :, :], tab[:, :, 0:GC], att[:, n, None, :].to_broadcast([P, TN, GC]), ALU.mult))
                        link(dve.tensor_reduce(tab[:, :, GC + 4 * n:GC + 4 * n + 4], tmp16[:, :, :].rearrange("p t (h e) -> p t h e", h=4),
                                                  AX_X, ALU.add))
                    dve.sem_inc(s_tab, 1)
                    next_batch(dve, i)
            note_left(between, merged)
            dve.tensor_scalar(over[:, :], left[:, 0:1], 0.0, None, ALU.is_gt).then_inc(s_over, 1)

        @block.tensor
        def _(pe):
            pe.wait_ge(s_ready, 1)
            pe.wait_ge(s_w, 16 * 13)
            for stage, first, end in stages():
                with pe.Fori(first, end) as i:
                    for t in range(TN):
                        pe.wait_ge(s_xn, t + 1)
                        for c in range(2):
                            last = pe.transpose(ps[:, 2 * c + t // 4, (t % 4) * P:(t % 4 + 1) * P], xn[:, t, c * P:(c + 1) * P], ident[:, :])
                        last.then_inc(s_tr, 1)
                    pe.wait_ge(s_xnT, 2)

                    def project(w, g, bank):
                        for nh in range(2):
                            for c in range(2):
                                last = pe.matmul(ps[:, bank + nh, :], w[:, c, g * P:(g + 1) * P], xnT[:, c, nh * 512:nh * 512 + 512],
                                                 start=c == 0, stop=c == 1)
                        return last

                    for g in range(2):
                        project(wq, g, 4 + 2 * g).then_inc(s_q, 1)
                    for g in range(2):
                        project(wk, g, 2 * g).then_inc(s_k, 1)
                    pe.wait_ge(s_qf, 4)
                    for t in range(TN):
                        for c in range(2):
                            last = pe.matmul(ps[:, 4 + t // 2, (t % 2) * D:(t % 2 + 1) * D], xnT[:, c, t * P:(t + 1) * P], wv[:, c, :],
                                             start=c == 0, stop=c == 1)
                    last.then_inc(s_v, 1)
                    pe.wait_ge(s_vt, 1)

                    def mask_tile(c):
                        if c == 0:
                            pe.wait_ge(s_mb[0], TN // 2)
                            pe.wait_ge(s_mb[1], TN // 2)
                            pe.wait_ge(s_kf, 2)
                        if c >= 2:
                            pe.wait_ge(s_mT, c - 1)
                        for t in range(TN):
                            last = pe.transpose(ps[:, c % 2, :].bitcast(BF16)[:, t * P:(t + 1) * P], mb[:, t, c * P:(c + 1) * P], ident16[:, :])
                        last.then_inc(s_mtp, 1)

                    def score_half(j, n):
                        h, t, mh = j, n // 2, n % 2
                        if n == 0:
                            pe.wait_ge(s_q1s[h % 4], 64)
                            pe.wait_ge(s_k1s[h % 4], 64)
                            if j >= 1:
                                pe.wait_ge(s_nm, j)
                        if n >= 2:
                            pe.wait_ge(s_mx, j * 2 * TN + n - 1)
                        elif n == 1 and j >= 1:
                            pe.wait_ge(s_mx, j * 2 * TN)
                        pe.matmul(ps[:, A0 + n % 2, :], q1s[:, h, t * P:(t + 1) * P], k1s[:, h, mh * 512:mh * 512 + 512],
                                  start=True, stop=True).then_inc(s_sc, 1)

                    def maxima_rows(j):
                        pe.wait_ge(s_m3, j + 1)
                        for t in range(TN):
                            last = pe.transpose(ps[0:96, A0, :].bitcast(BF16)[:, t * P:(t + 1) * P], m3[:, j % 2, t, :], ident16[:, :])
                        last.then_inc(s_nmp, 1)

                    def shifted_scores(j, c):
                        h, n = j, j * TN + c
                        if n >= 2:
                            pe.wait_ge(s_exp, n - 1)
                        else:
                            pe.wait_ge(s_mT, TN)
                        if c == 0:
                            pe.wait_ge(s_q2s[h % 4], 32)
                            pe.wait_ge(s_k2s[h % 4], 32)
                            pe.wait_ge(s_nm, j + 1)
                        for lhs, rhs in ((k1s, q1s), (k2s, q2s)):
                            for nh in range(2):
                                pe.matmul(ps[:, 2 * (n % 2) + nh, :], lhs[:, h, c * P:(c + 1) * P], rhs[:, h, nh * 512:nh * 512 + 512],
                                          start=lhs is k1s, stop=False)
                        for nh in range(2):
                            last = pe.matmul(ps[:, 2 * (n % 2) + nh, :], ident16[:, :], mT[:, c, nh * 512:nh * 512 + 512],
                                             start=False, stop=True)
                        last.then_inc(s_st, 1)

                    def weighted_values(j, c):
                        h, n = j, j * TN + c
                        if stage == "segments" and c == 0 and CHUNKS[j]:
                            pe.wait_ge(s_added, j - 2)
                        if c == 0 and j >= 2:
                            pe.wait_ge(s_num, 2 * j - 2)
                            pe.wait_ge(s_den, 2 * j - 2)
                        pe.wait_ge(s_exp, n + 1)
                        for nh in range(2):
                            for r, lhs in enumerate((vt[:, c, 32 * h:32 * h + 32], ones32[:, :])):
                                at = 64 * nh + 32 * r
                                last = pe.matmul(ps[at:at + 32, O0 + j % 2, :], lhs, pt[:, n % 2, nh * 512:nh * 512 + 512],
                                                 start=c == 0, stop=c == TN - 1, tile_position=(0, at))
                        last.then_inc(s_pv, 1)

                    def count_edges(j, k):
                        q = sum(CHUNKS[:j]) + k
                        if k == 0:
                            pe.wait_ge(s_num, 2 * j - 2)
                            pe.wait_ge(s_den, 2 * j - 2)
                        pe.wait_ge(s_hot, 2 * q + 2)
                        for c in range(HC):
                            last = pe.matmul(ps[:, O0 + j % 2, 0:P], onehot[:, q % 2, 0, :, c], onehot[:, q % 2, 1, :, c],
                                             start=k == 0 and c == 0, stop=k == CHUNKS[j] - 1 and c == HC - 1)
                        last.then_inc(s_counted, 1)

                    for c in range(TN):
                        score_half(0, 2 * c)
                        score_half(0, 2 * c + 1)
                        mask_tile(c)
                    maxima_rows(0)
                    for j in range(H):
                        for c in range(TN):
                            shifted_scores(j, c)
                            if c == 0 and j:
                                weighted_values(j - 1, TN - 1)
                            if j + 1 < H:
                                for n in range(sum(HALVES[:c]), sum(HALVES[:c + 1])):
                                    score_half(j + 1, n)
                            if stage == "segments" and CHUNKS[j + 1]:
                                for k in range(CHUNKS[j + 1]):
                                    if WITH[CHUNKS[j + 1]][k] == c:
                                        count_edges(j + 1, k)
                            if c:
                                weighted_values(j, c - 1)
                        if j + 1 < H:
                            maxima_rows(j + 1)
                    weighted_values(H - 1, TN - 1)
                    pe.wait_ge(s_exp, H * TN)
                    for t in range(TN):
                        pe.wait_ge(s_o, 3 + t * P // 512)
                        for g in range(2):
                            last = pe.matmul(ps[:, t // 2, (t % 2) * D:(t % 2 + 1) * D], oT[:, g, t * P:(t + 1) * P], wo[:, g, :],
                                             start=g == 0, stop=g == 1)
                        last.then_inc(s_wo, 1)
                    for t in range(TN):
                        pe.wait_ge(s_xn2, t + 1)
                        for c in range(2):
                            last = pe.transpose(ps[:, 4 + 2 * c + t // 4, (t % 4) * P:(t % 4 + 1) * P], xn[:, t, c * P:(c + 1) * P], ident[:, :])
                        last.then_inc(s_tr2, 1)
                    pe.wait_ge(s_xn2T, 2)
                    pe.wait_ge(s_x1, TN)
                    for t in range(TN):
                        for c in range(2):
                            last = pe.matmul(ps[:, 0, t * GC:(t + 1) * GC], xnT[:, c, t * P:(t + 1) * P], wgat[:, c, :],
                                             start=c == 0, stop=c == 1)
                    last.then_inc(s_h, 1)
                    next_batch(pe, i)


F = 2 * D
NE = 4
FT = F // P
CHUNK = 512
CT = CHUNK // P
BODY = 2 * NE
EARLY = 8


class Experts:

    def __init__(self, nc, ctx, name):
        def sb(n, shape):
            return ctx.enter_context(nc.sbuf_tensor(name + n, shape, F32))

        self.w1, self.w2 = sb("w1", [P, NE, 2, F]), sb("w2", [P, NE, FT, D])
        self.b1, self.b2 = sb("b1", [P, NE, FT]), sb("b2", [P, NE, D])
        self.xT = sb("xT", [P, 2, 2, CHUNK])
        self.hid = sb("hid", [P, 2, FT, CHUNK])
        self.ps = ctx.enter_context(nc.psum_tensor(name + "ps", [P, 8, 512], F32))
        self.s_w, self.s_up, self.s_act, self.s_down, self.s_y = (
            ctx.enter_context(nc.semaphore(name + n)) for n in ("s_w", "s_up", "s_act", "s_down", "s_y"))
        self.s_in = [ctx.enter_context(nc.semaphore(name + n)) for n in ("s_in0", "s_in1")]
        self.LOADED = 16 * (3 + NE * FT)

    def load(self, sp, d):
        sp.dma_start(self.w1[:, :, :, :], d.w1.rearrange("e (c p) f -> p e c f", p=P)).then_inc(self.s_w, 16)
        sp.dma_start(self.w2[:, :, :, :], d.w2.rearrange("e (c p) n -> p e c n", p=P)).then_inc(self.s_w, 16)
        sp.dma_start(self.b2[:, :, :].rearrange("p e n -> p (e n)"),
                     d.b2.rearrange("e n -> (e n)").rearrange("(a n) -> a n", a=1).to_broadcast([P, NE * D])).then_inc(self.s_w, 16)
        for e in range(NE):
            for f in range(FT):
                sp.dma_start(self.b1[:, e, f:f + 1], d.b1[e, f * P:(f + 1) * P].rearrange("(p a) -> p a", a=1)).then_inc(self.s_w, 16)

    def load_nodes(self, sp, graphs, i, h):
        sp.wait_ge(self.s_up, i * (BODY * FT) + (h + 1) * NE * FT)
        at = slice(i, i + 1) if isinstance(i, int) else bass.ds(i, 1)
        sp.dma_start(self.xT[:, h, :, :], graphs[at, :, :, h * CHUNK:(h + 1) * CHUNK].rearrange("a p c n -> p (a c) n"))\
            .then_inc(self.s_in[h], 16)

    def begin(self, dve, cells):
        dve.memset(cells[:, 0:1], 0.0).then_inc(self.s_up, BODY * FT)
        dve.memset(cells[:, 1:2], 0.0).then_inc(self.s_y, 2)
        dve.memset(cells[:, 2:3], 0.0).then_inc(self.s_down, 2)
        dve.memset(cells[:, 3:4], 0.0).then_inc(self.s_act, 4)

    def activate(self, act, i, n):
        act.wait_ge(self.s_down, i * BODY + n + 1)
        for f in range(FT):
            act.wait_ge(self.s_up, (i * BODY + n) * FT + BODY * FT + f + 1)
            act.activation(self.hid[:, n % 2, f, :], self.ps[:, f, :], ACT.Gelu, bias=self.b1[:, n % NE, f:f + 1]).then_inc(self.s_act, 1)

    def up(self, pe, i, n):
        h, e = n // NE, n % NE
        if e == 0:
            pe.wait_ge(self.s_in[h], i * 16 + 16)
        for f in range(FT):
            pe.wait_ge(self.s_act, (i * BODY + n) * FT + f + 1)
            for c in range(2):
                last = pe.matmul(self.ps[:, f, :], self.w1[:, e, c, f * P:(f + 1) * P], self.xT[:, h, c, :], start=c == 0, stop=c == 1)
            last.then_inc(self.s_up, 1)

    def down(self, pe, i, n):
        e, at = n % NE, 4 + 2 * (n % 2)
        pe.wait_ge(self.s_act, (i * BODY + n) * FT + FT + 4)
        pe.wait_ge(self.s_y, i * BODY + n + 1)
        for t in range(CT):
            for f in range(FT):
                last = pe.matmul(self.ps[:, at + t // 2, (t % 2) * D:(t % 2 + 1) * D], self.hid[:, n % 2, f, t * P:(t + 1) * P],
                                 self.w2[:, e, f, :], start=f == 0, stop=f == FT - 1)
        last.then_inc(self.s_down, 1)

    def graph(self, pe, i):
        self.up(pe, i, 0)
        for n in range(BODY):
            if n + 1 < BODY:
                self.up(pe, i, n + 1)
            self.down(pe, i, n)

    def take(self, dve, y, i, n):
        at = 4 + 2 * (n % 2)
        dve.wait_ge(self.s_down, i * BODY + n + 3)
        return dve.tensor_tensor(y, self.ps[:, at:at + 2, :].rearrange("p b (c n) -> p (b c) n", c=2),
                                 self.b2[:, None, n % NE, :].to_broadcast([P, CT, D]), ALU.add)


def message_phase(nc, d):
    with ExitStack() as ctx:
        class Slots:
            pass

        m = Slots()
        m.head = ctx.enter_context(nc.sbuf_tensor("m_head", [P, SLOTS], F32))
        m.same = ctx.enter_context(nc.sbuf_tensor("m_same", [P, SLOTS], F32))
        m.pen = ctx.enter_context(nc.sbuf_tensor("m_pen", [P, 2, SLOTS], F32))
        m.lowT = ctx.enter_context(nc.sbuf_tensor("m_lowT", [P, KT, P], F32))
        m.G = ctx.enter_context(nc.sbuf_tensor("m_G", [P, SLOTS, 24], F32))
        m.iota = ctx.enter_context(nc.sbuf_tensor("m_iota", [P, P], F32))
        m.ident = ctx.enter_context(nc.sbuf_tensor("m_ident", [P, P], F32))
        gather_rows(nc, d, m)
        sum_messages(nc, d, m)


def gather_rows(nc, d, m):
    with ExitStack() as ctx:
        def sb(name, shape, dt=F32):
            return ctx.enter_context(nc.sbuf_tensor(name, shape, dt))

        def sem(name):
            return ctx.enter_context(nc.semaphore(name))

        head, same, pen, lowT, G, iota, ident = m.head, m.same, m.pen, m.lowT, m.G, m.iota, m.ident
        x = Experts(nc, ctx, "early_")
        y = sb("m_y", [P, 2, CT, D])
        slots = sb("m_slots", [P, SLOTS])
        ki = sb("m_ki", [P, SLOTS], I32)
        dsti = sb("m_dsti", [P, SLOTS], I32)
        live = sb("m_live", [P, SLOTS])
        dst = sb("m_dst", [P, SLOTS + 2])
        low = sb("m_low", [P, SLOTS])
        idx = sb("m_idx", [P, SLOTS])
        idxT = sb("m_idxT", [P, KT, P], I32)
        sidx = sb("m_sidx", [P, 2, 16], I32)
        stage = sb("m_stage", [P, 2, 16, ROW])
        dummy, dummy2, zeros = sb("m_dummy", [P, 3]), sb("m_dummy2", [P, 8]), sb("m_zeros", [P, 8])
        ps = x.ps
        s_in, s_setup, s_v, s_idx, s_tr, s_stage, s_copied = (
            sem("m_s_" + n) for n in ("in", "setup", "v", "idx", "tr", "stage", "copied"))
        s_g = [sem("m_s_g0"), sem("m_s_g1")]
        s_stored = [sem("m_s_st0"), sem("m_s_st1")]
        block = ctx.enter_context(nc.Block())
        HALVES = SLOTS // 16 // EARLY
        COPY_AFTER = (1, 2, 3, 5, 6, 7)
        assert len(COPY_AFTER) == HALVES

        @block.sync
        def _(sp):
            sp.dma_start(slots[:, :], d.slots).then_inc(s_in, 16)
            x.load(sp, d)
            sp.wait_ge(s_setup, 5)
            for b in range(2):
                sp.dma_start(d.scrap[:, b * 8:b * 8 + 8], zeros[:, :]).then_inc(s_stored[b], 16)
            for h in range(2):
                x.load_nodes(sp, d.xnT, 0, h)
            with sp.Fori(0, EARLY) as i:
                for h in range(2):
                    for n in range(h * NE, h * NE + NE):
                        sp.wait_ge(x.s_y, i * BODY + n + 3)
                        sp.dma_start(d.early[bass.ds(i, 1), h, :, n % NE, :, :].rearrange("a p t c -> p (a t) c"), y[:, n % 2, :, :])\
                            .then_inc(s_stored[n % 2], 16)
                    x.load_nodes(sp, d.xnT, i + 1, h)
            for h in range(2):
                sp.wait_ge(x.s_in[h], 16 * (EARLY + 1))
            for b in range(2):
                sp.wait_ge(s_stored[b], 16 * (EARLY * NE + 1))

        @block.gpsimd
        def _(pool):
            def setup(n, ins):
                ins.then_inc(s_setup, 1)
                pool.wait_ge(s_setup, n)
            setup(1, pool.iota(iota[:, :], [[1, P]], base=0, channel_multiplier=0, allow_small_or_imprecise_dtypes=True))
            setup(2, pool.memset(ident[:, :], 0.0))
            setup(3, pool.affine_select(out=ident[:, :], in_=ident[:, :], compare_op=ALU.not_equal, fill=1.0, base=0,
                                        pattern=[[-1, P]], channel_multiplier=1))
            setup(4, pool.memset(dummy[:, :], 0.0))
            setup(5, pool.memset(zeros[:, :], 0.0))
            pool.wait_ge(s_idx, 3)
            table = d.tab.rearrange("b n c -> (b n) c")
            idx_flat = idxT[:, :, :].rearrange("p k b -> p (k b)")
            with pool.Fori(0, SLOTS // 32) as i:
                for b in range(2):
                    pool.wait_ge(s_copied, i * 2 + b + 1)
                    pool.tensor_copy(sidx[:, b, :], idx_flat[:, bass.ds(i * 32 + b * 16, 16)]).then_inc(s_stage, 1)
                    pool.wait_ge(s_stage, i * 4 + 2 * b + 1)
                    pool.tensor_tensor(dummy[:, 1 + b:2 + b], dummy[:, 0:1], dummy[:, 0:1], ALU.add).then_inc(s_stage, 1)
                    for c in range(16):
                        pool.indirect_dma_start(stage[:, b, c, :], None, table, bass.IndirectOffsetOnAxis(ap=sidx[:, b, c:c + 1], axis=0),
                                                bounds_check=LAST, oob_is_err=False).then_inc(s_g[b], 16)

        @block.scalar
        def _(act):
            act.wait_ge(x.s_w, x.LOADED)
            with act.Fori(0, EARLY) as i:
                for n in range(BODY):
                    x.activate(act, i, n)
                    if n in COPY_AFTER:
                        half = COPY_AFTER.index(n)
                        act.wait_ge(s_g[half % 2], i * (128 * HALVES) + (half // 2 * 256 + 256))
                        act.activation(G[:, bass.ds(i * (16 * HALVES) + half * 16, 16), :], stage[:, half % 2, :, 0:24], ACT.Copy)\
                            .then_inc(s_copied, 1)

        @block.tensor
        def _(pe):
            pe.wait_ge(s_setup, 4)
            pe.wait_ge(s_idx, 2)
            for n, t in enumerate((idx, low)):
                for k in range(KT):
                    last = pe.transpose(ps[:, 2 * n + k // 4, (k % 4) * P:(k % 4 + 1) * P], t[:, k * P:(k + 1) * P], ident[:, :])
                last.then_inc(s_tr, 1)
            pe.wait_ge(s_idx, 3)
            pe.wait_ge(x.s_w, x.LOADED)
            with pe.Fori(0, EARLY) as i:
                x.graph(pe, i)

        @block.vector
        def _(dve):
            link = Chain(dve, s_v)
            dve.wait_ge(s_setup, 4)
            dve.wait_ge(s_in, 16)
            link(dve.memset(dst[:, :], -2.0))
            link(dve.tensor_scalar(ki[:, :], slots[:, :].bitcast(I32), LAST, None, ALU.bitwise_and))
            link(dve.tensor_scalar(head[:, :], ki[:, :], float(LAST), None, ALU.is_equal))
            link(dve.tensor_scalar(dsti[:, :], slots[:, :].bitcast(I32), 14, LAST, ALU.logical_shift_right, ALU.bitwise_and))
            link(dve.tensor_scalar(live[:, :], slots[:, :], 0.0, None, ALU.is_gt))
            link(dve.scalar_tensor_tensor(out=idx[:, :], in0=dsti[:, :], scalar=-float(LAST), in1=head[:, :], op0=ALU.add, op1=ALU.mult))
            link(dve.tensor_tensor(idx[:, :], idx[:, :], ki[:, :], ALU.add))
            link(dve.scalar_tensor_tensor(out=dst[:, 1:SLOTS + 1], in0=dsti[:, :], scalar=1.0, in1=live[:, :], op0=ALU.add, op1=ALU.mult))
            link(dve.tensor_scalar(dst[:, 1:SLOTS + 1], dst[:, 1:SLOTS + 1], 1.0, None, ALU.subtract))
            link(dve.tensor_scalar(dsti[:, :], dsti[:, :], P - 1, None, ALU.bitwise_and))
            link(dve.tensor_scalar(low[:, :], live[:, :], -512.0, 512.0, ALU.mult, ALU.add))
            link(dve.tensor_tensor(low[:, :], low[:, :], dsti[:, :], ALU.add))
            link(dve.tensor_tensor(same[:, :], dst[:, 1:SLOTS + 1], dst[:, 0:SLOTS], ALU.is_equal))
            link(dve.tensor_scalar(pen[:, 0, :], same[:, :], 1.0, -MASKED, ALU.subtract, ALU.mult))
            link(dve.tensor_tensor(pen[:, 1, :], dst[:, 1:SLOTS + 1], dst[:, 2:SLOTS + 2], ALU.is_equal))
            link(dve.tensor_scalar(pen[:, 1, :], pen[:, 1, :], 1.0, -MASKED, ALU.subtract, ALU.mult))
            dve.memset(dummy2[:, 0:1], 0.0).then_inc(s_copied, 2)
            dve.memset(dummy2[:, 1:2], 0.0).then_inc(s_idx, 2)
            dve.wait_ge(s_tr, 2)
            psk = ps[:, 0:4, :].rearrange("p (n b) m -> p n (b m)", n=2)
            link(dve.tensor_copy(idxT[:, :, :].rearrange("p k b -> p (k b)"), psk[:, 0, 0:SLOTS]))
            link(dve.tensor_copy(lowT[:, :, :].rearrange("p k b -> p (k b)"), psk[:, 1, 0:SLOTS]))
            dve.memset(dummy2[:, 2:3], 0.0).then_inc(s_idx, 1)
            x.begin(dve, dummy2[:, 4:8])
            dve.wait_ge(x.s_w, x.LOADED)
            with dve.Fori(0, EARLY) as i:
                for n in range(BODY):
                    dve.wait_ge(s_stored[n % 2], i * (16 * NE) + (n // 2 * 16 + 16))
                    x.take(dve, y[:, n % 2, :, :], i, n).then_inc(x.s_y, 1)


def sum_messages(nc, d, m):
    with ExitStack() as ctx:
        def sb(name, shape, dt=F32):
            return ctx.enter_context(nc.sbuf_tensor(name, shape, dt))

        def sem(name):
            return ctx.enter_context(nc.semaphore(name))

        head, same, pen, lowT, G, iota, ident = m.head, m.same, m.pen, m.lowT, m.G, m.iota, m.ident
        work = sb("m_work", [P, 4, 4, SLOTS])
        s, dd, f, r = (work[:, n, :, :] for n in range(4))
        work_flat = work[:, :, :, :].rearrange("p a h s -> p (a h s)")
        hot = work_flat[:, 0:8 * SLOTS].rearrange("p (r c k n) -> p r c k n", r=2, c=4, k=KT)
        sumsT = work_flat[:, 8 * SLOTS:8 * SLOTS + 34 * P]
        rows_now = sb("m_rows_now", [P, 2, KT, 4, 32])
        rows = sb("m_rows", [P, P, ROW])
        crow = sb("m_crow", [P, ROW])
        cnt = sb("m_cnt", [P, P])
        A = sb("m_A", [P, P, 24])
        dummy2 = sb("m_dummy3", [P, 8])
        ps = ctx.enter_context(nc.psum_tensor("m_ps", [P, 8, 512], F32))
        s_in, s_v, s_sd, s_back, s_bk, s_hot, s_used, s_pre, s_exp, s_w, s_done, s_out = (
            sem("n_s_" + n) for n in ("in", "v", "sd", "back", "bk", "hot", "used", "pre", "exp", "w", "done", "out"))
        s_now, s_sumsT, s_sums = sem("n_s_now"), sem("n_s_sumsT"), sem("n_s_sums")
        block = ctx.enter_context(nc.Block())

        @block.sync
        def _(sp):
            sp.dma_start(cnt[:, :], d.cnt).then_inc(s_in, 16)
            sp.dma_start(rows[:, :, :], d.tab.rearrange("b n c -> (b n) c").rearrange("(t p) c -> p t c", p=P)).then_inc(s_in, 16)
            sp.dma_start(crow[:, :], d.tab.rearrange("b n c -> (b n) c")[LAST:LAST + 1, :].to_broadcast([P, ROW])).then_inc(s_in, 16)
            sp.wait_ge(s_done, 1)
            sp.dma_start(d.sums, A[:, :, 0:20]).then_inc(s_out, 16)
            sp.wait_ge(s_out, 16)

        @block.scalar
        def _(act):
            act.wait_ge(s_pre, 1)
            act.activation(s[:, :, :], s[:, :, :], ACT.Exp).then_inc(s_exp, 1)
            act.wait_ge(s_w, 2)
            by_bucket = G[:, :, :].rearrange("p (k b) c -> p k b c", k=KT)
            with act.Fori(0, P // 8) as i:
                for b in range(2):
                    act.wait_ge(s_used, i * 2 + b + 1)
                    act.activation(sumsT[:, bass.ds(i * (2 * P) + b * P, P)], ps[:, b, 0:P], ACT.Copy).then_inc(s_sumsT, 1)
                    act.activation(rows_now[:, b, :, :, 0:24], by_bucket[:, :, bass.ds(i * 8 + b * 4, 4), :], ACT.Copy).then_inc(s_now, 1)
            act.wait_ge(s_used, P // 4 + 2)
            for b in range(2):
                act.activation(sumsT[:, (32 + b) * P:(33 + b) * P], ps[:, b, 0:P], ACT.Copy).then_inc(s_sumsT, 1)
            act.wait_ge(s_pre, 2)
            act.activation(A[:, :, 20:24], A[:, :, 20:24], ACT.Exp).then_inc(s_exp, 1)
            act.activation(rows[:, :, 20:24], rows[:, :, 20:24], ACT.Exp).then_inc(s_exp, 1)

        @block.tensor
        def _(pe):
            for k in range(KT):
                for n in range(2):
                    if 2 * k + n >= 8:
                        pe.wait_ge(s_sd, 2 * k + n - 7)
                    for hd in range(4):
                        last = pe.transpose(ps[:, (2 * k + n) % 8, hd * P:(hd + 1) * P], G[:, k * P:(k + 1) * P, 16 + 4 * n + hd], ident[:, :])
                    last.then_inc(s_back, 1)
            pe.wait_ge(s_w, 1)
            for k in range(KT):
                for n, t in enumerate((s, f)):
                    if 2 * k + n >= 8:
                        pe.wait_ge(s_bk, 2 * k + n - 7)
                    for hd in range(4):
                        last = pe.transpose(ps[:, (2 * k + n) % 8, hd * P:(hd + 1) * P], t[:, hd, k * P:(k + 1) * P], ident[:, :])
                    last.then_inc(s_back, 1)
            pe.wait_ge(s_w, 2)
            with pe.Fori(0, P // 8) as i:
                for b in range(2):
                    pe.wait_ge(s_hot, i * 8 + (4 * b + 4))
                    pe.wait_ge(s_sumsT, i * 2 + b + 1)
                    pe.wait_ge(s_now, i * 2 + b + 1)
                    for k in range(KT):
                        for c in range(4):
                            last = pe.matmul(ps[32 * c:32 * c + 32, b, 0:P], rows_now[:, b, k, c, :], hot[:, b, c, k, :],
                                             start=k == 0, stop=k == KT - 1, tile_position=(0, 32 * c))
                    last.then_inc(s_used, 1)
            pe.wait_ge(s_sumsT, 34)
            for b in range(8):
                for c in range(4):
                    g = 4 * b + c
                    last = pe.transpose(ps[:, b, c * P:(c + 1) * P], sumsT[:, (g + 2) * P:(g + 3) * P], ident[:, :])
                last.then_inc(s_sums, 1)

        @block.vector
        def _(dve):
            link = Chain(dve, s_v)
            link(dve.memset(rows_now[:, :, :, :, :], 0.0))
            dve.memset(dummy2[:, 6:7], 0.0).then_inc(s_used, 2)
            dve.wait_ge(s_in, 48)
            for k in range(KT):
                for n, t in enumerate((s, dd)):
                    dve.wait_ge(s_back, 2 * k + n + 1)
                    dve.tensor_copy(t[:, :, k * P:(k + 1) * P], ps[:, (2 * k + n) % 8, :].rearrange("p (h b) -> p h b", h=4)).then_inc(s_sd, 1)
            dve.wait_ge(s_sd, 2 * KT)
            link(dve.tensor_tensor(dd[:, :, :], dd[:, :, :], head[:, None, :].to_broadcast([P, 4, SLOTS]), ALU.mult))
            for hd in range(4):
                dve.tensor_tensor_scan(r[:, hd, :], same[:, :], dd[:, hd, :], 0.0, ALU.mult, ALU.add)
                last = dve.tensor_tensor_scan(f[:, hd, :], pen[:, 0, :], s[:, hd, :], MASKED, ALU.add, ALU.max)
            link(last)
            for hd in range(4):
                last = dve.tensor_tensor_scan(dd[:, hd, ::-1], pen[:, 1, ::-1], f[:, hd, ::-1], MASKED, ALU.add, ALU.max)
            link(last)
            link(dve.tensor_copy(f[:, :, :], dd[:, :, :]))
            link(dve.tensor_tensor(s[:, :, :], s[:, :, :], r[:, :, :], ALU.add))
            link(dve.tensor_tensor(r[:, :, :], r[:, :, :], f[:, :, :], ALU.add))
            link(dve.scalar_tensor_tensor(out=s[:, :, :], in0=s[:, :, :], scalar=LEAK, in1=s[:, :, :], op0=ALU.mult, op1=ALU.max))
            link(dve.scalar_tensor_tensor(out=r[:, :, :], in0=r[:, :, :], scalar=LEAK, in1=r[:, :, :], op0=ALU.mult, op1=ALU.max))
            dve.tensor_tensor(s[:, :, :], s[:, :, :], r[:, :, :], ALU.subtract).then_inc(s_pre, 1)
            link(dve.tensor_tensor(f[:, :, :], f[:, :, :], head[:, None, :].to_broadcast([P, 4, SLOTS]), ALU.mult))
            dve.wait_ge(s_exp, 1)
            dve.memset(dummy2[:, 3:4], 0.0).then_inc(s_w, 1)
            for k in range(KT):
                for n in range(2):
                    dve.wait_ge(s_back, 2 * KT + 2 * k + n + 1)
                    dve.tensor_copy(G[:, k * P:(k + 1) * P, 16 + 4 * n:20 + 4 * n],
                                    ps[:, (2 * k + n) % 8, :].rearrange("p (h b) -> p b h", h=4)).then_inc(s_bk, 1)
            dve.wait_ge(s_bk, 2 * KT)
            dve.tensor_tensor(G[:, :, 0:16].rearrange("p t (h e) -> p t h e", h=4), G[:, :, 0:16].rearrange("p t (h e) -> p t h e", h=4),
                              G[:, :, 16:20][:, :, :, None].to_broadcast([P, SLOTS, 4, 4]), ALU.mult).then_inc(s_w, 1)
            with dve.Fori(0, P // 8) as i:
                for b in range(2):
                    dve.wait_ge(s_used, i * 2 + b + 1)
                    for c in range(4):
                        dve.tensor_tensor(hot[:, b, c, :, :], iota[:, None, :].to_broadcast([P, KT, P]),
                                          lowT[:, :, bass.ds(i * 8 + (b * 4 + c), 1)].to_broadcast([P, KT, P]), ALU.is_equal).then_inc(s_hot, 1)
            dve.wait_ge(s_sums, 8)
            for b in range(8):
                last = dve.tensor_copy(A[:, 16 * b:16 * b + 16, :], ps[:, b, :].rearrange("p (c n) -> p c n", n=32)[:, :, 0:24])
            link(last)
            def wide(x):
                return x.to_broadcast([P, P, 4])
            top, l, ad = A[:, :, 20:24], A[:, :, 16:20], rows[:, :, 20:24]
            en, ec = rows[:, :, 0:4], rows[:, :, 4:8]
            cs = crow[:, None, 16:20].to_broadcast([P, P, 4])
            link(dve.tensor_scalar(rows[:, :, 8:9], cnt[:, :, None], 0.0, MASKED, ALU.is_le, ALU.mult))
            link(dve.tensor_tensor(en, cs, wide(rows[:, :, 8:9]), ALU.add))
            link(dve.tensor_tensor(en, en, top, ALU.max))
            link(dve.tensor_tensor(en, en, ad, ALU.add))
            link(dve.tensor_tensor(top, top, ad, ALU.add))
            link(dve.tensor_tensor(ec, cs, ad, ALU.add))
            for x in (en, top, ec):
                link(dve.scalar_tensor_tensor(out=x, in0=x, scalar=LEAK, in1=x, op0=ALU.mult, op1=ALU.max))
            link(dve.tensor_tensor(top, top, en, ALU.subtract))
            link(dve.tensor_tensor(ec, ec, en, ALU.subtract))
            link(dve.tensor_scalar(ad, ec, 0.0, None, ALU.min))
            dve.memset(dummy2[:, 4:5], 0.0).then_inc(s_pre, 1)
            dve.wait_ge(s_exp, 3)
            link(dve.tensor_tensor(ad, ad, wide(cnt[:, :, None]), ALU.mult))
            link(dve.tensor_tensor(l, l, top, ALU.mult))
            link(dve.tensor_tensor(l, l, ad, ALU.add))
            for hd in range(4):
                acc = A[:, :, 4 * hd:4 * hd + 4]
                link(dve.tensor_tensor(acc, acc, wide(top[:, :, hd:hd + 1]), ALU.mult))
                link(dve.tensor_tensor(en, crow[:, None, 4 * hd:4 * hd + 4].to_broadcast([P, P, 4]), wide(ad[:, :, hd:hd + 1]), ALU.mult))
                link(dve.tensor_tensor(acc, acc, en, ALU.add))
            dve.memset(dummy2[:, 5:6], 0.0).then_inc(s_done, 1)


DEAD = 20000.0


def general_phase(nc, d, edges=E):
    with ExitStack() as ctx:
        def sb(name, shape, dt=F32):
            return ctx.enter_context(nc.sbuf_tensor(name, shape, dt))

        def sem(name):
            return ctx.enter_context(nc.semaphore(name))

        over, flag = sb("g_over", [P, 1]), sb("g_flag", [P, 1], I32)
        ident, low = sb("g_ident", [P, P]), sb("g_low", [P, P])
        cnt = sb("g_cnt", [P, P])
        crow = sb("g_crow", [P, ROW])
        rows = sb("g_rows", [P, P, ROW])
        state = sb("g_state", [P, P, ROW])
        e3 = sb("g_e3", [P, P, 12])
        esrc, edst = sb("g_esrc", [P, 1], I32), sb("g_edst", [P, 1], I32)
        keep, dst = sb("g_keep", [P, 1]), sb("g_dst", [P, 1])
        si, di, oi = sb("g_si", [P, 1], I32), sb("g_di", [P, 1], I32), sb("g_oi", [P, 1], I32)
        dup = sb("g_dup", [P, 1])
        g, old, new = sb("g_g", [P, ROW]), sb("g_old", [P, ROW]), sb("g_new", [P, ROW])
        eq, pen, t1 = sb("g_eq", [P, P]), sb("g_pen", [P, P]), sb("g_t1", [P, P])
        sm = sb("g_sm", [P, 4, P])
        x = sb("g_x", [P, 12])
        y = sb("g_y", [P, 8])
        v = sb("g_v", [P, 20])
        dummy = sb("g_dummy", [P, 8])
        ps = ctx.enter_context(nc.psum_tensor("g_ps", [P, 3, 512], F32))
        s_in, s_setup, s_flag, s_v, s_pre, s_exp, s_init, s_stored = (
            sem("g_s_" + n) for n in ("in", "setup", "flag", "v", "pre", "exp", "init", "stored"))
        s_e, s_next, s_idx, s_g, s_row, s_vv, s_sum, s_new, s_xx, s_yy, s_pool = (
            sem("g_s_" + n) for n in ("e", "next", "idx", "g", "row", "vv", "sum", "new", "xx", "yy", "pool"))
        s_back, s_sums, s_out = sem("g_s_back"), sem("g_s_sums"), sem("g_s_out")
        block = ctx.enter_context(nc.Block())
        TILES = edges // P
        table = d.tab.rearrange("b n c -> (b n) c")

        def by_tile(t):
            return t.rearrange("(t p) c -> p t c", p=P)

        def column(n, i):
            return d.edges[n, bass.ds(i * P, P)].rearrange("(p a) -> p a", a=1)

        @block.sync
        def _(sp):
            sp.dma_start(over[:, :], d.over).then_inc(s_in, 16)
            sp.wait_ge(s_flag, 1)
            overflow = sp.value_load(flag[0:1, 0:1], min_val=0, max_val=1)
            with sp.If(overflow > 0):
                sp.dma_start(cnt[:, :], d.cnt).then_inc(s_in, 16)
                sp.dma_start(rows[:, :, :], by_tile(table)).then_inc(s_in, 16)
                sp.dma_start(crow[:, :], table[LAST:LAST + 1, :].to_broadcast([P, ROW])).then_inc(s_in, 16)
                sp.wait_ge(s_init, 1)
                sp.dma_start(by_tile(d.state), state[:, :, :]).then_inc(s_stored, 16)
                with sp.Fori(0, TILES) as i:
                    sp.wait_ge(s_idx, i * 1 + 1)
                    sp.dma_start(esrc[:, :], column(0, i)).then_inc(s_e, 16)
                    sp.dma_start(edst[:, :], column(1, i)).then_inc(s_e, 16)
                sp.wait_ge(s_new, 16 * TILES + 16)
                sp.dma_start(state[:, :, :], by_tile(d.state)).then_inc(s_back, 16)
                sp.wait_ge(s_back, 16)
                sp.dma_start(d.sums, state[:, :, 0:20]).then_inc(s_out, 16)
                sp.wait_ge(s_out, 16)

        @block.gpsimd
        def _(pool):
            def setup(n, ins):
                ins.then_inc(s_setup, 1)
                pool.wait_ge(s_setup, n)
            pool.wait_ge(s_in, 16)
            pool.partition_all_reduce(flag[:, :], over[:, :], P, bass.bass_isa.ReduceOp.max).then_inc(s_flag, 1)
            pool.wait_ge(s_flag, 1)
            overflow = pool.value_load(flag[0:1, 0:1], min_val=0, max_val=1)
            with pool.If(overflow > 0):
                setup(1, pool.memset(ident[:, :], 0.0))
                setup(2, pool.affine_select(out=ident[:, :], in_=ident[:, :], compare_op=ALU.not_equal, fill=1.0, base=0,
                                            pattern=[[-1, P]], channel_multiplier=1))
                setup(3, pool.memset(low[:, :], 1.0))
                setup(4, pool.affine_select(out=low[:, :], in_=low[:, :], compare_op=ALU.is_gt, fill=0.0, base=0,
                                            pattern=[[-1, P]], channel_multiplier=1))
                setup(5, pool.memset(dummy[:, :], 0.0))
                pool.wait_ge(s_stored, 16)
                pool.dma_start(d.scrap[:, 0:8], ident[:, 0:8]).then_inc(s_new, 16)
                with pool.Fori(0, TILES) as i:
                    pool.wait_ge(s_idx, i * 1 + 2)
                    pool.tensor_tensor(dummy[:, 1:2], dummy[:, 0:1], dummy[:, 0:1], ALU.add).then_inc(s_pool, 1)
                    pool.indirect_dma_start(g[:, :], None, table, bass.IndirectOffsetOnAxis(ap=si[:, 0:1], axis=0),
                                            bounds_check=LAST, oob_is_err=False).then_inc(s_g, 16)
                    pool.wait_ge(s_new, i * 16 + 16)
                    pool.tensor_tensor(dummy[:, 2:3], dummy[:, 0:1], dummy[:, 0:1], ALU.add).then_inc(s_pool, 1)
                    pool.indirect_dma_start(old[:, :], None, d.state, bass.IndirectOffsetOnAxis(ap=di[:, 0:1], axis=0),
                                            bounds_check=LAST, oob_is_err=False).then_inc(s_g, 16)
                    pool.wait_ge(s_next, i * 1 + 1)
                    pool.tensor_tensor(dummy[:, 3:4], dummy[:, 0:1], dummy[:, 0:1], ALU.add).then_inc(s_pool, 1)
                    pool.indirect_dma_start(d.state, bass.IndirectOffsetOnAxis(ap=oi[:, 0:1], axis=0), new[:, :], None,
                                            bounds_check=LAST, oob_is_err=False).then_inc(s_new, 16)
                    pool.wait_ge(s_pool, i * 3 + 3)

        @block.scalar
        def _(act):
            act.wait_ge(s_flag, 1)
            overflow = act.value_load(flag[0:1, 0:1], min_val=0, max_val=1)
            with act.If(overflow > 0):
                act.wait_ge(s_pre, 1)
                act.activation(e3[:, :, 0:8], e3[:, :, 0:8], ACT.Exp).then_inc(s_exp, 1)
                with act.Fori(0, TILES) as i:
                    act.wait_ge(s_xx, i * 1 + 1)
                    act.activation(y[:, :], y[:, :], ACT.Exp).then_inc(s_yy, 1)

        @block.tensor
        def _(pe):
            pe.wait_ge(s_flag, 1)
            overflow = pe.value_load(flag[0:1, 0:1], min_val=0, max_val=1)
            with pe.If(overflow > 0):
                pe.wait_ge(s_setup, 5)
                with pe.Fori(0, TILES) as i:
                    pe.wait_ge(s_idx, i * 1 + 2)
                    pe.transpose(ps[:, 0, 0:P], dst[:, 0:1].to_broadcast([P, P]), ident[:, :]).then_inc(s_row, 1)
                    pe.wait_ge(s_g, i * 32 + 32)
                    for hd in range(4):
                        last = pe.transpose(ps[:, 1, hd * P:(hd + 1) * P], g[:, 16 + hd:17 + hd].to_broadcast([P, P]), ident[:, :])
                    last.then_inc(s_row, 1)
                    pe.wait_ge(s_vv, i * 1 + 1)
                    pe.matmul(ps[:, 2, 0:20], eq[:, :], v[:, :], start=True, stop=True).then_inc(s_sum, 1)

        @block.vector
        def _(dve):
            dve.wait_ge(s_flag, 1)
            overflow = dve.value_load(flag[0:1, 0:1], min_val=0, max_val=1)
            with dve.If(overflow > 0):
                link = Chain(dve, s_v)
                dve.wait_ge(s_setup, 5)
                dve.wait_ge(s_in, 64)
                def wide(t):
                    return t.to_broadcast([P, P, 4])
                ec, es, en, pn = e3[:, :, 0:4], e3[:, :, 4:8], e3[:, :, 8:12], state[:, :, 0:1]
                a, ad = rows[:, :, 16:20], rows[:, :, 20:24]
                acc, l, m = state[:, :, 0:16], state[:, :, 16:20], state[:, :, 20:24]
                cs = crow[:, None, 16:20].to_broadcast([P, P, 4])
                link(dve.memset(state[:, :, :], 0.0))
                link(dve.tensor_copy(state[:, :, 24:28], ad))
                link(dve.tensor_scalar(pn, cnt[:, :, None], 0.0, MASKED, ALU.is_le, ALU.mult))
                link(dve.tensor_tensor(m, cs, wide(pn), ALU.add))
                link(dve.tensor_tensor(m, m, a, ALU.max))
                link(dve.tensor_tensor(en, m, ad, ALU.add))
                link(dve.tensor_tensor(es, a, ad, ALU.add))
                link(dve.tensor_tensor(ec, cs, ad, ALU.add))
                link(dve.scalar_tensor_tensor(out=e3[:, :, :], in0=e3[:, :, :], scalar=LEAK, in1=e3[:, :, :], op0=ALU.mult, op1=ALU.max))
                link(dve.tensor_tensor(es, es, en, ALU.subtract))
                link(dve.tensor_tensor(ec, ec, en, ALU.subtract))
                link(dve.tensor_scalar(ec, ec, 0.0, None, ALU.min))
                dve.memset(dummy[:, 6:7], 0.0).then_inc(s_pre, 1)
                dve.wait_ge(s_exp, 1)
                link(dve.tensor_tensor(ec, ec, wide(cnt[:, :, None]), ALU.mult))
                link(dve.tensor_tensor(l, ec, es, ALU.add))
                for hd in range(4):
                    part = state[:, :, 4 * hd:4 * hd + 4]
                    link(dve.tensor_tensor(part, rows[:, :, 4 * hd:4 * hd + 4], wide(es[:, :, hd:hd + 1]), ALU.mult))
                    link(dve.tensor_tensor(en, crow[:, None, 4 * hd:4 * hd + 4].to_broadcast([P, P, 4]), wide(ec[:, :, hd:hd + 1]), ALU.mult))
                    link(dve.tensor_tensor(part, part, en, ALU.add))
                dve.memset(dummy[:, 7:8], 0.0).then_inc(s_init, 1)
                dve.memset(keep[:, :], 0.0).then_inc(s_idx, 1)

                def tile(i):
                    dve.wait_ge(s_e, i * 32 + 32)
                    link(dve.tensor_scalar(keep[:, :], esrc[:, :], float(LAST), None, ALU.is_lt))
                    link(dve.scalar_tensor_tensor(out=keep[:, :], in0=edst[:, :], scalar=float(M), in1=keep[:, :], op0=ALU.is_lt, op1=ALU.mult))
                    link(dve.scalar_tensor_tensor(out=dst[:, :], in0=edst[:, :], scalar=-DEAD, in1=keep[:, :], op0=ALU.add, op1=ALU.mult))
                    link(dve.tensor_scalar(dst[:, :], dst[:, :], DEAD, None, ALU.add))
                    link(dve.tensor_scalar(si[:, :], esrc[:, :], float(LAST), None, ALU.min))
                    link(dve.tensor_scalar(di[:, :], dst[:, :], float(LAST), None, ALU.min))
                    dve.memset(y[:, 0:1], 0.0).then_inc(s_idx, 1)
                    dve.wait_ge(s_row, i * 2 + 1)
                    link(dve.tensor_scalar(eq[:, :], ps[:, 0, 0:P], dst[:, 0:1], None, ALU.is_equal))
                    link(dve.tensor_scalar(pen[:, :], eq[:, :], 1.0, -MASKED, ALU.subtract, ALU.mult))
                    link(dve.tensor_tensor(t1[:, :], eq[:, :], low[:, :], ALU.mult))
                    link(dve.tensor_reduce(dup[:, :], t1[:, :], AX_X, ALU.max))
                    link(dve.tensor_scalar(dup[:, :], dup[:, :], DEAD, dst[:, 0:1], ALU.mult, ALU.add))
                    link(dve.tensor_copy(oi[:, :], dup[:, :]))
                    dve.wait_ge(s_row, i * 2 + 2)
                    link(dve.tensor_tensor(sm[:, :, :], ps[:, 1, :].rearrange("p (h n) -> p h n", h=4), pen[:, None, :].to_broadcast([P, 4, P]), ALU.add))
                    link(dve.tensor_reduce(x[:, 0:4], sm[:, :, :], AX_X, ALU.max))
                    dve.wait_ge(s_g, i * 32 + 32)
                    link(dve.tensor_tensor(new[:, 20:24], x[:, 0:4], old[:, 20:24], ALU.max))
                    link(dve.tensor_tensor(x[:, 8:12], new[:, 20:24], old[:, 24:28], ALU.add))
                    link(dve.tensor_tensor(x[:, 4:8], old[:, 20:24], old[:, 24:28], ALU.add))
                    link(dve.tensor_tensor(x[:, 0:4], g[:, 16:20], old[:, 24:28], ALU.add))
                    link(dve.scalar_tensor_tensor(out=x[:, :], in0=x[:, :], scalar=LEAK, in1=x[:, :], op0=ALU.mult, op1=ALU.max))
                    dve.tensor_tensor(y[:, :].rearrange("p (a b) -> p a b", a=2), x[:, 0:8].rearrange("p (a b) -> p a b", a=2),
                                      x[:, None, 8:12].to_broadcast([P, 2, 4]), ALU.subtract).then_inc(s_xx, 1)
                    dve.wait_ge(s_yy, i * 1 + 1)
                    link(dve.tensor_scalar(y[:, 0:4], y[:, 0:4], 1.0, keep[:, 0:1], ALU.min, ALU.mult))
                    link(dve.tensor_copy(v[:, 16:20], y[:, 0:4]))
                    dve.tensor_tensor(v[:, 0:16].rearrange("p (h e) -> p h e", h=4), g[:, 0:16].rearrange("p (h e) -> p h e", h=4),
                                      y[:, 0:4, None].to_broadcast([P, 4, 4]), ALU.mult).then_inc(s_vv, 1)
                    link(dve.tensor_tensor(new[:, 0:16].rearrange("p (h e) -> p h e", h=4), old[:, 0:16].rearrange("p (h e) -> p h e", h=4),
                                           y[:, 4:8, None].to_broadcast([P, 4, 4]), ALU.mult))
                    link(dve.tensor_tensor(new[:, 16:20], old[:, 16:20], y[:, 4:8], ALU.mult))
                    link(dve.tensor_copy(new[:, 24:32], old[:, 24:32]))
                    dve.wait_ge(s_sum, i * 1 + 1)
                    link(dve.tensor_tensor(new[:, 0:20], new[:, 0:20], ps[:, 2, 0:20], ALU.add))
                    dve.memset(dummy[:, 6:7], 0.0).then_inc(s_next, 1)
                    dve.wait_ge(s_new, i * 16 + 32)
                link.loop(TILES, tile)


def expert_phase(nc, d):
    with ExitStack() as ctx:
        def sb(name, shape, dt=F32):
            return ctx.enter_context(nc.sbuf_tensor(name, shape, dt))

        def sem(name):
            return ctx.enter_context(nc.semaphore(name))

        x = Experts(nc, ctx, "late_")
        gpar = sb("x_gpar", [P, 3, GC])
        sums = sb("x_sums", [P, P, 20])
        agg = sb("x_agg", [P, P, GC])
        sq = sb("x_sq", [P, P, GC])
        st = sb("x_st", [P, P, 4])
        score = sb("x_score", [P, P, NE])
        sel = sb("x_sel", [P, P, NE])
        gate = sb("x_gate", [P, P, NE])
        tri = sb("x_tri", [P, NE, NE])
        eps = sb("x_eps", [P, 1])
        res = sb("x_res", [P, 2, CT, D])
        early = sb("x_early", [P, 2, NE, CT, D])
        res2 = sb("x_res2", [P, 2, CT, D])
        y = sb("x_y", [P, 2, CT, D])
        dummy2, zeros = sb("x_dummy2", [P, 8]), sb("x_zeros", [P, 8])
        s_w, s_setup, s_v, s_std, s_var = (sem("x_s_" + n) for n in ("w", "setup", "v", "std", "var"))
        s_added, s_fin, s_fin2 = sem("x_s_added"), sem("x_s_fin"), sem("x_s_fin2")
        s_res, s_out, s_early = ([sem(f"x_s_{n}0"), sem(f"x_s_{n}1")] for n in ("res", "out", "early"))
        block = ctx.enter_context(nc.Block())
        NW = 4

        def node_rows(t, b, half):
            return t[bass.ds(b, 1), half * CHUNK:(half + 1) * CHUNK, :].rearrange("a (t p) n -> p (a t) n", p=P)

        @block.sync
        def _(sp):
            sp.dma_start(sums[:, :, :], d.sums).then_inc(s_w, 16)
            for n, t in enumerate((d.b_gat, d.gamma, d.beta)):
                sp.dma_start(gpar[:, n, :], t.rearrange("(a n) -> a n", a=1).to_broadcast([P, GC])).then_inc(s_w, 16)
            x.load(sp, d)
            with sp.Fori(0, 16 - EARLY) as i:
                for h in range(2):
                    x.load_nodes(sp, d.xnT[EARLY:, :, :, :], i, h)
                    sp.wait_ge(s_out[h], i * 32 + 32)
                    sp.dma_start(res[:, h, :, :], node_rows(d.x1[EARLY:, :, :], i, h)).then_inc(s_res[h], 16)
                    sp.dma_start(res2[:, h, :, :], node_rows(d.x1, i, h)).then_inc(s_early[h], 16)
                    sp.dma_start(early[:, h, :, :, :].rearrange("p e t c -> p (e t c)"),
                                 d.early[bass.ds(i, 1), h, :, :, :, :].rearrange("a p e t c -> p (a e t c)")).then_inc(s_early[h], 16)
            for h in range(2):
                sp.wait_ge(s_out[h], 32 * (17 - EARLY))

        @block.gpsimd
        def _(pool):
            def setup(n, ins):
                ins.then_inc(s_setup, 1)
                pool.wait_ge(s_setup, n)
            setup(1, pool.memset(eps[:, :], LN_EPS))
            setup(2, pool.memset(tri[:, :, :], 1.0))
            setup(3, pool.affine_select(out=tri[:, :, :], in_=tri[:, :, :], compare_op=ALU.is_gt, fill=0.0, base=0,
                                        pattern=[[1, NE], [-1, NE]], channel_multiplier=0))
            setup(4, pool.memset(zeros[:, :], 0.0))
            for h in range(2):
                pool.dma_start(d.scrap[:, h * 16:h * 16 + 8], zeros[:, :]).then_inc(s_out[h], 16)
                pool.dma_start(d.scrap[:, h * 16 + 8:h * 16 + 16], zeros[:, :]).then_inc(s_out[h], 16)
            with pool.Fori(0, 16 - EARLY) as i:
                for h in range(2):
                    pool.wait_ge(s_fin, i * 2 + h + 1)
                    pool.dma_start(node_rows(d.out[EARLY:, :, :], i, h), res[:, h, :, :]).then_inc(s_out[h], 16)
                    pool.wait_ge(s_fin2, i * 2 + h + 1)
                    pool.dma_start(node_rows(d.out, i, h), res2[:, h, :, :]).then_inc(s_out[h], 16)

        @block.scalar
        def _(act):
            act.wait_ge(x.s_w, x.LOADED)
            x.activate(act, 0, 0)
            act.wait_ge(s_setup, 3)
            act.wait_ge(s_var, 1)
            act.activation(st[:, :, 2], st[:, :, 1], ACT.Sqrt, bias=eps[:, 0:1]).then_inc(s_std, 1)
            x.activate(act, 0, 1)
            act.wait_ge(s_var, 2)
            act.activation(gate[:, :, :], gate[:, :, :], ACT.Exp).then_inc(s_std, 1)
            for n in range(2, BODY):
                x.activate(act, 0, n)
            with act.Fori(1, 16 - EARLY) as i:
                for n in range(BODY):
                    x.activate(act, i, n)

        @block.tensor
        def _(pe):
            pe.wait_ge(x.s_w, x.LOADED)
            with pe.Fori(0, 16 - EARLY) as i:
                x.graph(pe, i)

        @block.vector
        def _(dve):
            link = Chain(dve, s_v)
            dve.wait_ge(s_setup, 3)
            x.begin(dve, dummy2[:, 4:8])
            dve.wait_ge(s_w, 16 * NW)

            def wide(x, n):
                return x.to_broadcast([P, P, n])
            link(dve.tensor_scalar(st[:, :, :], sums[:, :, 16:20], 1e-16, None, ALU.add))
            link(dve.reciprocal(st[:, :, :], st[:, :, :]))
            link(dve.tensor_tensor(agg[:, :, :].rearrange("p t (h e) -> p t h e", h=4), sums[:, :, 0:16].rearrange("p t (h e) -> p t h e", h=4),
                                   st[:, :, :, None].to_broadcast([P, P, 4, 4]), ALU.mult))
            link(dve.tensor_tensor(agg[:, :, :], agg[:, :, :], gpar[:, None, 0, :].to_broadcast([P, P, GC]), ALU.add))
            link(dve.tensor_reduce(st[:, :, 0], agg[:, :, :], AX_X, ALU.add))
            link(dve.tensor_scalar(st[:, :, 0], st[:, :, 0], 1.0 / GC, None, ALU.mult))
            link(dve.tensor_tensor(agg[:, :, :], agg[:, :, :], wide(st[:, :, 0:1], GC), ALU.subtract))
            link(dve.tensor_tensor(sq[:, :, :], agg[:, :, :], agg[:, :, :], ALU.mult))
            link(dve.tensor_reduce(st[:, :, 1], sq[:, :, :], AX_X, ALU.add))
            dve.tensor_scalar(st[:, :, 1], st[:, :, 1], 1.0 / GC, None, ALU.mult).then_inc(s_var, 1)
            dve.wait_ge(s_std, 1)
            link(dve.reciprocal(st[:, :, 2], st[:, :, 2]))
            link(dve.tensor_tensor(agg[:, :, :], agg[:, :, :], wide(st[:, :, 2:3], GC), ALU.mult))
            link(dve.tensor_tensor(agg[:, :, :], agg[:, :, :], gpar[:, None, 1, :].to_broadcast([P, P, GC]), ALU.mult))
            link(dve.tensor_tensor(agg[:, :, :], agg[:, :, :], gpar[:, None, 2, :].to_broadcast([P, P, GC]), ALU.add))
            link(dve.tensor_reduce(score[:, :, :], agg[:, :, :].rearrange("p t (h e) -> p t e h", h=4), AX_X, ALU.add))
            link(dve.tensor_scalar(score[:, :, :], score[:, :, :], 0.25, None, ALU.mult))
            mine = score[:, :, :, None].to_broadcast([P, P, NE, NE])
            theirs = score[:, :, None, :].to_broadcast([P, P, NE, NE])
            pairs, ties = (t[:, :, :].rearrange("p t (a b) -> p t a b", a=NE) for t in (agg, sq))
            link(dve.tensor_tensor(pairs, theirs, mine, ALU.is_gt))
            link(dve.tensor_tensor(ties, theirs, mine, ALU.is_equal))
            link(dve.tensor_tensor(ties, ties, tri[:, None, :, :].to_broadcast([P, P, NE, NE]), ALU.mult))
            link(dve.tensor_tensor(pairs, pairs, ties, ALU.add))
            link(dve.tensor_reduce(sel[:, :, :], pairs, AX_X, ALU.add))
            link(dve.tensor_scalar(sel[:, :, :], sel[:, :, :], 1.5, None, ALU.is_lt))
            link(dve.tensor_reduce(st[:, :, 0], score[:, :, :], AX_X, ALU.max))
            dve.tensor_tensor(gate[:, :, :], score[:, :, :], wide(st[:, :, 0:1], NE), ALU.subtract).then_inc(s_var, 1)
            dve.wait_ge(s_std, 2)
            link(dve.tensor_tensor(gate[:, :, :], gate[:, :, :], sel[:, :, :], ALU.mult))
            link(dve.tensor_reduce(st[:, :, 0], gate[:, :, :], AX_X, ALU.add))
            link(dve.reciprocal(st[:, :, 0], st[:, :, 0]))
            link(dve.tensor_tensor(gate[:, :, :], gate[:, :, :], wide(st[:, :, 0:1], NE), ALU.mult))
            dve.wait_ge(x.s_w, x.LOADED)

            def combine(i):
                for n in range(BODY):
                    h, e = n // NE, n % NE
                    if e == 0:
                        dve.wait_ge(s_res[h], i * 16 + 16)
                    ins = x.take(dve, y[:, n % 2, :, :], i, n)
                    ins.then_inc(x.s_y, 1)
                    dve.wait_ge(x.s_y, i * BODY + n + 3)
                    for t in range(CT):
                        last = dve.scalar_tensor_tensor(out=res[:, h, t, :], in0=y[:, n % 2, t, :],
                                                        scalar=gate[:, bass.ds(i * 8 + (EARLY * 8 + h * CT + t), 1), e],
                                                        in1=res[:, h, t, :], op0=ALU.mult, op1=ALU.add)
                    if e == NE - 1:
                        last.then_inc(s_fin, 1)
                    else:
                        link(last)
                    if e == 0:
                        dve.wait_ge(s_early[h], i * 32 + 32)
                    for t in range(CT):
                        last = dve.scalar_tensor_tensor(out=res2[:, h, t, :], in0=early[:, h, e, t, :],
                                                        scalar=gate[:, bass.ds(i * 8 + (h * CT + t), 1), e],
                                                        in1=res2[:, h, t, :], op0=ALU.mult, op1=ALU.add)
                    if e == NE - 1:
                        last.then_inc(s_fin2, 1)
                    else:
                        link(last)
            link.loop(16 - EARLY, combine)


def build(nc, a, out):
    def scratch(name, shape, dt=F32):
        return nc.dram_tensor(name, shape, dt, kind="Internal").ap()

    d = Arrays()
    d.x, d.adj, d.out, d.edges = a["x"], a["adj"], out, a["L0_ffn_edge_index"]
    d.wqT, d.wkT, d.wvT, d.woT = a["WqT"], a["WkT"], a["WvT"], a["WoT"]
    d.bq, d.bk, d.bv, d.bo = a["L0_gnn_bq"], a["L0_gnn_bk"], a["L0_gnn_bv"], a["L0_gnn_bo"]
    d.wgat, d.att_src, d.att_dst, d.b_gat = a["L0_ffn_W_gat"], a["L0_ffn_att_src"], a["L0_ffn_att_dst"], a["L0_ffn_b_gat"]
    d.gamma, d.beta = a["L0_ffn_ln_gamma"], a["L0_ffn_ln_beta"]
    d.w1, d.b1, d.w2, d.b2 = a["L0_ffn_W1"], a["L0_ffn_b1"], a["L0_ffn_W2"], a["L0_ffn_b2"]
    d.x1 = scratch("x1_scratch", (16, N, D))
    d.xnT = scratch("xnT_scratch", (16, P, 2, N))
    d.tab = scratch("tab_scratch", (16, N, ROW))
    d.cells = scratch("cells_scratch", (P * CELLS, 1))
    d.slots = scratch("slots_scratch", (P, SLOTS))
    d.cnt = scratch("cnt_scratch", (P, P))
    d.over = scratch("over_scratch", (P, 1))
    d.sums = scratch("sums_scratch", (P, P, 20))
    d.state = scratch("state_scratch", (M, ROW))
    d.early = scratch("early_scratch", (EARLY, 2, P, NE, CT, D))
    d.scrap = scratch("scrap_scratch", (P, 32))
    attention_phase(nc, d, 16)
    message_phase(nc, d)
    general_phase(nc, d)
    expert_phase(nc, d)


_INS = ["x", "adj", "L0_gnn_bq", "L0_gnn_bk", "L0_gnn_bv", "L0_gnn_bo", "L0_ffn_W_gat", "L0_ffn_att_src", "L0_ffn_att_dst",
        "L0_ffn_b_gat", "L0_ffn_ln_gamma", "L0_ffn_ln_beta", "L0_ffn_W1", "L0_ffn_b1", "L0_ffn_W2", "L0_ffn_b2", "L0_ffn_edge_index"]
_TRANSPOSED = {"WqT": "L0_gnn_Wq", "WkT": "L0_gnn_Wk", "WvT": "L0_gnn_Wv", "WoT": "L0_gnn_Wo"}


def kernel(**inputs):
    import numpy as _np
    import concourse.bacc as _bacc
    from concourse import mybir as _mybir
    from concourse.bass_utils import run_bass_kernel_spmd as _run

    nc = _bacc.Bacc("TRN2", target_bir_lowering=False, num_devices=1)
    arrays, args = {}, {}
    laid = {n: _np.ascontiguousarray(inputs[n]) for n in _INS}
    laid.update({n: _np.ascontiguousarray(_np.asarray(inputs[s]).T) for n, s in _TRANSPOSED.items()})
    for name, a in laid.items():
        arrays[f"in_{name}"] = a
        args[name] = nc.dram_tensor(f"in_{name}", a.shape, _mybir.dt.from_np(a.dtype), kind="ExternalInput").ap()
    out = nc.dram_tensor("out_0", (16, N, D), _mybir.dt.float32, kind="ExternalOutput").ap()
    build(nc, args, out)
    r = _run(nc, [arrays], core_ids=[0])
    return r.results[0]["out_0"]
```
